# Optimizing a Trainium2 kernel written in Bass

```python
import numpy as np
import jax
import jax.numpy as jnp

def _softmax(x, axis=-1):
    return jax.nn.softmax(x, axis=axis)

def _gelu(x):
    return jax.nn.gelu(x, approximate=True)

def _silu(x):
    return jax.nn.silu(x)

def _sigmoid(x):
    return jax.nn.sigmoid(x)

def _layernorm(x, axis=-1, eps=1e-05):
    m = jnp.mean(x, axis=axis, keepdims=True)
    v = jnp.var(x, axis=axis, keepdims=True)
    return (x - m) / jnp.sqrt(v + eps)

def _scatter_add(tgt, idx, src, axis=0):
    return tgt.at[idx].add(src)

def _segment_sum(src, seg, n):
    return jax.ops.segment_sum(src, seg, n)
kernel_name = 'mk_xattn_ffn_d2_seqx_r2_e0c076'

def setup_inputs(seed: int=0):
    np.random.seed(seed)
    _w = jnp.asarray

    def _rec_inputs():
        import jax
        import jax.numpy as jnp
        _rk = jax.random.key(seed)
        x = 7.22e-05 + 1 * jax.random.normal(jax.random.fold_in(_rk, 1), (8, 512, 512), jnp.float32)
        _lenS = 512 - jax.random.randint(jax.random.fold_in(_rk, 7), (8,), 0, max(1, 512 // 4) + 1, jnp.int32)
        _lenS2 = 77 - jax.random.randint(jax.random.fold_in(_rk, 8), (8,), 0, max(1, 77 // 4) + 1, jnp.int32)
        _ctx_1024P = jax.random.normal(jax.random.fold_in(_rk, 11), (8, 16, 512), jnp.float32)
        _ctx_1024c = jax.random.dirichlet(jax.random.fold_in(_rk, 511), 0.3 * jnp.ones((16,), jnp.float32), (8, 77))
        _ctx_1024t = jnp.einsum('bsk,bkd->bsd', _ctx_1024c, _ctx_1024P)
        _ctx_1024t = _ctx_1024t * jax.lax.rsqrt(jnp.mean(jnp.square(_ctx_1024t)) + 1e-12) * 0.953939
        ctx_1024 = 4.13588e-05 + 0.999923 * (_ctx_1024t + 0.3 * jax.random.normal(jax.random.fold_in(_rk, 611), (8, 77, 512), jnp.float32))
        _validS = jnp.arange(512)[None, :] < _lenS[:, None]
        _validS2 = jnp.arange(77)[None, :] < _lenS2[:, None]
        _causal = jnp.tril(jnp.ones((512, 512), dtype=bool))
        mask_BxS2_ik0 = jnp.where(jnp.broadcast_to(_validS2[:, :], (8, 77)), 0, 1).astype(jnp.int32)
        return (x, ctx_1024, mask_BxS2_ik0)
    x, ctx_1024, mask_BxS2_ik0 = _rec_inputs()

    def _L0_xattn_setup():
        import jax, jax.numpy as jnp
        import numpy as np
        B, LQ, LK, D = (4, 1024, 1024, 512)
        H = 16
        HD = D // H

        def _split_heads(x):
            b, l, _ = x.shape
            return x.reshape(b, l, H, HD).transpose(0, 2, 1, 3)
        key = jax.random.key(seed)
        ks = jax.random.split(key, 10)
        s = 0.02
        return {'hidden_states': jax.random.normal(ks[0], (B, LQ, D), jnp.float32), 'context': jax.random.normal(ks[1], (B, LK, D), jnp.float32), 'attention_mask': jax.random.randint(ks[2], (B, LK), 0, 2, jnp.int32), 'q_w': jax.random.normal(ks[3], (D, D), jnp.float32) * s, 'q_b': jnp.zeros((D,), jnp.float32), 'k_w': jax.random.normal(ks[4], (D, D), jnp.float32) * s, 'k_b': jnp.zeros((D,), jnp.float32), 'v_w': jax.random.normal(ks[5], (D, D), jnp.float32) * s, 'v_b': jnp.zeros((D,), jnp.float32)}
    _L0_xattn_all = _L0_xattn_setup()
    _L0_xattn_in = {k: v for k, v in _L0_xattn_all.items() if k in ('q_w', 'q_b', 'k_w', 'k_b', 'v_w', 'v_b')}
    del _L0_xattn_all

    def _L0_ffn_setup():
        import jax, jax.numpy as jnp
        import numpy as np
        IN_F = 512
        OUT_F = 512
        B, S = (8, 2048)

        def _pack_ternary(tern):
            enc = (tern + 1.0).astype(jnp.int32).reshape(-1)
            return (enc[0::4] | enc[1::4] << 2 | enc[2::4] << 4 | enc[3::4] << 6).astype(jnp.int32)
        key = jax.random.key(seed)
        kx, kw = jax.random.split(key)
        x = jax.random.normal(kx, (B, S, IN_F), dtype=jnp.float32)
        w = jax.random.normal(kw, (OUT_F, IN_F), dtype=jnp.float32) * 0.02
        scale = jnp.maximum(jnp.mean(jnp.abs(w)), 1e-05)
        wn = w / scale
        tern = jnp.sign(wn) * (jnp.abs(wn) > 0.5).astype(jnp.float32)
        packed = _pack_ternary(tern)
        bias = jnp.zeros((OUT_F,), dtype=jnp.float32)
        return {'x': x, 'packed_weight': packed, 'weight_scale': scale.reshape(1), 'bias': bias}
    _L0_ffn_all = _L0_ffn_setup()
    _L0_ffn_in = {k: v for k, v in _L0_ffn_all.items() if k in ('packed_weight', 'weight_scale', 'bias')}
    del _L0_ffn_all

    def _L1_xattn_setup():
        import jax, jax.numpy as jnp
        import numpy as np
        B, S, D = (2, 1024, 512)
        H, HD = (16, 64)
        key = jax.random.key(seed)
        ks = jax.random.split(key, 10)
        scale = 1.0 / np.sqrt(D)
        inputs_q = jax.random.normal(ks[0], (B, S, D), dtype=jnp.float32)
        inputs_kv = inputs_q
        Wq = jax.random.normal(ks[1], (D, H, HD), dtype=jnp.float32) * scale
        Wk = jax.random.normal(ks[2], (D, H, HD), dtype=jnp.float32) * scale
        Wv = jax.random.normal(ks[3], (D, H, HD), dtype=jnp.float32) * scale
        Wo = jax.random.normal(ks[4], (H, HD, D), dtype=jnp.float32) * scale
        bq = jnp.zeros((H, HD), dtype=jnp.float32)
        bk = jnp.zeros((H, HD), dtype=jnp.float32)
        bv = jnp.zeros((H, HD), dtype=jnp.float32)
        bo = jnp.zeros((D,), dtype=jnp.float32)
        return {'inputs_q': inputs_q, 'inputs_kv': inputs_kv, 'Wq': Wq, 'bq': bq, 'Wk': Wk, 'bk': bk, 'Wv': Wv, 'bv': bv, 'Wo': Wo, 'bo': bo}
    _L1_xattn_all = _L1_xattn_setup()
    _L1_xattn_in = {k: v for k, v in _L1_xattn_all.items() if k in ('Wq', 'bq', 'Wk', 'bk', 'Wv', 'bv', 'Wo', 'bo')}
    del _L1_xattn_all

    def _L1_ffn_setup():
        import jax, jax.numpy as jnp
        import numpy as np
        B, N, D = (4, 1024, 512)
        SPARSITY = 0.01
        key = jax.random.key(seed)
        k1, k2, k3 = jax.random.split(key, 3)
        x = jax.random.normal(k1, (B, N, D), dtype=jnp.float32)
        spatial = jax.random.normal(k2, (D, D), dtype=jnp.float32) * 0.02
        freq = jnp.fft.fft(spatial, axis=-1)
        k = int(D * SPARSITY)
        mag = jnp.abs(freq)
        kth = jax.lax.top_k(mag, k)[0][:, -1:]
        w_sparse = jnp.where(mag >= kth, freq, 0.0 + 0j)
        bias = jax.random.normal(k3, (D,), dtype=jnp.float32) * 0.01
        return {'x': x, 'w_freq_real': jnp.real(w_sparse).astype(jnp.float32), 'w_freq_imag': jnp.imag(w_sparse).astype(jnp.float32), 'bias': bias}
    _L1_ffn_all = _L1_ffn_setup()
    _L1_ffn_in = {k: v for k, v in _L1_ffn_all.items() if k in ('w_freq_real', 'w_freq_imag', 'bias')}
    del _L1_ffn_all
    return {'x': x, 'ctx_1024': ctx_1024, 'mask_BxS2_ik0': mask_BxS2_ik0, 'L0_xattn_q_w': _L0_xattn_in['q_w'], 'L0_xattn_q_b': _L0_xattn_in['q_b'], 'L0_xattn_k_w': _L0_xattn_in['k_w'], 'L0_xattn_k_b': _L0_xattn_in['k_b'], 'L0_xattn_v_w': _L0_xattn_in['v_w'], 'L0_xattn_v_b': _L0_xattn_in['v_b'], 'L0_ffn_packed_weight': _L0_ffn_in['packed_weight'], 'L0_ffn_weight_scale': _L0_ffn_in['weight_scale'], 'L0_ffn_bias': _L0_ffn_in['bias'], 'L1_xattn_Wq': _L1_xattn_in['Wq'], 'L1_xattn_bq': _L1_xattn_in['bq'], 'L1_xattn_Wk': _L1_xattn_in['Wk'], 'L1_xattn_bk': _L1_xattn_in['bk'], 'L1_xattn_Wv': _L1_xattn_in['Wv'], 'L1_xattn_bv': _L1_xattn_in['bv'], 'L1_xattn_Wo': _L1_xattn_in['Wo'], 'L1_xattn_bo': _L1_xattn_in['bo'], 'L1_ffn_w_freq_real': _L1_ffn_in['w_freq_real'], 'L1_ffn_w_freq_imag': _L1_ffn_in['w_freq_imag'], 'L1_ffn_bias': _L1_ffn_in['bias']}

def reference(x, ctx_1024, mask_BxS2_ik0, L0_xattn_q_w, L0_xattn_q_b, L0_xattn_k_w, L0_xattn_k_b, L0_xattn_v_w, L0_xattn_v_b, L0_ffn_packed_weight, L0_ffn_weight_scale, L0_ffn_bias, L1_xattn_Wq, L1_xattn_bq, L1_xattn_Wk, L1_xattn_bk, L1_xattn_Wv, L1_xattn_bv, L1_xattn_Wo, L1_xattn_bo, L1_ffn_w_freq_real, L1_ffn_w_freq_imag, L1_ffn_bias):
    import jax
    import jax.numpy as jnp

    def _L0_xattn_ref(hidden_states, context, attention_mask, q_w, q_b, k_w, k_b, v_w, v_b):
        import jax, jax.numpy as jnp
        import numpy as np
        B, LQ, LK, D = (4, 1024, 1024, 512)
        H = 16
        HD = D // H

        def _split_heads(x):
            b, l, _ = x.shape
            return x.reshape(b, l, H, HD).transpose(0, 2, 1, 3)
        q = _split_heads(hidden_states @ q_w.T + q_b)
        k = _split_heads(context @ k_w.T + k_b)
        v = _split_heads(context @ v_w.T + v_b)
        scores = jnp.einsum('bhqd,bhkd->bhqk', q, k) / jnp.sqrt(jnp.float32(HD))
        mask = (attention_mask > 0)[:, None, None, :]
        scores = jnp.where(mask, -jnp.inf, scores)
        probs = jax.nn.softmax(scores, axis=-1)
        ctx = jnp.einsum('bhqk,bhkd->bhqd', probs, v)
        ctx = ctx.transpose(0, 2, 1, 3).reshape(ctx.shape[0], ctx.shape[2], H * HD)
        return ctx

    def _L0_ffn_ref(x, packed_weight, weight_scale, bias):
        import jax, jax.numpy as jnp
        import numpy as np
        IN_F = 512
        OUT_F = 512
        B, S = (8, 2048)

        def _pack_ternary(tern):
            enc = (tern + 1.0).astype(jnp.int32).reshape(-1)
            return (enc[0::4] | enc[1::4] << 2 | enc[2::4] << 4 | enc[3::4] << 6).astype(jnp.int32)
        n = OUT_F * IN_F
        shifts = jnp.array([0, 2, 4, 6], dtype=jnp.int32)
        enc = (packed_weight[None, :] >> shifts[:, None] & 3).reshape(-1)[:n]
        w = (enc.astype(jnp.float32) - 1.0).reshape(OUT_F, IN_F) * weight_scale
        act_scale = 127.0 / jnp.maximum(jnp.max(jnp.abs(x), axis=-1, keepdims=True), 1e-05)
        x_dq = jnp.clip(jnp.round(x * act_scale), -128.0, 127.0) / act_scale
        return jnp.einsum('bsi,oi->bso', x_dq, w) + bias

    def _L1_xattn_ref(inputs_q, inputs_kv, Wq, bq, Wk, bk, Wv, bv, Wo, bo):
        import jax, jax.numpy as jnp
        import numpy as np
        B, S, D = (2, 1024, 512)
        H, HD = (16, 64)
        q = jnp.einsum('bsd,dhe->bshe', inputs_q, Wq) + bq
        k = jnp.einsum('bsd,dhe->bshe', inputs_kv, Wk) + bk
        v = jnp.einsum('bsd,dhe->bshe', inputs_kv, Wv) + bv
        q = q / jnp.sqrt(jnp.asarray(HD, dtype=q.dtype))
        scores = jnp.einsum('bqhd,bkhd->bhqk', q, k)
        weights = jax.nn.softmax(scores, axis=-1)
        ctx = jnp.einsum('bhqk,bkhd->bqhd', weights, v)
        out = jnp.einsum('bqhd,hde->bqe', ctx, Wo) + bo
        return out

    def _L1_ffn_ref(x, w_freq_real, w_freq_imag, bias):
        import jax, jax.numpy as jnp
        import numpy as np
        B, N, D = (4, 1024, 512)
        SPARSITY = 0.01
        w = jax.lax.complex(w_freq_real, w_freq_imag)
        x_freq = jnp.fft.fft(x, axis=-1)
        y_freq = jnp.einsum('bnd,do->bno', x_freq, w)
        y = jnp.real(jnp.fft.ifft(y_freq, axis=-1))
        return y + bias
    x = x + _L0_xattn_ref(_layernorm(x, axis=-1), ctx_1024, mask_BxS2_ik0, L0_xattn_q_w, L0_xattn_q_b, L0_xattn_k_w, L0_xattn_k_b, L0_xattn_v_w, L0_xattn_v_b)
    x = x + _L0_ffn_ref(_layernorm(x, axis=-1), L0_ffn_packed_weight, L0_ffn_weight_scale, L0_ffn_bias)
    x = x + _L1_xattn_ref(_layernorm(x, axis=-1), ctx_1024, L1_xattn_Wq, L1_xattn_bq, L1_xattn_Wk, L1_xattn_bk, L1_xattn_Wv, L1_xattn_bv, L1_xattn_Wo, L1_xattn_bo)
    x = x + _L1_ffn_ref(_layernorm(x, axis=-1), L1_ffn_w_freq_real, L1_ffn_w_freq_imag, L1_ffn_bias)
    return x

_drawn_inputs = setup_inputs


def setup_inputs(seed=0):
    import zlib

    import numpy as np

    out = dict(_drawn_inputs(seed))
    spreads = {'L0_xattn_q_b': (0.0, 0.8),
     'L0_xattn_k_b': (0.0, 0.8),
     'L0_xattn_v_b': (0.0, 0.1),
     'L0_ffn_bias': (0.0, 0.1),
     'L1_xattn_bq': (0.0, 0.323),
     'L1_xattn_bk': (0.0, 0.8),
     'L1_xattn_bv': (0.0, 0.1),
     'L1_xattn_bo': (0.0, 0.1)}
    factors = {'L0_xattn_q_w': 3.824, 'L0_xattn_k_w': 3.737, 'L1_ffn_bias': 8.0}
    for name, (base, spread) in spreads.items():
        noise = np.random.default_rng([zlib.crc32(name.encode()), seed]).standard_normal(out[name].shape)
        drawn = base * np.exp(spread * noise) if base else spread * noise
        out[name] = jnp.asarray(drawn.astype(out[name].dtype))
    for name, factor in factors.items():
        out[name] = (out[name] * factor).astype(out[name].dtype)
    return out
```

```python
import numpy as np
import concourse.bass as bass
from concourse import mybir
from contextlib import ExitStack

F32 = mybir.dt.float32
F16 = mybir.dt.float16
BF16 = mybir.dt.bfloat16
I32 = mybir.dt.int32
ALU = mybir.AluOpType
ACT = mybir.ActivationFunctionType
AX = mybir.AxisListType

P = 128
B, S, D = 8, 512, 512
KEYS = 77
ROWS = B * KEYS
NT = S // P
ND = D // P
H0, H1 = 32, 64
D1 = 16 * H1
ND1 = D1 // P
G = 4
GK = 4 * KEYS
CH = (GK + 2) // 3
GKP = 3 * CH
RC = (ROWS + P - 1) // P
RL = ROWS - (RC - 1) * P
EPS = 1e-5
MAGIC = 12582912.0
PS = 256.0
BIG = -1e30


class Count:

    def __init__(self):
        self.base, self.local = 0, 0

    def next(self):
        self.local += 1
        return self.base + self.local


BANK_ORDER = []
for _s in range(11):
    if _s % 2 == 1 and _s < 8:
        BANK_ORDER.append(("Z", "out", _s // 2))
    if _s % 2 == 0 and _s >= 4:
        BANK_ORDER.append(("X", "pv", _s // 2 - 2))
BANK_ORDER += [("Y", "t", t) for t in range(NT)]
BANK_ORDER += [("Y", "q", m) for m in range(ND1)]
BANK_ORDER += [("X", "t", t) for t in range(NT)] + [("X", "f", t) for t in range(NT)]
BANK_ORDER += [("Z", "t", t) for t in range(NT)]
BANK_ORDER += [("Z", "f", t) for t in range(NT)]
BANK_ORDER += [("W", "t", t) for t in range(NT)]
BANK_ORDER += [("W", "q", m) for m in range(ND)]
BANK_ORDER += [("Y", "pv", j) for j in range(ND1)]
HI_ORDER = [u for u in BANK_ORDER if u[:2] in (("Y", "t"), ("Y", "q"), ("Z", "t"), ("W", "t"), ("W", "q"), ("Y", "pv"))]
STAGES = "XYZW"
PER = {s: sum(u[0] == s for u in BANK_ORDER) for s in STAGES}
PER_HI = {s: sum(u[0] == s for u in HI_ORDER) for s in STAGES}


class Iteration:

    def __init__(self, i, present):
        self.i, self.present = i, present
        lag = {"W": -1, "X": 0, "Y": 1, "Z": 2}
        self.done = {s: (i - lag[s] if s in present else (0 if isinstance(i, int) and i < lag[s] else B)) for s in STAGES}
        self.order = [u for u in BANK_ORDER if u[0] in present]
        self.hi_order = [u for u in HI_ORDER if u[0] in present]

    def total(self, per):
        out = 0
        for s in STAGES:
            if per.get(s):
                out = out + self.done[s] * per[s]
        return out

    def bank(self, *use):
        k = self.order.index(use)
        return k % 2, self.total(PER) + k

    def hi(self, *use):
        return self.total(PER_HI) + self.hi_order.index(use)

    def unit(self, stage, u):
        k = u + (8 if stage == "Y" and "X" in self.present else 0)
        return self.total({"X": 8, "Y": 8}) + k


def plan():
    return ([(-1, "W"), (0, "WX"), (1, "WXY")], (2, B - 1, "WXYZ"), [(B - 1, "XYZ"), (B, "YZ"), (B + 1, "Z")])


def walk(eng, body):
    first, (a, b, stages), last = plan()
    for i, p in first:
        body(Iteration(i, p), None)
    with eng.Fori(a, b) as i:
        body(Iteration(i, stages), (a, b))
    for i, p in last:
        body(Iteration(i, p), None)


def products(pe, out, lhs, rhs, start, stop, skip=False):
    kw = dict(skip_group_check=True) if skip else {}
    pe.matmul(out, lhs(0), rhs(0), start=start, stop=False, **kw)
    pe.matmul(out, lhs(0), rhs(1), start=False, stop=False, **kw)
    return pe.matmul(out, lhs(1), rhs(0), start=False, stop=stop, **kw)


def program(nc, x, ctxT, mask, wq0, bq0, wk0, bk0, wv0, bv0, packed, wscale, bf0,
            wq1, bq1, wk1, bk1, wv1, bv1, wo, bo, wf, bf1, dft, eye, out):
    scr_k0 = nc.dram_tensor("scr_k0", (P, B, 2 * ND * KEYS), F16, kind="Internal").ap()
    scr_k1 = nc.dram_tensor("scr_k1", (P, B, 2 * ND1 * KEYS), F16, kind="Internal").ap()
    scr_v0 = nc.dram_tensor("scr_v0", (RC * P, 4, 2 * G * H0), F16, kind="Internal").ap()
    scr_v1 = nc.dram_tensor("scr_v1", (RC * P, 4, 2 * G * H1), F16, kind="Internal").ap()
    keep = ExitStack()
    with keep:
        def sb(stack, name, shape, dt):
            return stack.enter_context(nc.sbuf_tensor(name, shape, dt))

        k = {}
        k["wq0"] = sb(keep, "wq0_hl", [P, 2, ND, D], F16)
        k["wq1"] = sb(keep, "wq1_hl", [P, 2, ND, D1], F16)
        k["wo"] = sb(keep, "wo_hl", [P, 2, ND1, D], F16)
        k["m"] = sb(keep, "m_hl", [P, 2, ND, D], F16)
        k["tern"] = sb(keep, "tern", [P, ND, D], BF16)
        k["ident"] = sb(keep, "ident", [P, P], F32)
        k["identb"] = sb(keep, "identb", [P, P], BF16)
        k["bq0"] = sb(keep, "bq0_s", [P, ND], F32)
        k["bq1"] = sb(keep, "bq1_s", [P, ND1], F32)
        k["bo"] = sb(keep, "bo_b", [P, D], F32)
        k["bf0"] = sb(keep, "bf0_b", [P, D], F32)
        k["bf1"] = sb(keep, "bf1_b", [P, D], F32)
        k["maskall"] = sb(keep, "maskall", [1, B, KEYS], BF16)
        k["scale"] = sb(keep, "scale", [P, 16], F32)
        k["inv"] = sb(keep, "inv", [P, 16], F32)
        k["factor"] = sb(keep, "factor", [P, 8], F32)
        setup_context(nc, k, ctxT, wk0, bk0, wv0, bv0, wk1, bk1, wv1, bv1, scr_k0, scr_k1, scr_v0, scr_v1)
        setup_weights(nc, k, mask, wq0, bq0, packed, wscale, bf0, wq1, bq1, wo, bo, wf, bf1, dft, eye)
        layers(nc, k, x, scr_k0, scr_k1, scr_v0, scr_v1, out)


S_CTX, S_WK0, S_WV0, S_WK1A, S_WK1B, S_WV1A, S_WV1B, S_K0, S_V0, S_K1, S_V1, S_WF, S_WQ0, S_WQ1, S_WO, S_M = range(16)
F_E0, F_E1, F_PV0, F_OUT, F_WSC, F_A, F_KV = range(7)


class Chain:

    def __init__(self, dve, sem):
        self.dve, self.sem, self.count = dve, sem, Count()

    def __call__(self, ins):
        v = self.count.next()
        ins.then_inc(self.sem, 1)
        self.dve.wait_ge(self.sem, v)


def find_scale(dve, step, k, slot, absmax, allmax, absmax_ready, allmax_ready, n):
    dve.wait_ge(allmax_ready, n + 1)
    a = allmax[:, slot:slot + 1]
    step(dve.tensor_scalar(a, a, 1e-30, 1e37, ALU.max, ALU.min))
    step(dve.tensor_scalar(a.bitcast(I32), a.bitcast(I32), 0x7F800000, None, ALU.bitwise_and))
    step(dve.reciprocal(k["scale"][:, slot:slot + 1], a))
    step(dve.tensor_scalar(k["scale"][:, slot:slot + 1], k["scale"][:, slot:slot + 1], 32.0, None, ALU.mult))
    step(dve.tensor_scalar(k["inv"][:, slot:slot + 1], a, 1.0 / 32.0, None, ALU.mult))


def setup_context(nc, k, ctxT, wk0, bk0, wv0, bv0, wk1, bk1, wv1, bv1, scr_k0, scr_k1, scr_v0, scr_v1):
    here = ExitStack()
    with here:
        def sb(name, shape, dt):
            return here.enter_context(nc.sbuf_tensor(name, shape, dt))

        def sem(name):
            return here.enter_context(nc.semaphore(name))

        stage = sb("a_stage", [P, 2, ND, ROWS], F32)
        ctx_hl = sb("a_ctx_hl", [P, 2, ND, ROWS], F16)
        w_hl = sb("a_w_hl", [P, 2, 2, ND, D], F16)
        kf = sb("a_kf", [P, ND1, ROWS], F32)
        vf = sb("a_vf", [P, RC, D1], F32)
        ks = sb("a_ks", [P, B * 2 * ND1 * KEYS], F16)
        vs = sb("a_vs", [P, RC * 2 * D1], F16)
        kb0, kb1 = sb("a_kb0", [P, ND], F32), sb("a_kb1", [P, ND1], F32)
        vb0, vb1 = sb("a_vb0", [P, D], F32), sb("a_vb1", [P, D1], F32)
        absmax, allmax = sb("a_absmax", [P, 16], F32), sb("a_allmax", [P, 16], F32)
        kbank = here.enter_context(nc.psum_tensor("a_kbank", [P, 4, D], F32))
        vbank = here.enter_context(nc.psum_tensor("a_vbank", [P, 4, D], F32))

        loaded = [sem(f"a_loaded{i}") for i in range(2)]
        bias_in, dve_step, absmax_ready, allmax_ready = sem("a_bias_in"), sem("a_dve_step"), sem("a_absmax_ready"), sem("a_allmax_ready")
        scale_ready, hi_done, lo_done = sem("a_scale_ready"), sem("a_hi_done"), sem("a_lo_done")
        k_full, k_free, v_full, v_free = sem("a_k_full"), sem("a_k_free"), sem("a_v_full"), sem("a_v_free")
        kout, vout = sem("a_kout"), sem("a_vout")

        W = [(S_CTX, ROWS, ctxT), (S_WK0, D, wk0), (S_WV0, D, wv0), (S_WK1A, D, wk1[:, :, 0:D]), (S_WK1B, D, wk1[:, :, D:D1]),
             (S_WV1A, D, wv1[:, :, 0:D]), (S_WV1B, D, wv1[:, :, D:D1])]
        SPLITS = [0, 1, 2, 3, "K0", "V0", 4, 5, "K1", 6, "V1"]
        nth = {s: n for n, s in enumerate(SPLITS)}
        K0N, K1N = 2 * ND, 2 * ND1
        last_use = {1: ("k", K0N), 2: ("v", RC), 3: ("k", K0N + K1N // 2), 4: ("k", K0N + K1N)}

        block = here.enter_context(nc.Block())

        def dst(s):
            if s == 0:
                return [ctx_hl[:, h, :, :] for h in range(2)], stage[:, 0, :, :], S_CTX
            if isinstance(s, int):
                return [w_hl[:, (s - 1) % 2, h, :, :] for h in range(2)], stage[:, s % 2, :, 0:D], W[s][0]
            if s[0] == "K":
                m = ND if s == "K0" else ND1
                o = ks[:, 0:B * 2 * m * KEYS].rearrange("p (b h m k) -> p h m b k", b=B, h=2, m=m)
                return [o[:, h] for h in range(2)], kf[:, 0:m, :].rearrange("p m (b k) -> p m b k", b=B), S_K0 if s == "K0" else S_K1
            n = D if s == "V0" else D1
            o = vs[:, 0:RC * 2 * n].rearrange("p (r j h d) -> p h (r j) d", r=RC, j=4, h=2)
            i = vf[:, :, :].rearrange("p r n -> p (r n)")[:, 0:RC * n].rearrange("p (rj d) -> p rj d", d=n // 4)
            return [o[:, h] for h in range(2)], i, S_V0 if s == "V0" else S_V1

        @block.sync
        def _(sp):
            for n, (slot, width, src) in enumerate(W):
                if n >= 2:
                    sp.wait_ge(lo_done, nth[n - 2] + 1)
                sp.dma_start(stage[:, n % 2, :, 0:width], src).then_inc(loaded[n % 2], 16)
            sp.wait_ge(kout, 32)
            sp.wait_ge(vout, 32)

        @block.gpsimd
        def _(pool):
            pool.dma_start(kb0[:, :], bk0).then_inc(bias_in, 16)
            pool.dma_start(kb1[:, :], bk1).then_inc(bias_in, 16)
            pool.dma_start(vb0[:, :], bv0.partition_broadcast(P)).then_inc(bias_in, 16)
            pool.dma_start(vb1[:, :], bv1.partition_broadcast(P)).then_inc(bias_in, 16)
            for n, s in enumerate(SPLITS):
                slot = dst(s)[2]
                pool.wait_ge(absmax_ready, n + 1)
                pool.partition_all_reduce(allmax[:, slot:slot + 1], absmax[:, slot:slot + 1], P,
                                          bass.bass_isa.ReduceOp.absmax).then_inc(allmax_ready, 1)
                if s in ("K0", "V0", "K1", "V1"):
                    pool.wait_ge(lo_done, n + 1)
                if s == "K0":
                    pool.dma_start(scr_k0.rearrange("p b n -> p (b n)"), ks[:, 0:B * 2 * ND * KEYS]).then_inc(kout, 16)
                if s == "K1":
                    pool.dma_start(scr_k1.rearrange("p b n -> p (b n)"), ks[:, :]).then_inc(kout, 16)
                if s == "V0":
                    pool.dma_start(scr_v0.rearrange("(r p) j n -> p r (j n)", p=P),
                                   vs[:, 0:RC * 2 * D].rearrange("p (r n) -> p r n", r=RC)).then_inc(vout, 16)
                if s == "V1":
                    pool.dma_start(scr_v1.rearrange("(r p) j n -> p r (j n)", p=P),
                                   vs[:, :].rearrange("p (r n) -> p r n", r=RC)).then_inc(vout, 16)

        @block.vector
        def _(dve):
            step = Chain(dve, dve_step)
            step(dve.memset(vf[:, :, :], 0.0))

            def split(s):
                n = nth[s]
                (hi, lo), src, slot = dst(s)
                if isinstance(s, int):
                    dve.wait_ge(loaded[s % 2], 16 * (s // 2 + 1))
                elif s[0] == "K":
                    dve.wait_ge(k_free, K0N if s == "K0" else K0N + K1N)
                dve.tensor_reduce(absmax[:, slot:slot + 1], src, AX.XYZ if len(src.shape) == 4 else AX.XY, ALU.max,
                                  apply_absolute_value=True).then_inc(absmax_ready, 1)
                find_scale(dve, step, k, slot, absmax, allmax, absmax_ready, allmax_ready, n)
                dve.tensor_copy(allmax[:, slot:slot + 1], k["scale"][:, slot:slot + 1]).then_inc(scale_ready, 1)
                dve.wait_ge(hi_done, n + 1)
                if len(src.shape) == 4:
                    for m in range(src.shape[1]):
                        ins = dve.scalar_tensor_tensor(out=lo[:, m], in0=src[:, m], scalar=k["scale"][:, slot:slot + 1],
                                                       in1=hi[:, m], op0=ALU.mult, op1=ALU.subtract)
                else:
                    ins = dve.scalar_tensor_tensor(out=lo, in0=src, scalar=k["scale"][:, slot:slot + 1], in1=hi,
                                                   op0=ALU.mult, op1=ALU.subtract)
                ins.then_inc(lo_done, 1)

            def v_evacuate(w, slot, bias, n0, col, width):
                step(dve.tensor_tensor(k["factor"][:, F_KV:F_KV + 1], k["inv"][:, S_CTX:S_CTX + 1],
                                       k["inv"][:, slot:slot + 1], ALU.mult))
                flat = vf[:, :, :].rearrange("p r n -> p (r n)")
                for r in range(RC):
                    rows = P if r < RC - 1 else RL
                    dve.wait_ge(v_full, n0 + r + 1)
                    dve.scalar_tensor_tensor(out=flat[0:rows, r * width + col:r * width + col + D], in0=vbank[0:rows, (n0 + r) % 4, :],
                                             scalar=k["factor"][0:rows, F_KV:F_KV + 1], in1=bias[0:rows, :],
                                             op0=ALU.mult, op1=ALU.add).then_inc(v_free, 1)
                dve.wait_ge(v_free, n0 + RC)

            for s in (0, 1, 2, 3):
                split(s)
            split("K0")
            dve.wait_ge(bias_in, 64)
            v_evacuate(2, S_WV0, vb0, 0, 0, D)
            split("V0")
            dve.wait_ge(lo_done, nth["V0"] + 1)
            step(dve.memset(vf[:, :, :], 0.0))
            split(4)
            split(5)
            split("K1")
            split(6)
            v_evacuate(5, S_WV1A, vb1[:, 0:D], RC, 0, D1)
            v_evacuate(6, S_WV1B, vb1[:, D:D1], 2 * RC, D, D1)
            split("V1")

        @block.scalar
        def _(act):
            fac = sb("a_kfactor", [P, 4], F32)

            def hi_part(s):
                n = nth[s]
                (hi, lo), src, slot = dst(s)
                act.wait_ge(scale_ready, n + 1)
                if s in last_use:
                    pass
                if isinstance(s, int) and s - 2 in last_use:
                    kind, v = last_use[s - 2]
                    act.wait_ge(k_full if kind == "k" else v_full, v)
                if s == "K1":
                    act.wait_ge(kout, 16)
                if s == "V1":
                    act.wait_ge(vout, 16)
                if len(src.shape) == 4:
                    for m in range(src.shape[1]):
                        ins = act.activation(hi[:, m], src[:, m], ACT.Copy, scale=k["scale"][:, slot:slot + 1])
                else:
                    ins = act.activation(hi, src, ACT.Copy, scale=k["scale"][:, slot:slot + 1])
                ins.then_inc(hi_done, 1)

            kfac = sem("a_kfac")

            def k_evacuate(n0, m0, slot, bias, j):
                act.activation(fac[:, j:j + 1], k["inv"][:, S_CTX:S_CTX + 1], ACT.Copy,
                               scale=k["inv"][:, slot:slot + 1]).then_inc(kfac, 1)
                act.wait_ge(kfac, j + 1)
                for m in range(ND):
                    for half in range(2):
                        n = n0 + 2 * m + half
                        act.wait_ge(k_full, n + 1)
                        act.activation(kf[:, m0 + m, half * ROWS // 2:(half + 1) * ROWS // 2], kbank[:, n % 4, 0:ROWS // 2],
                                       ACT.Identity, bias=bias[:, m0 + m:m0 + m + 1], scale=fac[:, j:j + 1]).then_inc(k_free, 1)

            for s in (0, 1, 2):
                hi_part(s)
            act.wait_ge(bias_in, 64)
            k_evacuate(0, 0, S_WK0, kb0, 0)
            for s in (3, "K0"):
                hi_part(s)
            hi_part("V0")
            act.wait_ge(lo_done, nth["K0"] + 1)
            k_evacuate(K0N, 0, S_WK1A, kb1, 1)
            hi_part(4)
            k_evacuate(2 * K0N, ND, S_WK1B, kb1, 2)
            for s in (5, "K1", 6, "V1"):
                hi_part(s)

        @block.tensor
        def _(pe):
            def keys(w, n0):
                pe.wait_ge(lo_done, nth[w] + 1)
                for m in range(ND):
                    for half in range(2):
                        n = n0 + 2 * m + half
                        if n >= 4:
                            pe.wait_ge(k_free, n - 3)
                        for c in range(ND):
                            ins = products(pe, kbank[:, n % 4, 0:ROWS // 2],
                                           lambda h: w_hl[:, (w - 1) % 2, h, c, m * P:(m + 1) * P],
                                           lambda h: ctx_hl[:, h, c, half * ROWS // 2:(half + 1) * ROWS // 2], c == 0, c == ND - 1)
                        ins.then_inc(k_full, 1)

            def values(w, n0):
                pe.wait_ge(lo_done, nth[w] + 1)
                for r in range(RC):
                    rows, n = (P if r < RC - 1 else RL), n0 + r
                    if n >= 4:
                        pe.wait_ge(v_free, n - 3)
                    for c in range(ND):
                        ins = products(pe, vbank[0:rows, n % 4, :], lambda h: ctx_hl[:, h, c, r * P:r * P + rows],
                                       lambda h: w_hl[:, (w - 1) % 2, h, c, :], c == 0, c == ND - 1)
                    ins.then_inc(v_full, 1)

            pe.wait_ge(lo_done, 1)
            keys(1, 0)
            values(2, 0)
            keys(3, K0N)
            keys(4, 2 * K0N)
            values(5, RC)
            values(6, 2 * RC)


def setup_weights(nc, k, mask, wq0, bq0, packed, wscale, bf0, wq1, bq1, wo, bo, wf, bf1, dft, eye):
    here = ExitStack()
    with here:
        def sb(name, shape, dt):
            return here.enter_context(nc.sbuf_tensor(name, shape, dt))

        def sem(name):
            return here.enter_context(nc.semaphore(name))

        stage = sb("b_stage", [P, 2, 8 * D], F32)
        dft_hl = sb("b_dft", [P, 3, 2, ND, D], F16)
        wf_hl = sb("b_wf_hl", [P, 2, 2 * ND, D], F16)
        a_hl = sb("b_a_hl", [P, 2, 2, ND, D], F16)
        mf = sb("b_mf", [P, ND, D], F32)
        pk, enc = sb("b_pk", [P, D], I32), sb("b_enc", [P, 4, D], I32)
        ternrow = sb("b_ternrow", [P, 4, D], BF16)
        absmax, allmax = sb("b_absmax", [P, 16], F32), sb("b_allmax", [P, 16], F32)
        bmax = sb("b_bmax", [P, 2], F32)
        mraw, mkf = sb("b_mraw", [1, B, KEYS], I32), sb("b_mkf", [1, B, KEYS], F32)
        nval = sb("b_nval", [1, B], F32)
        bank = here.enter_context(nc.psum_tensor("b_bank", [P, 4, D], F32))
        tbank = here.enter_context(nc.psum_tensor("b_tbank", [P, 4, 2 * D], BF16))

        loaded = [sem(f"b_loaded{i}") for i in range(2)]
        small_in, dft_in, dve_step = sem("b_small_in"), sem("b_dft_in"), sem("b_dve_step")
        absmax_ready, allmax_ready, scale_ready = sem("b_absmax_ready"), sem("b_allmax_ready"), sem("b_scale_ready")
        hi_done, lo_done = sem("b_hi_done"), sem("b_lo_done")
        full, a_hi, free = sem("b_full"), sem("b_a_hi"), sem("b_free")
        tern_rows, tern_full = sem("b_tern_rows"), sem("b_tern_full")

        W = [(S_WF, wf_hl, wf, 2 * ND * D), (S_WQ0, k["wq0"], wq0, ND * D), (S_WQ1, k["wq1"], wq1, ND * D1),
             (S_WO, k["wo"], wo, ND1 * D)]
        block = here.enter_context(nc.Block())

        def flat(t, h):
            return t[:, h, :, :].rearrange("p a n -> p (a n)")

        @block.sync
        def _(sp):
            for n, (slot, _, src, width) in enumerate(W):
                if n == 1:
                    sp.dma_start(dft_hl[:, :, :, :, :].rearrange("p a h c n -> p (a h c n)"), dft).then_inc(dft_in, 16)
                if n >= 2:
                    sp.wait_ge(lo_done, n - 1)
                sp.dma_start(stage[:, n % 2, 0:width], src).then_inc(loaded[n % 2], 16)

        @block.gpsimd
        def _(pool):
            pool.dma_start(pk[:, :], packed).then_inc(small_in, 16)
            pool.dma_start(k["ident"][:, :], eye).then_inc(small_in, 16)
            pool.dma_start(k["bq0"][:, :], bq0).then_inc(small_in, 16)
            pool.dma_start(k["bq1"][:, :], bq1).then_inc(small_in, 16)
            pool.dma_start(k["bo"][:, :], bo.partition_broadcast(P)).then_inc(small_in, 16)
            pool.dma_start(k["bf0"][:, :], bf0.partition_broadcast(P)).then_inc(small_in, 16)
            pool.dma_start(k["bf1"][:, :], bf1.partition_broadcast(P)).then_inc(small_in, 16)
            pool.dma_start(k["factor"][:, F_WSC:F_WSC + 1], wscale.partition_broadcast(P)).then_inc(small_in, 16)
            pool.dma_start(mraw[:, :, :].rearrange("o b n -> o (b n)"), mask).then_inc(small_in, 16)
            for n, slot in enumerate((S_WF, S_WQ0, S_WQ1, S_WO, S_M)):
                pool.wait_ge(absmax_ready, n + 1)
                pool.partition_all_reduce(allmax[:, slot:slot + 1], absmax[:, slot:slot + 1], P,
                                          bass.bass_isa.ReduceOp.absmax).then_inc(allmax_ready, 1)

        @block.vector
        def _(dve):
            step = Chain(dve, dve_step)

            def split(n, slot, src, out):
                am = absmax[:, slot:slot + 1]
                if slot in (S_WQ0, S_WQ1):
                    b, j = (k["bq0"], 0) if slot == S_WQ0 else (k["bq1"], 1)
                    step(dve.tensor_reduce(bmax[:, j:j + 1], b[:, :], AX.X, ALU.max, apply_absolute_value=True))
                    step(dve.tensor_reduce(am, src, AX.X, ALU.max, apply_absolute_value=True))
                    dve.scalar_tensor_tensor(out=am, in0=bmax[:, j:j + 1], scalar=1.0 / 256.0, in1=am,
                                             op0=ALU.mult, op1=ALU.max).then_inc(absmax_ready, 1)
                else:
                    dve.tensor_reduce(am, src, AX.X, ALU.max, apply_absolute_value=True).then_inc(absmax_ready, 1)
                find_scale(dve, step, k, slot, absmax, allmax, absmax_ready, allmax_ready, n)
                sc = k["scale"][:, slot:slot + 1]
                dve.tensor_copy(allmax[:, slot:slot + 1], sc).then_inc(scale_ready, 1)
                if slot in (S_WQ0, S_WQ1):
                    step(dve.tensor_scalar(b[:, :], b[:, :], sc, None, ALU.mult))
                dve.wait_ge(hi_done, n + 1)
                dve.scalar_tensor_tensor(out=flat(out, 1), in0=src, scalar=sc, in1=flat(out, 0),
                                         op0=ALU.mult, op1=ALU.subtract).then_inc(lo_done, 1)

            dve.wait_ge(loaded[0], 16)
            split(0, S_WF, stage[:, 0, :], wf_hl)
            dve.wait_ge(small_in, 144)
            for s in range(4):
                step(dve.tensor_scalar(enc[:, s, :], pk[:, :], 2 * s, 3, ALU.logical_shift_right, ALU.bitwise_and))
            step(dve.tensor_copy(k["identb"][:, :], k["ident"][:, :]))
            dve.tensor_scalar(ternrow[:, :, :], enc[:, :, :], -1.0, None, ALU.add).then_inc(tern_rows, 1)
            step(dve.tensor_scalar(mkf[:, :, :], mraw[:, :, :], 0.0, None, ALU.is_gt))
            step(dve.tensor_reduce(nval[:, :], mkf[:, :, :], AX.X, ALU.add))
            step(dve.tensor_scalar(nval[:, :], nval[:, :], -1.0, float(KEYS), ALU.mult, ALU.add))
            step(dve.reciprocal(nval[:, :], nval[:, :]))
            step(dve.tensor_scalar(nval[:, :], nval[:, :], 0.0, None, ALU.mult))
            step(dve.tensor_scalar(mkf[:, :, :], mkf[:, :, :], BIG, None, ALU.mult))
            step(dve.tensor_tensor(k["maskall"][:, :, :], mkf[:, :, :],
                                   nval[:, :].rearrange("o (b u) -> o b u", u=1).broadcast_to([1, B, KEYS]), ALU.add))
            dve.wait_ge(loaded[1], 16)
            split(1, S_WQ0, stage[:, 1, 0:ND * D], k["wq0"])
            for c in range(ND):
                dve.wait_ge(tern_full, c + 1)
                dve.tensor_copy(k["tern"][:, c, :], tbank[:, c, 0:D])
            for j in range(2 * ND):
                dve.wait_ge(a_hi, j + 1)
                dve.scalar_tensor_tensor(out=a_hl[:, j // ND, 1, j % ND, :], in0=bank[:, j % 4, :], scalar=0.25,
                                         in1=a_hl[:, j // ND, 0, j % ND, :], op0=ALU.mult, op1=ALU.subtract).then_inc(free, 1)
            dve.wait_ge(loaded[0], 32)
            split(2, S_WQ1, stage[:, 0, :], k["wq1"])
            step(dve.tensor_scalar(k["factor"][:, F_A:F_A + 1], k["inv"][:, S_WF:S_WF + 1], 4.0 / D, None, ALU.mult))
            for j in range(ND):
                dve.wait_ge(full, 2 * ND + j + 1)
                dve.tensor_scalar(mf[:, j, :], bank[:, j % 4, :], k["factor"][:, F_A:F_A + 1], None, ALU.mult).then_inc(free, 1)
            dve.wait_ge(loaded[1], 32)
            split(3, S_WO, stage[:, 1, :], k["wo"])
            dve.wait_ge(free, 3 * ND)
            split(4, S_M, mf[:, :, :].rearrange("p a n -> p (a n)"), k["m"])
            def factor(slot, a, b, c):
                f = k["factor"][:, slot:slot + 1]
                if b is None:
                    step(dve.tensor_scalar(f, k["inv"][:, a:a + 1], c, None, ALU.mult))
                else:
                    step(dve.tensor_scalar(f, k["inv"][:, a:a + 1], k["inv"][:, b:b + 1], None, ALU.mult))
                    step(dve.tensor_scalar(f, f, c, None, ALU.mult))
            factor(F_E0, S_WQ0, S_K0, float(H0) ** -0.5)
            factor(F_E1, S_WQ1, S_K1, float(H1) ** -0.5)
            factor(F_PV0, S_V0, None, 1.0 / PS)
            factor(F_OUT, S_V1, S_WO, 1.0 / PS)
            f = k["factor"][:, F_WSC:F_WSC + 1]
            step(dve.tensor_scalar(f, f, 1.0 / 127.0, None, ALU.mult))

        @block.scalar
        def _(act):
            def hi_part(n, slot, src, out):
                act.wait_ge(scale_ready, n + 1)
                act.activation(flat(out, 0), src, ACT.Copy, scale=k["scale"][:, slot:slot + 1]).then_inc(hi_done, 1)

            hi_part(0, S_WF, stage[:, 0, :], wf_hl)
            hi_part(1, S_WQ0, stage[:, 1, 0:ND * D], k["wq0"])
            for j in range(2 * ND):
                act.wait_ge(full, j + 1)
                act.activation(a_hl[:, j // ND, 0, j % ND, :], bank[:, j % 4, :], ACT.Copy, scale=0.25).then_inc(a_hi, 1)
            hi_part(2, S_WQ1, stage[:, 0, :], k["wq1"])
            hi_part(3, S_WO, stage[:, 1, :], k["wo"])
            hi_part(4, S_M, mf[:, :, :].rearrange("p a n -> p (a n)"), k["m"])

        @block.tensor
        def _(pe):
            pe.wait_ge(tern_rows, 1)
            for c in range(ND):
                for s in range(4):
                    ins = pe.transpose(tbank[:, c, s * P:(s + 1) * P], ternrow[:, s, c * P:(c + 1) * P], k["identb"][:, :])
                ins.then_inc(tern_full, 1)
            pe.wait_ge(lo_done, 1)
            pe.wait_ge(dft_in, 16)
            COS, SIN, NSIN = range(3)
            for j in range(2 * ND):
                part, o = j // ND, j % ND
                if j >= 4:
                    pe.wait_ge(free, j - 3)
                terms = ((0, COS), (1, SIN)) if part == 0 else ((1, COS), (0, NSIN))
                for n, (w, f) in enumerate(terms):
                    for c in range(ND):
                        ins = products(pe, bank[:, j % 4, :], lambda h: wf_hl[:, h, w * ND + c, o * P:(o + 1) * P],
                                       lambda h: dft_hl[:, f, h, c, :], n == 0 and c == 0, n == 1 and c == ND - 1)
                ins.then_inc(full, 1)
            for j in range(ND):
                n = 2 * ND + j
                pe.wait_ge(free, n - 3 if j else 2 * ND)
                for part, f in ((0, COS), (1, NSIN)):
                    for c in range(ND):
                        ins = products(pe, bank[:, n % 4, :], lambda h: a_hl[:, part, h, c, j * P:(j + 1) * P],
                                       lambda h: dft_hl[:, f, h, c, :], part == 0 and c == 0, part == 1 and c == ND - 1)
                ins.then_inc(full, 1)


def layers(nc, k, x, scr_k0, scr_k1, scr_v0, scr_v1, out):
    here = ExitStack()
    with here:
        def sb(name, shape, dt):
            return here.enter_context(nc.sbuf_tensor(name, shape, dt))

        def sem(name):
            return here.enter_context(nc.semaphore(name))

        x_in = sb("x_in", [P, NT, D], F32)
        x1 = sb("x1", [P, NT, D], F32)
        x2 = sb("x2", [P, NT, D], F32)
        x2b = sb("x2b", [P, NT, D], F32)
        x3 = sb("x3", [P, NT, D], F32)
        xn = sb("xn", [P, NT, D], F32)
        qi = sb("qi", [P, NT, D], BF16)
        xT = sb("xT", [P, 2, ND, S], F16)
        qiT = xT[:, 0, :, :].bitcast(BF16)
        q0T = sb("q0T", [P, 2, ND, S], F16)
        qc = sb("qc", [P, 2, ND1, S], F16)
        prT = sb("prT", [CH, 2, G, 3, S], F16)
        pr = [sb(f"pr{i}", [P, 2, GKP], F32) for i in range(4)]
        k0d, k1d = sb("k0d", [P, 2, ND, KEYS], F16), sb("k1d", [P, 2, ND1, KEYS], F16)
        k0b = sb("k0b", [P, 2, ND, 4, KEYS], F16)
        k1b = sb("k1b", [P, 2, ND1, 2, KEYS], F16)
        v0b = sb("v0b", [CH, 3, 2, 2, G, H0], F16)
        v1b = sb("v1b", [CH, 2, G, 8, H1], F16)
        mrow = sb("mrow", [1, 4, KEYS], BF16)
        ones = sb("ones", [1, P], BF16)
        mx, sm = sb("mx", [P, 4, 8], F32), sb("sm", [P, 4, 8], F32)
        stats = sb("stats", [P, 4, NT, 6], F32)
        mean, half = sb("mean", [P, 4, NT], F32), sb("half", [P, 4, NT], F32)
        var, rstd = sb("var", [P, 4, NT], F32), sb("rstd", [P, 4, NT], F32)
        mhalf = sb("mhalf", [P, NT], F32)
        amax, ascale, cscale = sb("amax", [P, NT], F32), sb("ascale", [P, NT], F32), sb("cscale", [P, NT], F32)
        sc = here.enter_context(nc.psum_tensor("scores", [P, 2, 2, D], F32))
        ptb = here.enter_context(nc.psum_tensor("ptb", [P, 2, D], F32))
        wb = here.enter_context(nc.psum_tensor("wb", [P, 2, D], F32))

        dve_step, prep = sem("dve_step"), sem("prep")
        x_loaded, k0_loaded, k1_loaded, v0_loaded, v1_loaded, stored = (sem(n) for n in (
            "x_loaded", "k0_loaded", "k1_loaded", "v0_loaded", "v1_loaded", "stored"))
        k0_ready, k1_ready = sem("k0_ready"), sem("k1_ready")
        bank_full, bank_hi, bank_free = sem("bank_full"), sem("bank_hi"), sem("bank_free")
        scores_full, scores_free, exp_done, sums_ready, probs_ready = (sem(n) for n in (
            "scores_full", "scores_free", "exp_done", "sums_ready", "probs_ready"))
        prT_full, prT_hi, prT_free = sem("prT_full"), sem("prT_hi"), sem("prT_free")
        ln_var = [sem(f"ln_var{i}") for i in range(4)]
        ln_rstd = [sem(f"ln_rstd{i}") for i in range(4)]
        ln_done = [sem(f"ln_done{i}") for i in range(4)]
        x1_biased, x2_biased, x3_biased = sem("x1_biased"), sem("x2_biased"), sem("x3_biased")

        x_v = x.rearrange("b (p t) d -> b p t d", t=NT)
        out_v = out.rearrange("b (p t) d -> b p t d", t=NT)
        PIECES = []
        for hh in range(4):
            r = hh * KEYS
            while r < (hh + 1) * KEYS:
                c = r // CH
                n = min((c + 1) * CH, (hh + 1) * KEYS) - r
                PIECES.append((hh, c, r - c * CH, r - hh * KEYS, n))
                r += n
        V1SLOT = {(0, 0): 0, (1, 0): 1, (1, 1): 3, (2, 1): 4, (2, 2): 6, (3, 2): 7}
        PREP = 7
        block = here.enter_context(nc.Block())

        @block.sync
        def _(sp):
            def load_kv(layer, b):
                kd, scr_k, kl = (k0d, scr_k0, k0_loaded) if layer == 0 else (k1d, scr_k1, k1_loaded)
                sp.dma_start(kd[:, :, :, :].rearrange("p h m n -> p (h m n)"), scr_k[:, b, :]).then_inc(kl, 16)
                for hh, c, r0, k0, n in PIECES:
                    if layer == 0:
                        src = scr_v0[bass.ds(b * KEYS + k0, n), hh, :]
                        sp.dma_start(v0b[r0:r0 + n, c, hh - c, :, :, :].rearrange("p h g d -> p (h g d)"), src).then_inc(v0_loaded, 16)
                    else:
                        src = scr_v1[bass.ds(b * KEYS + k0, n), hh, :]
                        sp.dma_start(v1b[r0:r0 + n, :, :, V1SLOT[hh, c], :].rearrange("p h g d -> p (h g) d"),
                                     src.rearrange("p (q d) -> p q d", d=H1)).then_inc(v1_loaded, 16)

            sp.wait_ge(prep, PREP)

            def body(it, loop):
                i = it.i
                if "Y" in it.present:
                    if not (isinstance(i, int) and i == 1):
                        sp.wait_ge(k1_ready, it.done["Y"])
                        sp.wait_ge(bank_full, it.bank(*it.order[0])[1])
                    load_kv(1, it.done["Y"])
                if "W" in it.present:
                    if "X" in it.present:
                        sp.wait_ge(bank_free, it.bank("X", "pv", NT - 1)[1] + 1)
                        sp.wait_ge(k0_ready, it.done["W"])
                    sp.dma_start(x_in[:, :, :], x_v[it.done["W"]]).then_inc(x_loaded, 16)
                    load_kv(0, it.done["W"])
                if "Z" in it.present:
                    sp.wait_ge(bank_free, it.bank("Z", "f", NT - 1)[1] + 1)
                    sp.dma_start(out_v[it.done["Z"]], x3[:, :, :]).then_inc(stored, 16)

            walk(sp, body)
            sp.wait_ge(stored, 16 * B)

        @block.gpsimd
        def _(pool):
            pool.memset(v0b[:, :, :, :, :, :], 0.0).then_inc(prep, 1)
            pool.memset(v1b[:, :, :, :, :], 0.0).then_inc(prep, 1)
            pool.memset(k0b[:, :, :, :, :], 0.0).then_inc(prep, 1)
            pool.memset(k1b[:, :, :, :, :], 0.0).then_inc(prep, 1)
            pool.memset(ones[:, :], 1.0).then_inc(prep, 1)
            pool.memset(mhalf[:, :], -0.5).then_inc(prep, 1)
            for n in range(4):
                last = pool.memset(pr[n][:, :, GK:GKP], 0.0)
            last.then_inc(prep, 1)
            pool.wait_ge(prep, PREP)

            def rstd_of(j, b):
                pool.wait_ge(ln_var[j], b + 1)
                pool.tensor_tensor(rstd[:, j, :], var[:, j, :], mhalf[:, :], ALU.pow).then_inc(ln_rstd[j], 1)

            def normalise(U, n):
                p = pr[n % 4]
                pool.wait_ge(sums_ready, U + 1)
                v = p[:, :, 0:GK].rearrange("p g (h n) -> p g h n", h=4)
                s = sm[:, n % 4, :].rearrange("p (g h u) -> p g h u", g=2, u=1).broadcast_to([P, 2, 4, KEYS])
                pool.tensor_tensor(v, v, s, ALU.mult).then_inc(probs_ready, 1)

            def add_bias(o, a, bias, ready):
                for t in range(NT):
                    last = pool.tensor_tensor(o[:, t, :], a[:, t, :], bias[:, :], ALU.add)
                last.then_inc(ready, 1)

            def body(it, loop):
                X, Y, Z, Wb = (it.done[s] for s in "XYZW")
                if "X" in it.present:
                    for u in range(8):
                        normalise(it.unit("X", u), u)
                if "Y" in it.present:
                    if "Z" in it.present:
                        pool.wait_ge(bank_free, it.bank("Z", "out", NT - 1)[1] + 1)
                    add_bias(x2b, x2, k["bo"], x2_biased)
                if "X" in it.present:
                    rstd_of(1, X)
                if "Z" in it.present:
                    rstd_of(3, Z)
                if "X" in it.present:
                    pool.wait_ge(ln_done[1], NT * (X + 1))
                    add_bias(x1, x1, k["bf0"], x1_biased)
                if "Z" in it.present:
                    pool.wait_ge(ln_done[3], NT * (Z + 1))
                    add_bias(x3, x3, k["bf1"], x3_biased)
                if "W" in it.present:
                    rstd_of(0, Wb)
                if "Y" in it.present:
                    for u in range(8):
                        normalise(it.unit("Y", u), u)
                if "X" in it.present:
                    rstd_of(2, X)

            walk(pool, body)

        @block.scalar
        def _(act):
            act.wait_ge(prep, PREP)

            def hi_part(it, use, o, **kw):
                bank, n = it.bank(*use)
                act.wait_ge(bank_full, n + 1)
                src = wb[:, bank, :]
                if len(o.shape) == 3:
                    src = src.rearrange("p (c n) -> p c n", c=ND)
                act.activation(o, src, **kw).then_inc(bank_hi, 1)

            def exp(it, stage, u):
                U = it.unit(stage, u)
                act.wait_ge(scores_free, U + 1)
                p = pr[u % 4][:, :, 0:GK]
                f = F_E0 if stage == "X" else F_E1
                act.activation(p, p, ACT.Exp, scale=k["factor"][:, f:f + 1]).then_inc(exp_done, 1)

            def prT_high(it, stage, u):
                U, t, h = it.unit(stage, u), u // 2, u % 2
                act.wait_ge(prT_full, U + 1)
                o = prT[:, 0, 2 * h:2 * h + 2, :, t * P:(t + 1) * P]
                act.activation(o, ptb[0:CH, :, 0:3 * P].rearrange("p g (c n) -> p g c n", c=3), ACT.Copy,
                               scale=PS).then_inc(prT_hi, 1)

            def softmax(it, stage):
                for s in range(10):
                    if s < 8:
                        exp(it, stage, s)
                    if s >= 2:
                        prT_high(it, stage, s - 2)

            def transposed(it, stage):
                for t in range(NT):
                    hi_part(it, (stage, "t", t), xT[:, 0, :, t * P:(t + 1) * P], func=ACT.Copy)

            def diagonal(layer, it, b):
                kd, kb, n, w = (k0d, k0b, 4, H0) if layer == 0 else (k1d, k1b, 2, H1)
                act.wait_ge(k0_loaded if layer == 0 else k1_loaded, (b + 1) * 16)
                for j in range(n):
                    last = act.activation(kb[j * w:(j + 1) * w, :, :, j, :], kd[j * w:(j + 1) * w, :, :, :], ACT.Copy)
                if layer == 0:
                    act.activation(mrow[:, :, :], k["maskall"][:, bass.ds(b, 1), :].broadcast_to([1, 4, KEYS]), ACT.Copy).then_inc(k0_ready, 1)
                else:
                    last.then_inc(k1_ready, 1)

            def body(it, loop):
                if "X" in it.present:
                    softmax(it, "X")
                if "Y" in it.present:
                    diagonal(1, it, it.done["Y"])
                    transposed(it, "Y")
                    for m in range(ND1):
                        hi_part(it, ("Y", "q", m), qc[:, 0, m, :], func=ACT.Identity, bias=k["bq1"][:, m:m + 1])
                if "Z" in it.present:
                    transposed(it, "Z")
                if "Y" in it.present:
                    for s in range(10):
                        if s < 8:
                            exp(it, "Y", s)
                        if s == 3 and "W" in it.present:
                            diagonal(0, it, it.done["W"])
                        if s == 4 and "W" in it.present:
                            transposed(it, "W")
                        if 5 <= s < 9 and "W" in it.present:
                            hi_part(it, ("W", "q", s - 5), q0T[:, 0, s - 5, :], func=ACT.Identity, bias=k["bq0"][:, s - 5:s - 4])
                        if s >= 2:
                            prT_high(it, "Y", s - 2)
                elif "W" in it.present:
                    diagonal(0, it, it.done["W"])
                    transposed(it, "W")
                    for m in range(ND):
                        hi_part(it, ("W", "q", m), q0T[:, 0, m, :], func=ACT.Identity, bias=k["bq0"][:, m:m + 1])
                if "Y" in it.present:
                    for j in range(ND1):
                        hi_part(it, ("Y", "pv", j), qc[:, 0, j, :], func=ACT.Copy)

            walk(act, body)

        @block.vector
        def _(dve):
            step = Chain(dve, dve_step)
            dve.wait_ge(prep, PREP)

            def ln_stats(j, src, tiles):
                for t in tiles:
                    last = dve.bn_stats(stats[:, j, t, :], src[:, t, :])
                if tiles[-1] == NT - 1:
                    step(last)
                    e, o = stats[:, j, :, 1], stats[:, j, :, 4]
                    dve.tensor_tensor(mean[:, j, :], e, o, ALU.add)
                    dve.tensor_tensor(half[:, j, :], e, o, ALU.subtract)
                    step(dve.tensor_tensor(var[:, j, :], stats[:, j, :, 2], stats[:, j, :, 5], ALU.add))
                    dve.tensor_scalar(mean[:, j, :], mean[:, j, :], 0.5, None, ALU.mult)
                    dve.tensor_scalar(var[:, j, :], var[:, j, :], 1.0 / D, EPS, ALU.mult, ALU.add)
                    step(dve.scalar_tensor_tensor(out=half[:, j, :], in0=half[:, j, :], scalar=0.25, in1=half[:, j, :],
                                                  op0=ALU.mult, op1=ALU.mult))
                    dve.tensor_tensor(var[:, j, :], var[:, j, :], half[:, j, :], ALU.add).then_inc(ln_var[j], 1)

            def ln_apply(j, src, tiles, b, signal=True):
                if tiles[0] == 0:
                    dve.wait_ge(ln_rstd[j], b + 1)
                for t in tiles:
                    ins = dve.tensor_scalar(xn[:, t, :], src[:, t, :], mean[:, j, t:t + 1], rstd[:, j, t:t + 1],
                                            ALU.subtract, ALU.mult)
                    if signal:
                        ins.then_inc(ln_done[j], 1)
                    else:
                        step(ins)

            def quantise(t):
                a, c = amax[:, t:t + 1], cscale[:, t:t + 1]
                step(dve.tensor_reduce(a, xn[:, t, :], AX.X, ALU.max, apply_absolute_value=True))
                step(dve.tensor_scalar(a, a, 1e-5, None, ALU.max))
                step(dve.tensor_scalar(c, a, k["factor"][:, F_WSC:F_WSC + 1], None, ALU.mult))
                step(dve.reciprocal(ascale[:, t:t + 1], a))
                step(dve.tensor_scalar(ascale[:, t:t + 1], ascale[:, t:t + 1], 127.0, None, ALU.mult))
                step(dve.tensor_scalar(xn[:, t, :], xn[:, t, :], ascale[:, t:t + 1], MAGIC, ALU.mult, ALU.add))
                dve.tensor_scalar(qi[:, t, :], xn[:, t, :], MAGIC, 127.0, ALU.subtract, ALU.min).then_inc(ln_done[1], 1)

            def lo_part(it, use, lo, hi, bias=0.0):
                bank, n = it.bank(*use)
                dve.wait_ge(bank_hi, it.hi(*use) + 1)
                src = wb[:, bank, :]
                if len(lo.shape) == 3:
                    src = src.rearrange("p (c n) -> p c n", c=ND)
                if isinstance(bias, float):
                    ins = dve.tensor_tensor(lo, src, hi, ALU.subtract)
                else:
                    ins = dve.scalar_tensor_tensor(out=lo, in0=src, scalar=bias, in1=hi, op0=ALU.add, op1=ALU.subtract)
                ins.then_inc(bank_free, 1)

            def add_to(it, use, o, factor, a):
                bank, n = it.bank(*use)
                dve.wait_ge(bank_full, n + 1)
                dve.scalar_tensor_tensor(out=o, in0=wb[:, bank, :], scalar=factor, in1=a,
                                         op0=ALU.mult, op1=ALU.add).then_inc(bank_free, 1)

            def transposed(it, stage):
                for t in range(NT):
                    o = slice(t * P, (t + 1) * P)
                    lo_part(it, (stage, "t", t), xT[:, 1, :, o], xT[:, 0, :, o])

            def four(ap):
                return ap.rearrange("p g (h n) -> p g h n", h=4)

            def maxima(it, stage, u):
                U = it.unit(stage, u)
                dve.wait_ge(scores_full, U + 1)
                s = four(sc[:, u % 2, :, 0:GK])
                m = mx[:, u % 4, :].rearrange("p (g h) -> p g h", g=2)
                step(dve.tensor_reduce(m, s, AX.X, ALU.max))
                m4 = mx[:, u % 4, :].rearrange("p (g h u) -> p g h u", g=2, u=1).broadcast_to([P, 2, 4, KEYS])
                dve.tensor_tensor(four(pr[u % 4][:, :, 0:GK]), s, m4, ALU.subtract).then_inc(scores_free, 1)

            def sums(it, stage, u):
                U = it.unit(stage, u)
                dve.wait_ge(exp_done, U + 1)
                step(dve.tensor_reduce(sm[:, u % 4, :].rearrange("p (g h) -> p g h", g=2), four(pr[u % 4][:, :, 0:GK]), AX.X, ALU.add))
                dve.reciprocal(sm[:, u % 4, :], sm[:, u % 4, :]).then_inc(sums_ready, 1)

            def prT_low(it, stage, u):
                U, t, h = it.unit(stage, u), u // 2, u % 2
                dve.wait_ge(prT_hi, U + 1)
                pair = [prT[:, j, 2 * h:2 * h + 2, :, t * P:(t + 1) * P].rearrange("p g c n -> p (g c) n") for j in range(2)]
                for g in range(2):
                    ins = dve.scalar_tensor_tensor(out=pair[1][:, 3 * g:3 * g + 3], in0=ptb[0:CH, g, 0:3 * P].rearrange("p (c n) -> p c n", c=3),
                                                   scalar=PS, in1=pair[0][:, 3 * g:3 * g + 3], op0=ALU.mult, op1=ALU.subtract)
                ins.then_inc(prT_free, 1)

            f = k["factor"]

            def body(it, loop):
                X, Y, Z, Wb = (it.done[s] for s in "XYZW")
                pres = it.present
                if loop:
                    start = step.count.base + step.count.local
                    step.count.base, step.count.local = start + (it.i - loop[0]) * STEPS_PER_ITERATION, 0
                for s in range(11):
                    if "X" in pres:
                        if s < 8:
                            maxima(it, "X", s)
                        if 1 <= s < 9:
                            sums(it, "X", s - 1)
                    if "Z" in pres and s % 2 == 1 and s < 8:
                        t = s // 2
                        if t == 0:
                            if not (isinstance(Z, int) and Z == 0):
                                dve.wait_ge(stored, 16 * Z)
                            dve.wait_ge(x2_biased, Z + 1)
                        add_to(it, ("Z", "out", t), x3[:, t, :], f[:, F_OUT:F_OUT + 1], x2b[:, t, :])
                    if "X" in pres:
                        if 2 <= s < 10:
                            prT_low(it, "X", s - 2)
                        if s % 2 == 0 and s >= 4:
                            t = s // 2 - 2
                            add_to(it, ("X", "pv", t), x1[:, t, :], f[:, F_PV0:F_PV0 + 1], x_in[:, t, :])
                if "Y" in pres:
                    transposed(it, "Y")
                if "X" in pres:
                    dve.wait_ge(bank_free, it.bank("X", "pv", NT - 1)[1] + 1)
                if "Z" in pres:
                    dve.wait_ge(bank_free, it.bank("Z", "out", NT - 1)[1] + 1)
                for m in range(ND1):
                    if "Y" in pres:
                        lo_part(it, ("Y", "q", m), qc[:, 1, m, :], qc[:, 0, m, :], k["bq1"][:, m:m + 1])
                    if "X" in pres:
                        if m < 2:
                            ln_stats(1, x1, [2 * m, 2 * m + 1])
                        if 2 <= m < 6:
                            ln_apply(1, x1, [m - 2], X, signal=False)
                            quantise(m - 2)
                    if "Z" in pres and m >= 6:
                        ln_stats(3, x3, [2 * m - 12, 2 * m - 11])
                if "X" in pres:
                    for t in range(NT):
                        bank, n = it.bank("X", "t", t)
                        dve.wait_ge(bank_full, n + 1)
                        dve.tensor_copy(qiT[:, :, t * P:(t + 1) * P], wb[:, bank, :].bitcast(BF16)[:, 0:D].rearrange(
                            "p (c n) -> p c n", c=ND)).then_inc(bank_free, 1)
                    dve.wait_ge(x1_biased, X + 1)
                    if "Y" in pres:
                        dve.wait_ge(x2_biased, Y + 1)
                    for t in range(NT):
                        add_to(it, ("X", "f", t), x2[:, t, :], cscale[:, t:t + 1], x1[:, t, :])
                if "Z" in pres:
                    ln_apply(3, x3, list(range(NT)), Z)
                    transposed(it, "Z")
                if "W" in pres:
                    dve.wait_ge(x_loaded, 16 * (Wb + 1))
                if "Z" in pres:
                    dve.wait_ge(x3_biased, Z + 1)
                for s in range(11):
                    if "Y" in pres:
                        if s < 8:
                            maxima(it, "Y", s)
                        if 1 <= s < 9:
                            sums(it, "Y", s - 1)
                    if "Z" in pres and s < 4:
                        add_to(it, ("Z", "f", s), x3[:, s, :], k["inv"][:, S_M:S_M + 1], x3[:, s, :])
                    if "W" in pres:
                        if s < 2:
                            ln_stats(0, x_in, [2 * s, 2 * s + 1])
                        if s == 3:
                            ln_apply(0, x_in, list(range(NT)), Wb)
                        if s == 4:
                            transposed(it, "W")
                        if 5 <= s < 9:
                            lo_part(it, ("W", "q", s - 5), q0T[:, 1, s - 5, :], q0T[:, 0, s - 5, :], k["bq0"][:, s - 5:s - 4])
                    if "Y" in pres and 2 <= s < 10:
                        prT_low(it, "Y", s - 2)
                if "X" in pres:
                    dve.wait_ge(bank_free, it.bank("X", "f", NT - 1)[1] + 1)
                    if "W" in pres:
                        dve.wait_ge(bank_full, it.bank("W", "t", NT - 1)[1] + 1)
                for j in range(ND1):
                    if "Y" in pres:
                        lo_part(it, ("Y", "pv", j), qc[:, 1, j, :], qc[:, 0, j, :])
                    if "X" in pres:
                        if j < 4:
                            ln_stats(2, x2, [j])
                        else:
                            ln_apply(2, x2, [j - 4], X)
                if loop:
                    assert step.count.local == STEPS_PER_ITERATION, step.count.local
                    step.count.base, step.count.local = start + (loop[1] - loop[0]) * STEPS_PER_ITERATION, 0

            walk(dve, body)

        @block.tensor
        def _(pe):
            pe.wait_ge(prep, PREP)
            ident, identb = k["ident"], k["identb"]

            def take(it, *use):
                bank, n = it.bank(*use)
                if not (isinstance(n, int) and n < 2):
                    pe.wait_ge(bank_free, n - 1)
                return bank

            def transpose_tiles(it, stage, j, b):
                for t in range(NT):
                    bank = take(it, stage, "t", t)
                    pe.wait_ge(ln_done[j], NT * b + t + 1)
                    for c in range(ND):
                        if stage == "X":
                            ins = pe.transpose(wb[:, bank, :].bitcast(BF16)[:, c * P:(c + 1) * P], qi[:, t, c * P:(c + 1) * P], identb[:, :])
                        else:
                            ins = pe.transpose(wb[:, bank, c * P:(c + 1) * P], xn[:, t, c * P:(c + 1) * P], ident[:, :])
                    ins.then_inc(bank_full, 1)

            def project(it, stage, m, w, cols, src, what="q"):
                bank = take(it, stage, what, m)
                if m == 0:
                    pe.wait_ge(bank_free, it.bank(stage, "t", NT - 1)[1] + 1)
                for c in range(ND):
                    ins = products(pe, wb[:, bank, :], lambda h: w[:, h, c, m * P:(m + 1) * P], lambda h: src[:, h, c, :],
                                   c == 0, c == ND - 1)
                ins.then_inc(bank_full, 1)

            def scores(it, stage, u):
                U, t, half = it.unit(stage, u), u // 2, u % 2
                if not (isinstance(U, int) and U < 2):
                    pe.wait_ge(scores_free, U - 1)
                tok = slice(t * P, (t + 1) * P)
                for gg in range(2):
                    g = 2 * half + gg
                    if stage == "X":
                        o = sc[:, u % 2, gg, 0:GK]
                        pe.matmul(o, ones[:, :], mrow[:, :, :].rearrange("o h n -> o (h n)"), start=True, stop=False)
                        ins = products(pe, o, lambda h: q0T[:, h, g, tok],
                                       lambda h: k0b[:, h, g, :, :].rearrange("p j n -> p (j n)"), False, True)
                    else:
                        for e in range(2):
                            pair = 2 * g + e
                            ins = products(pe, sc[:, u % 2, gg, e * 2 * KEYS:(e + 1) * 2 * KEYS], lambda h: qc[:, h, pair, tok],
                                           lambda h: k1b[:, h, pair, :, :].rearrange("p j n -> p (j n)"), e == 0, True, skip=True)
                ins.then_inc(scores_full, 1)

            def probs_transpose(it, stage, u):
                U = it.unit(stage, u)
                pe.wait_ge(probs_ready, U + 1)
                if not (isinstance(U, int) and U < 1):
                    pe.wait_ge(prT_free, U)
                for gg in range(2):
                    for c in range(3):
                        ins = pe.transpose(ptb[0:CH, gg, c * P:(c + 1) * P], pr[u % 4][:, gg, c * CH:(c + 1) * CH], ident[:, :])
                ins.then_inc(prT_full, 1)

            def values0(it, t):
                bank = take(it, "X", "pv", t)
                pe.wait_ge(prT_free, it.unit("X", 2 * t + 1) + 1)
                first = True
                for g in range(G):
                    for c in range(3):
                        o = wb[:, bank, g * P + c * H0:g * P + (c + 2) * H0]
                        ins = products(pe, o, lambda h: prT[:, h, g, c, t * P:(t + 1) * P], lambda h: v0b[:, c, :, h, g, :],
                                       first, g == G - 1 and c == 2, skip=True)
                        first = False
                ins.then_inc(bank_full, 1)

            def values1(it, pair):
                bank = take(it, "Y", "pv", pair)
                if pair == 0:
                    pe.wait_ge(prT_free, it.unit("Y", 7) + 1)
                g, e = pair // 2, pair % 2
                for n, (c, slot) in enumerate(((0, 0), (1, 2)) if e == 0 else ((1, 4), (2, 6))):
                    ins = products(pe, wb[:, bank, :], lambda h: v1b[:, h, g, slot:slot + 2, :].rearrange("p s d -> p (s d)"),
                                   lambda h: prT[:, h, g, c, :], n == 0, n == 1)
                ins.then_inc(bank_full, 1)

            def output(it, t):
                bank = take(it, "Z", "out", t)
                for j in range(ND1):
                    ins = products(pe, wb[:, bank, :], lambda h: qc[:, h, j, t * P:(t + 1) * P], lambda h: k["wo"][:, h, j, :],
                                   j == 0, j == ND1 - 1)
                ins.then_inc(bank_full, 1)

            def ffn0(it, t):
                bank = take(it, "X", "f", t)
                if t == 0:
                    pe.wait_ge(bank_free, it.bank("X", "t", NT - 1)[1] + 1)
                for c in range(ND):
                    ins = pe.matmul(wb[:, bank, :], qiT[:, c, t * P:(t + 1) * P], k["tern"][:, c, :], start=c == 0, stop=c == ND - 1)
                ins.then_inc(bank_full, 1)

            def ffn1(it, t):
                bank = take(it, "Z", "f", t)
                if t == 0:
                    pe.wait_ge(bank_free, it.bank("Z", "t", NT - 1)[1] + 1)
                for c in range(ND):
                    ins = products(pe, wb[:, bank, :], lambda h: xT[:, h, c, t * P:(t + 1) * P], lambda h: k["m"][:, h, c, :],
                                   c == 0, c == ND - 1)
                ins.then_inc(bank_full, 1)

            def body(it, loop):
                X, Y, Z, Wb = (it.done[s] for s in "XYZW")
                pres = it.present
                if "X" in pres:
                    pe.wait_ge(k0_ready, X + 1)
                    pe.wait_ge(v0_loaded, 16 * len(PIECES) * (X + 1))
                    pe.wait_ge(bank_free, it.bank(*it.order[0])[1])
                if "Z" in pres and "X" not in pres:
                    pe.wait_ge(bank_free, it.bank(*it.order[0])[1])
                for s in range(11):
                    if "X" in pres and s < 8:
                        scores(it, "X", s)
                    if "Z" in pres and s % 2 == 1 and s < 8:
                        output(it, s // 2)
                    if "X" in pres:
                        if 2 <= s < 10:
                            probs_transpose(it, "X", s - 2)
                        if s % 2 == 0 and s >= 4:
                            values0(it, s // 2 - 2)
                if "Y" in pres:
                    transpose_tiles(it, "Y", 2, Y)
                    for m in range(ND1):
                        project(it, "Y", m, k["wq1"], D1, xT)
                if "X" in pres:
                    transpose_tiles(it, "X", 1, X)
                    for t in range(NT):
                        ffn0(it, t)
                if "Z" in pres:
                    transpose_tiles(it, "Z", 3, Z)
                if "Y" in pres:
                    pe.wait_ge(k1_ready, Y + 1)
                    pe.wait_ge(v1_loaded, 16 * len(PIECES) * (Y + 1))
                for s in range(11):
                    if "Y" in pres and s < 8:
                        if s == 0:
                            pe.wait_ge(bank_free, it.bank("Y", "q", ND1 - 1)[1] + 1)
                        scores(it, "Y", s)
                    if "Z" in pres and s < 4:
                        ffn1(it, s)
                    if "W" in pres:
                        if s == 4:
                            transpose_tiles(it, "W", 0, Wb)
                        if 5 <= s < 9:
                            project(it, "W", s - 5, k["wq0"], D, xT)
                    if "Y" in pres and 2 <= s < 10:
                        probs_transpose(it, "Y", s - 2)
                if "Y" in pres:
                    for j in range(ND1):
                        values1(it, j)

            walk(pe, body)


STEPS_PER_ITERATION = 4 * 3 + 2 * 8 * 2 + NT * 7



def constants():
    n = np.arange(D)
    a = 2.0 * np.pi * ((n[:, None] * n[None, :]) % D) / D
    c, s = np.cos(a), np.sin(a)
    parts = []
    for m in (c, s, -s):
        hi = m.astype(np.float16)
        lo = (m - hi.astype(np.float64)).astype(np.float16)
        for v in (hi, lo):
            parts.append(v.reshape(ND, P, D).transpose(1, 0, 2).reshape(P, ND * D))
    return np.ascontiguousarray(np.concatenate(parts, axis=1)), np.eye(P, dtype=np.float32)


def kernel(**inputs):
    import concourse.bacc as _bacc
    from concourse.bass_utils import run_bass_kernel_spmd as _run

    a = {n: np.asarray(v) for n, v in inputs.items()}

    def blocks(w):
        return w.reshape(-1, P, w.shape[1]).transpose(1, 0, 2)

    def flat(w):
        v = blocks(w)
        return v.reshape(P, -1)

    def by_slot(w, d):
        return w.reshape(w.shape[:-1] + (G, 4, d)).swapaxes(-3, -2).reshape(w.shape)

    dft, eye = constants()
    data = {
        "x": a["x"],
        "ctxT": blocks(a["ctx_1024"].reshape(ROWS, D).T),
        "mask": a["mask_BxS2_ik0"].reshape(1, ROWS),
        "wq0": flat(a["L0_xattn_q_w"].T),
        "bq0": a["L0_xattn_q_b"].reshape(ND, P).T,
        "wk0": blocks(a["L0_xattn_k_w"].T),
        "bk0": a["L0_xattn_k_b"].reshape(ND, P).T,
        "wv0": blocks(by_slot(a["L0_xattn_v_w"].T, H0)),
        "bv0": by_slot(a["L0_xattn_v_b"], H0),
        "packed": a["L0_ffn_packed_weight"].reshape(P, D),
        "wscale": a["L0_ffn_weight_scale"],
        "bf0": a["L0_ffn_bias"],
        "wq1": flat(a["L1_xattn_Wq"].reshape(D, D1)),
        "bq1": a["L1_xattn_bq"].reshape(ND1, P).T,
        "wk1": blocks(a["L1_xattn_Wk"].reshape(D, D1)),
        "bk1": a["L1_xattn_bk"].reshape(ND1, P).T,
        "wv1": blocks(by_slot(a["L1_xattn_Wv"].reshape(D, D1), H1)),
        "bv1": by_slot(a["L1_xattn_bv"].reshape(D1), H1),
        "wo": flat(a["L1_xattn_Wo"].reshape(D1, D)),
        "bo": a["L1_xattn_bo"],
        "wf": np.concatenate([flat(a["L1_ffn_w_freq_real"]), flat(a["L1_ffn_w_freq_imag"])], axis=1),
        "bf1": a["L1_ffn_bias"],
        "dft": dft,
        "eye": eye,
    }
    nc = _bacc.Bacc("TRN2", target_bir_lowering=False, num_devices=1)
    arrays, args = {}, []
    for name, v in data.items():
        v = np.ascontiguousarray(v)
        arrays[f"in_{name}"] = v
        args.append(nc.dram_tensor(f"in_{name}", v.shape, mybir.dt.from_np(v.dtype), kind="ExternalInput").ap())
    out = nc.dram_tensor("out_x", (B, S, D), F32, kind="ExternalOutput").ap()
    program(nc, *args, out)
    r = _run(nc, [arrays], core_ids=[0])
    return r.results[0]["out_x"]
```

```python
import numpy as np
import concourse.bass as bass
from concourse import mybir
from contextlib import ExitStack

F32 = mybir.dt.float32
F16 = mybir.dt.float16
BF16 = mybir.dt.bfloat16
I32 = mybir.dt.int32
ALU = mybir.AluOpType
ACT = mybir.ActivationFunctionType
AX = mybir.AxisListType

P = 128
B, S, D = 8, 512, 512
KEYS = 77
ROWS = B * KEYS
NT = S // P
ND = D // P
H0, H1 = 32, 64
D1 = 16 * H1
ND1 = D1 // P
G = 4
GK = 4 * KEYS
CH = (GK + 2) // 3
GKP = 3 * CH
RC = (ROWS + P - 1) // P
RL = ROWS - (RC - 1) * P
EPS = 1e-5
MAGIC = 12582912.0
PS = 256.0
BIG = -1e30


class Count:

    def __init__(self):
        self.base, self.local = 0, 0

    def next(self):
        self.local += 1
        return self.base + self.local


A_USES = [[("Y", "t", 0)], [("Z", "out", 0), ("Y", "t", 1)], [("Y", "t", 2)], [("Z", "out", 1), ("Y", "t", 3)],
          [("X", "pv", 0)], [("Z", "out", 2)], [("X", "pv", 1)], [("Z", "out", 3)],
          [("Y", "q", 0), ("X", "pv", 2)], [("Y", "q", 1)]]
M_USES = [("X", "pv", 3), ("Y", "q", 2), ("X", "t", 0), ("Y", "q", 3), ("X", "t", 1), ("Y", "q", 4)]
B_USES = [[("Y", "q", 5), ("X", "t", 2)], [("Y", "q", 6), ("X", "t", 3)], [("Y", "q", 7), ("X", "f", 0), ("X", "f", 1)],
          [("X", "f", 2), ("X", "f", 3), ("Z", "t", 0)], [("Z", "t", 1), ("Z", "f", 0)],
          [("Z", "t", 2), ("Z", "f", 1), ("Z", "t", 3)], [("Y", "pv", 0), ("Z", "f", 2)],
          [("W", "t", 0), ("Z", "f", 3), ("W", "t", 1), ("Y", "pv", 1)],
          [("W", "t", 2), ("Y", "pv", 2), ("W", "t", 3), ("Y", "pv", 3)], [("W", "q", 0)]]
C_USES = [("Y", "pv", 4), ("W", "q", 1), ("Y", "pv", 5), ("W", "q", 2), ("Y", "pv", 6), ("W", "q", 3), ("Y", "pv", 7)]
BANK_ORDER = sum(A_USES, []) + M_USES + sum(B_USES, []) + C_USES
AFTER_W = len(BANK_ORDER) - 1 - BANK_ORDER.index(("W", "q", 3))
HI_ORDER = [u for u in BANK_ORDER if u[:2] in (("Y", "t"), ("Y", "q"), ("Z", "t"), ("W", "t"), ("W", "q"), ("Y", "pv"))]
STAGES = "XYZW"
PER = {s: sum(u[0] == s for u in BANK_ORDER) for s in STAGES}
PER_HI = {s: sum(u[0] == s for u in HI_ORDER) for s in STAGES}


class Iteration:

    def __init__(self, i, present):
        self.i, self.present = i, present
        lag = {"W": -1, "X": 0, "Y": 1, "Z": 2}
        self.done = {s: (i - lag[s] if s in present else (0 if isinstance(i, int) and i < lag[s] else B)) for s in STAGES}
        self.order = [u for u in BANK_ORDER if u[0] in present]
        self.hi_order = [u for u in HI_ORDER if u[0] in present]

    def uses(self, listed):
        return [u for u in listed if u[0] in self.present]

    def total(self, per):
        out = 0
        for s in STAGES:
            if per.get(s):
                out = out + self.done[s] * per[s]
        return out

    def bank(self, *use):
        k = self.order.index(use)
        return k % 2, self.total(PER) + k

    def hi(self, *use):
        return self.total(PER_HI) + self.hi_order.index(use)

    def unit(self, stage, u):
        k = u + (8 if stage == "Y" and "X" in self.present else 0)
        return self.total({"X": 8, "Y": 8}) + k


def plan():
    return ([(-1, "W"), (0, "WX"), (1, "WXY")], (2, B - 1, "WXYZ"), [(B - 1, "XYZ"), (B, "YZ"), (B + 1, "Z")])


def walk(eng, body):
    first, (a, b, stages), last = plan()
    for i, p in first:
        body(Iteration(i, p), None)
    with eng.Fori(a, b) as i:
        body(Iteration(i, stages), (a, b))
    for i, p in last:
        body(Iteration(i, p), None)


def products(pe, out, lhs, rhs, start, stop, skip=False):
    kw = dict(skip_group_check=True) if skip else {}
    pe.matmul(out, lhs(0), rhs(0), start=start, stop=False, **kw)
    pe.matmul(out, lhs(0), rhs(1), start=False, stop=False, **kw)
    return pe.matmul(out, lhs(1), rhs(0), start=False, stop=stop, **kw)


def program(nc, x, ctxT, mask, wq0, bq0, wk0, bk0, wv0, bv0, packed, wscale, bf0,
            wq1, bq1, wk1, bk1, wv1, bv1, wo, bo, wf, bf1, dft, eye, out):
    scr_k0 = nc.dram_tensor("scr_k0", (P, B, 2 * ND * KEYS), F16, kind="Internal").ap()
    scr_k1 = nc.dram_tensor("scr_k1", (P, B, 2 * ND1 * KEYS), F16, kind="Internal").ap()
    scr_v0 = nc.dram_tensor("scr_v0", (RC * P, 4, 2 * G * H0), F16, kind="Internal").ap()
    scr_v1 = nc.dram_tensor("scr_v1", (RC * P, 4, 2 * G * H1), F16, kind="Internal").ap()
    keep = ExitStack()
    with keep:
        def sb(stack, name, shape, dt):
            return stack.enter_context(nc.sbuf_tensor(name, shape, dt))

        k = {}
        k["wq0"] = sb(keep, "wq0_hl", [P, 2, ND, D], F16)
        k["wq1"] = sb(keep, "wq1_hl", [P, 2, ND, D1], F16)
        k["wo"] = sb(keep, "wo_hl", [P, 2, ND1, D], F16)
        k["m"] = sb(keep, "m_hl", [P, 2, ND, D], F16)
        k["tern"] = sb(keep, "tern", [P, ND, D], BF16)
        k["ident"] = sb(keep, "ident", [P, P], F32)
        k["identb"] = sb(keep, "identb", [P, P], BF16)
        k["bq0"] = sb(keep, "bq0_s", [P, ND], F32)
        k["bq1"] = sb(keep, "bq1_s", [P, ND1], F32)
        k["bo"] = sb(keep, "bo_b", [P, D], F32)
        k["bf0"] = sb(keep, "bf0_b", [P, D], F32)
        k["bf1"] = sb(keep, "bf1_b", [P, D], F32)
        k["maskall"] = sb(keep, "maskall", [1, B, KEYS], BF16)
        k["scale"] = sb(keep, "scale", [P, 16], F32)
        k["inv"] = sb(keep, "inv", [P, 16], F32)
        k["factor"] = sb(keep, "factor", [P, 8], F32)
        setup_context(nc, k, ctxT, wk0, bk0, wv0, bv0, wk1, bk1, wv1, bv1, scr_k0, scr_k1, scr_v0, scr_v1)
        setup_weights(nc, k, mask, wq0, bq0, packed, wscale, bf0, wq1, bq1, wo, bo, wf, bf1, dft, eye)
        layers(nc, k, x, scr_k0, scr_k1, scr_v0, scr_v1, out)


S_CTX, S_WK0, S_WV0, S_WK1A, S_WK1B, S_WV1A, S_WV1B, S_K0, S_V0, S_K1, S_V1, S_WF, S_WQ0, S_WQ1, S_WO, S_M = range(16)
F_E0, F_E1, F_PV0, F_OUT, F_WSC, F_A, F_KV = range(7)


class Chain:

    def __init__(self, dve, sem):
        self.dve, self.sem, self.count = dve, sem, Count()

    def __call__(self, ins):
        v = self.count.next()
        ins.then_inc(self.sem, 1)
        self.dve.wait_ge(self.sem, v)


def find_scale(dve, step, k, slot, absmax, allmax, absmax_ready, allmax_ready, n):
    dve.wait_ge(allmax_ready, n + 1)
    a = allmax[:, slot:slot + 1]
    step(dve.tensor_scalar(a, a, 1e-30, 1e37, ALU.max, ALU.min))
    step(dve.tensor_scalar(a.bitcast(I32), a.bitcast(I32), 0x7F800000, None, ALU.bitwise_and))
    step(dve.reciprocal(k["scale"][:, slot:slot + 1], a))
    step(dve.tensor_scalar(k["scale"][:, slot:slot + 1], k["scale"][:, slot:slot + 1], 32.0, None, ALU.mult))
    step(dve.tensor_scalar(k["inv"][:, slot:slot + 1], a, 1.0 / 32.0, None, ALU.mult))


def setup_context(nc, k, ctxT, wk0, bk0, wv0, bv0, wk1, bk1, wv1, bv1, scr_k0, scr_k1, scr_v0, scr_v1):
    here = ExitStack()
    with here:
        def sb(name, shape, dt):
            return here.enter_context(nc.sbuf_tensor(name, shape, dt))

        def sem(name):
            return here.enter_context(nc.semaphore(name))

        stage = sb("a_stage", [P, 2, ND, ROWS], F32)
        ctx_hl = sb("a_ctx_hl", [P, 2, ND, ROWS], F16)
        w_hl = sb("a_w_hl", [P, 2, 2, ND, D], F16)
        kf = sb("a_kf", [P, ND1, ROWS], F32)
        vf = sb("a_vf", [P, RC, D1], F32)
        ks = sb("a_ks", [P, B * 2 * ND1 * KEYS], F16)
        vs = sb("a_vs", [P, RC * 2 * D1], F16)
        kb0, kb1 = sb("a_kb0", [P, ND], F32), sb("a_kb1", [P, ND1], F32)
        vb0, vb1 = sb("a_vb0", [P, D], F32), sb("a_vb1", [P, D1], F32)
        absmax, allmax = sb("a_absmax", [P, 16], F32), sb("a_allmax", [P, 16], F32)
        kbank = here.enter_context(nc.psum_tensor("a_kbank", [P, 4, D], F32))
        vbank = here.enter_context(nc.psum_tensor("a_vbank", [P, 4, D], F32))

        loaded = [sem(f"a_loaded{i}") for i in range(2)]
        bias_in, dve_step, absmax_ready, allmax_ready = sem("a_bias_in"), sem("a_dve_step"), sem("a_absmax_ready"), sem("a_allmax_ready")
        scale_ready, hi_done, lo_done = sem("a_scale_ready"), sem("a_hi_done"), sem("a_lo_done")
        k_full, k_free, v_full, v_free = sem("a_k_full"), sem("a_k_free"), sem("a_v_full"), sem("a_v_free")
        kout, vout = sem("a_kout"), sem("a_vout")

        W = [(S_CTX, ROWS, ctxT), (S_WK0, D, wk0), (S_WV0, D, wv0), (S_WK1A, D, wk1[:, :, 0:D]), (S_WK1B, D, wk1[:, :, D:D1]),
             (S_WV1A, D, wv1[:, :, 0:D]), (S_WV1B, D, wv1[:, :, D:D1])]
        SPLITS = [0, 1, 2, 3, "K0", "V0", 4, 5, "K1", 6, "V1"]
        nth = {s: n for n, s in enumerate(SPLITS)}
        K0N, K1N = 2 * ND, 2 * ND1
        last_use = {1: ("k", K0N), 2: ("v", RC), 3: ("k", K0N + K1N // 2), 4: ("k", K0N + K1N)}

        block = here.enter_context(nc.Block())

        def dst(s):
            if s == 0:
                return [ctx_hl[:, h, :, :] for h in range(2)], stage[:, 0, :, :], S_CTX
            if isinstance(s, int):
                return [w_hl[:, (s - 1) % 2, h, :, :] for h in range(2)], stage[:, s % 2, :, 0:D], W[s][0]
            if s[0] == "K":
                m = ND if s == "K0" else ND1
                o = ks[:, 0:B * 2 * m * KEYS].rearrange("p (b h m k) -> p h m b k", b=B, h=2, m=m)
                return [o[:, h] for h in range(2)], kf[:, 0:m, :].rearrange("p m (b k) -> p m b k", b=B), S_K0 if s == "K0" else S_K1
            n = D if s == "V0" else D1
            o = vs[:, 0:RC * 2 * n].rearrange("p (r j h d) -> p h (r j) d", r=RC, j=4, h=2)
            i = vf[:, :, :].rearrange("p r n -> p (r n)")[:, 0:RC * n].rearrange("p (rj d) -> p rj d", d=n // 4)
            return [o[:, h] for h in range(2)], i, S_V0 if s == "V0" else S_V1

        @block.sync
        def _(sp):
            for n, (slot, width, src) in enumerate(W):
                if n >= 2:
                    sp.wait_ge(lo_done, nth[n - 2] + 1)
                sp.dma_start(stage[:, n % 2, :, 0:width], src).then_inc(loaded[n % 2], 16)
            sp.wait_ge(kout, 32)
            sp.wait_ge(vout, 32)

        @block.gpsimd
        def _(pool):
            pool.dma_start(kb0[:, :], bk0).then_inc(bias_in, 16)
            pool.dma_start(kb1[:, :], bk1).then_inc(bias_in, 16)
            pool.dma_start(vb0[:, :], bv0.partition_broadcast(P)).then_inc(bias_in, 16)
            pool.dma_start(vb1[:, :], bv1.partition_broadcast(P)).then_inc(bias_in, 16)
            for n, s in enumerate(SPLITS):
                slot = dst(s)[2]
                pool.wait_ge(absmax_ready, n + 1)
                pool.partition_all_reduce(allmax[:, slot:slot + 1], absmax[:, slot:slot + 1], P,
                                          bass.bass_isa.ReduceOp.absmax).then_inc(allmax_ready, 1)
                if s in ("K0", "V0", "K1", "V1"):
                    pool.wait_ge(lo_done, n + 1)
                if s == "K0":
                    pool.dma_start(scr_k0.rearrange("p b n -> p (b n)"), ks[:, 0:B * 2 * ND * KEYS]).then_inc(kout, 16)
                if s == "K1":
                    pool.dma_start(scr_k1.rearrange("p b n -> p (b n)"), ks[:, :]).then_inc(kout, 16)
                if s == "V0":
                    pool.dma_start(scr_v0.rearrange("(r p) j n -> p r (j n)", p=P),
                                   vs[:, 0:RC * 2 * D].rearrange("p (r n) -> p r n", r=RC)).then_inc(vout, 16)
                if s == "V1":
                    pool.dma_start(scr_v1.rearrange("(r p) j n -> p r (j n)", p=P),
                                   vs[:, :].rearrange("p (r n) -> p r n", r=RC)).then_inc(vout, 16)

        @block.vector
        def _(dve):
            step = Chain(dve, dve_step)
            step(dve.memset(vf[:, :, :], 0.0))

            def split(s):
                n = nth[s]
                (hi, lo), src, slot = dst(s)
                if isinstance(s, int):
                    dve.wait_ge(loaded[s % 2], 16 * (s // 2 + 1))
                elif s[0] == "K":
                    dve.wait_ge(k_free, K0N if s == "K0" else K0N + K1N)
                dve.tensor_reduce(absmax[:, slot:slot + 1], src, AX.XYZ if len(src.shape) == 4 else AX.XY, ALU.max,
                                  apply_absolute_value=True).then_inc(absmax_ready, 1)
                find_scale(dve, step, k, slot, absmax, allmax, absmax_ready, allmax_ready, n)
                dve.tensor_copy(allmax[:, slot:slot + 1], k["scale"][:, slot:slot + 1]).then_inc(scale_ready, 1)
                dve.wait_ge(hi_done, n + 1)
                if len(src.shape) == 4:
                    for m in range(src.shape[1]):
                        ins = dve.scalar_tensor_tensor(out=lo[:, m], in0=src[:, m], scalar=k["scale"][:, slot:slot + 1],
                                                       in1=hi[:, m], op0=ALU.mult, op1=ALU.subtract)
                else:
                    ins = dve.scalar_tensor_tensor(out=lo, in0=src, scalar=k["scale"][:, slot:slot + 1], in1=hi,
                                                   op0=ALU.mult, op1=ALU.subtract)
                ins.then_inc(lo_done, 1)

            def v_evacuate(w, slot, bias, n0, col, width):
                step(dve.tensor_tensor(k["factor"][:, F_KV:F_KV + 1], k["inv"][:, S_CTX:S_CTX + 1],
                                       k["inv"][:, slot:slot + 1], ALU.mult))
                flat = vf[:, :, :].rearrange("p r n -> p (r n)")
                for r in range(RC):
                    rows = P if r < RC - 1 else RL
                    dve.wait_ge(v_full, n0 + r + 1)
                    dve.scalar_tensor_tensor(out=flat[0:rows, r * width + col:r * width + col + D], in0=vbank[0:rows, (n0 + r) % 4, :],
                                             scalar=k["factor"][0:rows, F_KV:F_KV + 1], in1=bias[0:rows, :],
                                             op0=ALU.mult, op1=ALU.add).then_inc(v_free, 1)
                dve.wait_ge(v_free, n0 + RC)

            for s in (0, 1, 2, 3):
                split(s)
            split("K0")
            dve.wait_ge(bias_in, 64)
            v_evacuate(2, S_WV0, vb0, 0, 0, D)
            split("V0")
            dve.wait_ge(lo_done, nth["V0"] + 1)
            step(dve.memset(vf[:, :, :], 0.0))
            split(4)
            split(5)
            split("K1")
            split(6)
            v_evacuate(5, S_WV1A, vb1[:, 0:D], RC, 0, D1)
            v_evacuate(6, S_WV1B, vb1[:, D:D1], 2 * RC, D, D1)
            split("V1")

        @block.scalar
        def _(act):
            fac = sb("a_kfactor", [P, 4], F32)

            def hi_part(s):
                n = nth[s]
                (hi, lo), src, slot = dst(s)
                act.wait_ge(scale_ready, n + 1)
                if s in last_use:
                    pass
                if isinstance(s, int) and s - 2 in last_use:
                    kind, v = last_use[s - 2]
                    act.wait_ge(k_full if kind == "k" else v_full, v)
                if s == "K1":
                    act.wait_ge(kout, 16)
                if s == "V1":
                    act.wait_ge(vout, 16)
                if len(src.shape) == 4:
                    for m in range(src.shape[1]):
                        ins = act.activation(hi[:, m], src[:, m], ACT.Copy, scale=k["scale"][:, slot:slot + 1])
                else:
                    ins = act.activation(hi, src, ACT.Copy, scale=k["scale"][:, slot:slot + 1])
                ins.then_inc(hi_done, 1)

            kfac = sem("a_kfac")

            def k_evacuate(n0, m0, slot, bias, j):
                act.activation(fac[:, j:j + 1], k["inv"][:, S_CTX:S_CTX + 1], ACT.Copy,
                               scale=k["inv"][:, slot:slot + 1]).then_inc(kfac, 1)
                act.wait_ge(kfac, j + 1)
                for m in range(ND):
                    for half in range(2):
                        n = n0 + 2 * m + half
                        act.wait_ge(k_full, n + 1)
                        act.activation(kf[:, m0 + m, half * ROWS // 2:(half + 1) * ROWS // 2], kbank[:, n % 4, 0:ROWS // 2],
                                       ACT.Identity, bias=bias[:, m0 + m:m0 + m + 1], scale=fac[:, j:j + 1]).then_inc(k_free, 1)

            for s in (0, 1, 2):
                hi_part(s)
            act.wait_ge(bias_in, 64)
            k_evacuate(0, 0, S_WK0, kb0, 0)
            for s in (3, "K0"):
                hi_part(s)
            hi_part("V0")
            act.wait_ge(lo_done, nth["K0"] + 1)
            k_evacuate(K0N, 0, S_WK1A, kb1, 1)
            hi_part(4)
            k_evacuate(2 * K0N, ND, S_WK1B, kb1, 2)
            for s in (5, "K1", 6, "V1"):
                hi_part(s)

        @block.tensor
        def _(pe):
            def keys(w, n0):
                pe.wait_ge(lo_done, nth[w] + 1)
                for m in range(ND):
                    for half in range(2):
                        n = n0 + 2 * m + half
                        if n >= 4:
                            pe.wait_ge(k_free, n - 3)
                        for c in range(ND):
                            ins = products(pe, kbank[:, n % 4, 0:ROWS // 2],
                                           lambda h: w_hl[:, (w - 1) % 2, h, c, m * P:(m + 1) * P],
                                           lambda h: ctx_hl[:, h, c, half * ROWS // 2:(half + 1) * ROWS // 2], c == 0, c == ND - 1)
                        ins.then_inc(k_full, 1)

            def values(w, n0):
                pe.wait_ge(lo_done, nth[w] + 1)
                for r in range(RC):
                    rows, n = (P if r < RC - 1 else RL), n0 + r
                    if n >= 4:
                        pe.wait_ge(v_free, n - 3)
                    for c in range(ND):
                        ins = products(pe, vbank[0:rows, n % 4, :], lambda h: ctx_hl[:, h, c, r * P:r * P + rows],
                                       lambda h: w_hl[:, (w - 1) % 2, h, c, :], c == 0, c == ND - 1)
                    ins.then_inc(v_full, 1)

            pe.wait_ge(lo_done, 1)
            keys(1, 0)
            values(2, 0)
            keys(3, K0N)
            keys(4, 2 * K0N)
            values(5, RC)
            values(6, 2 * RC)


def setup_weights(nc, k, mask, wq0, bq0, packed, wscale, bf0, wq1, bq1, wo, bo, wf, bf1, dft, eye):
    here = ExitStack()
    with here:
        def sb(name, shape, dt):
            return here.enter_context(nc.sbuf_tensor(name, shape, dt))

        def sem(name):
            return here.enter_context(nc.semaphore(name))

        stage = sb("b_stage", [P, 2, 8 * D], F32)
        dft_hl = sb("b_dft", [P, 3, 2, ND, D], F16)
        wf_hl = sb("b_wf_hl", [P, 2, 2 * ND, D], F16)
        a_hl = sb("b_a_hl", [P, 2, 2, ND, D], F16)
        mf = sb("b_mf", [P, ND, D], F32)
        pk, enc = sb("b_pk", [P, D], I32), sb("b_enc", [P, 4, D], I32)
        ternrow = sb("b_ternrow", [P, 4, D], BF16)
        absmax, allmax = sb("b_absmax", [P, 16], F32), sb("b_allmax", [P, 16], F32)
        bmax = sb("b_bmax", [P, 2], F32)
        mraw, mkf = sb("b_mraw", [1, B, KEYS], I32), sb("b_mkf", [1, B, KEYS], F32)
        nval = sb("b_nval", [1, B], F32)
        bank = here.enter_context(nc.psum_tensor("b_bank", [P, 4, D], F32))
        tbank = here.enter_context(nc.psum_tensor("b_tbank", [P, 4, 2 * D], BF16))

        loaded = [sem(f"b_loaded{i}") for i in range(2)]
        small_in, dft_in, dve_step = sem("b_small_in"), sem("b_dft_in"), sem("b_dve_step")
        absmax_ready, allmax_ready, scale_ready = sem("b_absmax_ready"), sem("b_allmax_ready"), sem("b_scale_ready")
        hi_done, lo_done = sem("b_hi_done"), sem("b_lo_done")
        full, a_hi, free = sem("b_full"), sem("b_a_hi"), sem("b_free")
        tern_rows, tern_full = sem("b_tern_rows"), sem("b_tern_full")

        W = [(S_WF, wf_hl, wf, 2 * ND * D), (S_WQ0, k["wq0"], wq0, ND * D), (S_WQ1, k["wq1"], wq1, ND * D1),
             (S_WO, k["wo"], wo, ND1 * D)]
        block = here.enter_context(nc.Block())

        def flat(t, h):
            return t[:, h, :, :].rearrange("p a n -> p (a n)")

        @block.sync
        def _(sp):
            for n, (slot, _, src, width) in enumerate(W):
                if n == 1:
                    sp.dma_start(dft_hl[:, :, :, :, :].rearrange("p a h c n -> p (a h c n)"), dft).then_inc(dft_in, 16)
                if n >= 2:
                    sp.wait_ge(lo_done, n - 1)
                sp.dma_start(stage[:, n % 2, 0:width], src).then_inc(loaded[n % 2], 16)

        @block.gpsimd
        def _(pool):
            pool.dma_start(pk[:, :], packed).then_inc(small_in, 16)
            pool.dma_start(k["ident"][:, :], eye).then_inc(small_in, 16)
            pool.dma_start(k["bq0"][:, :], bq0).then_inc(small_in, 16)
            pool.dma_start(k["bq1"][:, :], bq1).then_inc(small_in, 16)
            pool.dma_start(k["bo"][:, :], bo.partition_broadcast(P)).then_inc(small_in, 16)
            pool.dma_start(k["bf0"][:, :], bf0.partition_broadcast(P)).then_inc(small_in, 16)
            pool.dma_start(k["bf1"][:, :], bf1.partition_broadcast(P)).then_inc(small_in, 16)
            pool.dma_start(k["factor"][:, F_WSC:F_WSC + 1], wscale.partition_broadcast(P)).then_inc(small_in, 16)
            pool.dma_start(mraw[:, :, :].rearrange("o b n -> o (b n)"), mask).then_inc(small_in, 16)
            for n, slot in enumerate((S_WF, S_WQ0, S_WQ1, S_WO, S_M)):
                pool.wait_ge(absmax_ready, n + 1)
                pool.partition_all_reduce(allmax[:, slot:slot + 1], absmax[:, slot:slot + 1], P,
                                          bass.bass_isa.ReduceOp.absmax).then_inc(allmax_ready, 1)

        @block.vector
        def _(dve):
            step = Chain(dve, dve_step)

            def split(n, slot, src, out):
                am = absmax[:, slot:slot + 1]
                if slot in (S_WQ0, S_WQ1):
                    b, j = (k["bq0"], 0) if slot == S_WQ0 else (k["bq1"], 1)
                    step(dve.tensor_reduce(bmax[:, j:j + 1], b[:, :], AX.X, ALU.max, apply_absolute_value=True))
                    step(dve.tensor_reduce(am, src, AX.X, ALU.max, apply_absolute_value=True))
                    dve.scalar_tensor_tensor(out=am, in0=bmax[:, j:j + 1], scalar=1.0 / 256.0, in1=am,
                                             op0=ALU.mult, op1=ALU.max).then_inc(absmax_ready, 1)
                else:
                    dve.tensor_reduce(am, src, AX.X, ALU.max, apply_absolute_value=True).then_inc(absmax_ready, 1)
                find_scale(dve, step, k, slot, absmax, allmax, absmax_ready, allmax_ready, n)
                sc = k["scale"][:, slot:slot + 1]
                dve.tensor_copy(allmax[:, slot:slot + 1], sc).then_inc(scale_ready, 1)
                if slot in (S_WQ0, S_WQ1):
                    step(dve.tensor_scalar(b[:, :], b[:, :], sc, None, ALU.mult))
                dve.wait_ge(hi_done, n + 1)
                dve.scalar_tensor_tensor(out=flat(out, 1), in0=src, scalar=sc, in1=flat(out, 0),
                                         op0=ALU.mult, op1=ALU.subtract).then_inc(lo_done, 1)

            dve.wait_ge(loaded[0], 16)
            split(0, S_WF, stage[:, 0, :], wf_hl)
            dve.wait_ge(small_in, 144)
            for s in range(4):
                step(dve.tensor_scalar(enc[:, s, :], pk[:, :], 2 * s, 3, ALU.logical_shift_right, ALU.bitwise_and))
            step(dve.tensor_copy(k["identb"][:, :], k["ident"][:, :]))
            dve.tensor_scalar(ternrow[:, :, :], enc[:, :, :], -1.0, None, ALU.add).then_inc(tern_rows, 1)
            step(dve.tensor_scalar(mkf[:, :, :], mraw[:, :, :], 0.0, None, ALU.is_gt))
            step(dve.tensor_reduce(nval[:, :], mkf[:, :, :], AX.X, ALU.add))
            step(dve.tensor_scalar(nval[:, :], nval[:, :], -1.0, float(KEYS), ALU.mult, ALU.add))
            step(dve.reciprocal(nval[:, :], nval[:, :]))
            step(dve.tensor_scalar(nval[:, :], nval[:, :], 0.0, None, ALU.mult))
            step(dve.tensor_scalar(mkf[:, :, :], mkf[:, :, :], BIG, None, ALU.mult))
            step(dve.tensor_tensor(k["maskall"][:, :, :], mkf[:, :, :],
                                   nval[:, :].rearrange("o (b u) -> o b u", u=1).broadcast_to([1, B, KEYS]), ALU.add))
            dve.wait_ge(loaded[1], 16)
            split(1, S_WQ0, stage[:, 1, 0:ND * D], k["wq0"])
            for c in range(ND):
                dve.wait_ge(tern_full, c + 1)
                dve.tensor_copy(k["tern"][:, c, :], tbank[:, c, 0:D])
            for j in range(2 * ND):
                dve.wait_ge(a_hi, j + 1)
                dve.scalar_tensor_tensor(out=a_hl[:, j // ND, 1, j % ND, :], in0=bank[:, j % 4, :], scalar=0.25,
                                         in1=a_hl[:, j // ND, 0, j % ND, :], op0=ALU.mult, op1=ALU.subtract).then_inc(free, 1)
            dve.wait_ge(loaded[0], 32)
            split(2, S_WQ1, stage[:, 0, :], k["wq1"])
            step(dve.tensor_scalar(k["factor"][:, F_A:F_A + 1], k["inv"][:, S_WF:S_WF + 1], 4.0 / D, None, ALU.mult))
            for j in range(ND):
                dve.wait_ge(full, 2 * ND + j + 1)
                dve.tensor_scalar(mf[:, j, :], bank[:, j % 4, :], k["factor"][:, F_A:F_A + 1], None, ALU.mult).then_inc(free, 1)
            dve.wait_ge(loaded[1], 32)
            split(3, S_WO, stage[:, 1, :], k["wo"])
            dve.wait_ge(free, 3 * ND)
            split(4, S_M, mf[:, :, :].rearrange("p a n -> p (a n)"), k["m"])
            def factor(slot, a, b, c):
                f = k["factor"][:, slot:slot + 1]
                if b is None:
                    step(dve.tensor_scalar(f, k["inv"][:, a:a + 1], c, None, ALU.mult))
                else:
                    step(dve.tensor_scalar(f, k["inv"][:, a:a + 1], k["inv"][:, b:b + 1], None, ALU.mult))
                    step(dve.tensor_scalar(f, f, c, None, ALU.mult))
            factor(F_E0, S_WQ0, S_K0, float(H0) ** -0.5)
            factor(F_E1, S_WQ1, S_K1, float(H1) ** -0.5)
            factor(F_PV0, S_V0, None, 1.0 / PS)
            factor(F_OUT, S_V1, S_WO, 1.0 / PS)
            f = k["factor"][:, F_WSC:F_WSC + 1]
            step(dve.tensor_scalar(f, f, 1.0 / 127.0, None, ALU.mult))

        @block.scalar
        def _(act):
            def hi_part(n, slot, src, out):
                act.wait_ge(scale_ready, n + 1)
                act.activation(flat(out, 0), src, ACT.Copy, scale=k["scale"][:, slot:slot + 1]).then_inc(hi_done, 1)

            hi_part(0, S_WF, stage[:, 0, :], wf_hl)
            hi_part(1, S_WQ0, stage[:, 1, 0:ND * D], k["wq0"])
            for j in range(2 * ND):
                act.wait_ge(full, j + 1)
                act.activation(a_hl[:, j // ND, 0, j % ND, :], bank[:, j % 4, :], ACT.Copy, scale=0.25).then_inc(a_hi, 1)
            hi_part(2, S_WQ1, stage[:, 0, :], k["wq1"])
            hi_part(3, S_WO, stage[:, 1, :], k["wo"])
            hi_part(4, S_M, mf[:, :, :].rearrange("p a n -> p (a n)"), k["m"])

        @block.tensor
        def _(pe):
            pe.wait_ge(tern_rows, 1)
            for c in range(ND):
                for s in range(4):
                    ins = pe.transpose(tbank[:, c, s * P:(s + 1) * P], ternrow[:, s, c * P:(c + 1) * P], k["identb"][:, :])
                ins.then_inc(tern_full, 1)
            pe.wait_ge(lo_done, 1)
            pe.wait_ge(dft_in, 16)
            COS, SIN, NSIN = range(3)
            for j in range(2 * ND):
                part, o = j // ND, j % ND
                if j >= 4:
                    pe.wait_ge(free, j - 3)
                terms = ((0, COS), (1, SIN)) if part == 0 else ((1, COS), (0, NSIN))
                for n, (w, f) in enumerate(terms):
                    for c in range(ND):
                        ins = products(pe, bank[:, j % 4, :], lambda h: wf_hl[:, h, w * ND + c, o * P:(o + 1) * P],
                                       lambda h: dft_hl[:, f, h, c, :], n == 0 and c == 0, n == 1 and c == ND - 1)
                ins.then_inc(full, 1)
            for j in range(ND):
                n = 2 * ND + j
                pe.wait_ge(free, n - 3 if j else 2 * ND)
                for part, f in ((0, COS), (1, NSIN)):
                    for c in range(ND):
                        ins = products(pe, bank[:, n % 4, :], lambda h: a_hl[:, part, h, c, j * P:(j + 1) * P],
                                       lambda h: dft_hl[:, f, h, c, :], part == 0 and c == 0, part == 1 and c == ND - 1)
                ins.then_inc(full, 1)


def layers(nc, k, x, scr_k0, scr_k1, scr_v0, scr_v1, out):
    here = ExitStack()
    with here:
        def sb(name, shape, dt):
            return here.enter_context(nc.sbuf_tensor(name, shape, dt))

        def sem(name):
            return here.enter_context(nc.semaphore(name))

        x1 = sb("x1", [P, NT, D], F32)
        x2 = sb("x2", [P, NT, D], F32)
        x2b = sb("x2b", [P, NT, D], F32)
        x3 = sb("x3", [P, NT, D], F32)
        xn = sb("xn", [P, NT, D], F32)
        qi = sb("qi", [P, NT, D], BF16)
        xT = sb("xT", [P, 2, ND, S], F16)
        xT4 = sb("xT4", [P, 2, ND, S], F16)
        qiT = sb("qiT", [P, ND, S], BF16)
        q0T = sb("q0T", [P, 2, ND, S], F16)
        qc = sb("qc", [P, 2, ND1, S], F16)
        prT = sb("prT", [CH, 2, G, 3, S], F16)
        pr = [sb(f"pr{i}", [P, 2, GKP], F32) for i in range(4)]
        kd = sb("kd", [P, 2, ND1, KEYS], F16)
        k0d, k1d = kd[:, 0, :, :].rearrange("p (h m) n -> p h m n", h=2), kd[:, :, :, :]
        k0b = sb("k0b", [P, 2, ND, 4, KEYS], F16)
        k1b = sb("k1b", [P, 2, ND1, 2, KEYS], F16)
        v0b = sb("v0b", [CH, 3, 2, 2, G, H0], F16)
        v1b = sb("v1b", [CH, 2, G, 8, H1], F16)
        mrow = sb("mrow", [1, 4, KEYS], BF16)
        ones = sb("ones", [1, P], BF16)
        mx, sm = sb("mx", [P, 4, 8], F32), sb("sm", [P, 4, 8], F32)
        stats = sb("stats", [P, 4, NT, 6], F32)
        mean, half = sb("mean", [P, 4, NT], F32), sb("half", [P, 4, NT], F32)
        var, rstd = sb("var", [P, 4, NT], F32), sb("rstd", [P, 4, NT], F32)
        mhalf = sb("mhalf", [P, NT], F32)
        amax, ascale, cscale = sb("amax", [P, NT], F32), sb("ascale", [P, NT], F32), sb("cscale", [P, NT], F32)
        sc = here.enter_context(nc.psum_tensor("scores", [P, 2, 2, D], F32))
        ptb = here.enter_context(nc.psum_tensor("ptb", [P, 2, D], F32))
        wb = here.enter_context(nc.psum_tensor("wb", [P, 2, D], F32))

        dve_step, prep = sem("dve_step"), sem("prep")
        x_loaded, k0_loaded, k1_loaded, v0_loaded, v1_loaded, stored = (sem(n) for n in (
            "x_loaded", "k0_loaded", "k1_loaded", "v0_loaded", "v1_loaded", "stored"))
        k0_ready, k1_ready = sem("k0_ready"), sem("k1_ready")
        bank_full, bank_hi, bank_free = sem("bank_full"), sem("bank_hi"), sem("bank_free")
        scores_full, shifted, exp_done, sums_ready, probs_ready = (sem(n) for n in (
            "scores_full", "shifted", "exp_done", "sums_ready", "probs_ready"))
        prT_full, prT_hi, prT_free = sem("prT_full"), sem("prT_hi"), sem("prT_free")
        ln_var = [sem(f"ln_var{i}") for i in range(4)]
        ln_rstd = [sem(f"ln_rstd{i}") for i in range(4)]
        ln_done = [sem(f"ln_done{i}") for i in range(4)]
        x1_biased, x2_biased, x3_biased = sem("x1_biased"), sem("x2_biased"), sem("x3_biased")

        x_v = x.rearrange("b (p t) d -> b p t d", t=NT)
        out_v = out.rearrange("b (p t) d -> b p t d", t=NT)
        PIECES = []
        for hh in range(4):
            r = hh * KEYS
            while r < (hh + 1) * KEYS:
                c = r // CH
                n = min((c + 1) * CH, (hh + 1) * KEYS) - r
                PIECES.append((hh, c, r - c * CH, r - hh * KEYS, n))
                r += n
        V1SLOT = {(0, 0): 0, (1, 0): 1, (1, 1): 3, (2, 1): 4, (2, 2): 6, (3, 2): 7}

        def unit_place(stage, u):
            return (u // 2, u % 2) if stage == "X" else (u % NT, u // NT)

        def parts(j, b, tiles):
            return (2 * b + (2 if tiles.stop == NT else 1)) if j == 1 else b + 1

        PREP = 7
        block = here.enter_context(nc.Block())

        @block.sync
        def _(sp):
            def load_k(layer, b):
                scr_k, kl, width = (scr_k0, k0_loaded, 2 * ND * KEYS) if layer == 0 else (scr_k1, k1_loaded, 2 * ND1 * KEYS)
                sp.dma_start(kd[:, :, :, :].rearrange("p h m n -> p (h m n)")[:, 0:width], scr_k[:, b, :]).then_inc(kl, 16)

            def load_v(layer, b):
                for hh, c, r0, k0, n in PIECES:
                    if layer == 0:
                        src = scr_v0[bass.ds(b * KEYS + k0, n), hh, :]
                        sp.dma_start(v0b[r0:r0 + n, c, hh - c, :, :, :].rearrange("p h g d -> p (h g d)"), src).then_inc(v0_loaded, 16)
                    else:
                        src = scr_v1[bass.ds(b * KEYS + k0, n), hh, :]
                        sp.dma_start(v1b[r0:r0 + n, :, :, V1SLOT[hh, c], :].rearrange("p h g d -> p (h g) d"),
                                     src.rearrange("p (q d) -> p q d", d=H1)).then_inc(v1_loaded, 16)

            sp.wait_ge(prep, PREP)

            def body(it, loop):
                i = it.i
                if "Y" in it.present:
                    sp.wait_ge(k0_ready, it.done["X"] + 1 if "X" in it.present else B)
                    load_k(1, it.done["Y"])
                    if not (isinstance(i, int) and i == 1):
                        sp.wait_ge(bank_full, it.bank(*it.order[0])[1])
                    load_v(1, it.done["Y"])
                if "W" in it.present:
                    if "Y" in it.present:
                        sp.wait_ge(k1_ready, it.done["Y"] + 1)
                    elif "X" in it.present:
                        sp.wait_ge(k0_ready, it.done["X"] + 1)
                    load_k(0, it.done["W"])
                    if "X" in it.present:
                        sp.wait_ge(bank_full, it.bank("X", "pv", NT - 1)[1] + 1)
                    load_v(0, it.done["W"])
                    if "X" in it.present:
                        sp.wait_ge(bank_free, it.bank("X", "f", NT - 1)[1] + 1)
                    sp.dma_start(x1[:, :, :], x_v[it.done["W"]]).then_inc(x_loaded, 16)
                if "Z" in it.present:
                    sp.wait_ge(bank_free, it.bank("Z", "f", NT - 1)[1] + 1)
                    sp.dma_start(out_v[it.done["Z"]], x3[:, :, :]).then_inc(stored, 16)

            walk(sp, body)
            sp.wait_ge(stored, 16 * B)

        @block.gpsimd
        def _(pool):
            pool.memset(v0b[:, :, :, :, :, :], 0.0).then_inc(prep, 1)
            pool.memset(v1b[:, :, :, :, :], 0.0).then_inc(prep, 1)
            pool.memset(k0b[:, :, :, :, :], 0.0).then_inc(prep, 1)
            pool.memset(k1b[:, :, :, :, :], 0.0).then_inc(prep, 1)
            pool.memset(ones[:, :], 1.0).then_inc(prep, 1)
            pool.memset(mhalf[:, :], -0.5).then_inc(prep, 1)
            for n in range(4):
                last = pool.memset(pr[n][:, :, GK:GKP], 0.0)
            last.then_inc(prep, 1)
            pool.wait_ge(prep, PREP)

            def rstd_of(j, b, tiles=slice(0, NT)):
                pool.wait_ge(ln_var[j], parts(j, b, tiles))
                pool.tensor_tensor(rstd[:, j, tiles], var[:, j, tiles], mhalf[:, tiles], ALU.pow).then_inc(ln_rstd[j], 1)

            def normalise(U, n):
                p = pr[n % 4]
                pool.wait_ge(sums_ready, U + 1)
                v = p[:, :, 0:GK].rearrange("p g (h n) -> p g h n", h=4)
                s = sm[:, n % 4, :].rearrange("p (g h u) -> p g h u", g=2, u=1).broadcast_to([P, 2, 4, KEYS])
                pool.tensor_tensor(v, v, s, ALU.mult).then_inc(probs_ready, 1)

            def add_bias(o, a, bias, ready, normed, b, t):
                if normed is not None:
                    pool.wait_ge(normed, NT * b + t + 1)
                pool.tensor_tensor(o[:, t, :], a[:, t, :], bias[:, :], ALU.add).then_inc(ready, 1)

            def body(it, loop):
                X, Y, Z, Wb = (it.done[s] for s in "XYZW")
                pres = it.present
                if "X" in pres:
                    for u in range(8):
                        if u == 7:
                            rstd_of(1, X, slice(0, 2))
                        normalise(it.unit("X", u), u)
                if "Z" in pres:
                    rstd_of(3, Z)
                for t in range(NT):
                    if t == 2 and "X" in pres:
                        for tile in (0, 1):
                            add_bias(x1, x1, k["bf0"], x1_biased, ln_done[1], X, tile)
                        rstd_of(1, X, slice(2, NT))
                    if "Y" in pres:
                        if t == 0 and "Z" in pres:
                            pool.wait_ge(bank_free, it.bank("Z", "out", NT - 1)[1] + 1)
                        add_bias(x2b, x2, k["bo"], x2_biased, None, Y, t)
                for u in range(8):
                    if "X" in pres and u == 4:
                        rstd_of(2, X)
                    if u == 6 and "W" in pres:
                        rstd_of(0, Wb)
                    if "Y" in pres:
                        normalise(it.unit("Y", u), u)
                    if "X" in pres and u == 0:
                        for tile in (2, 3):
                            add_bias(x1, x1, k["bf0"], x1_biased, ln_done[1], X, tile)
                    if "Z" in pres and 1 <= u <= NT:
                        add_bias(x3, x3, k["bf1"], x3_biased, ln_done[3], Z, u - 1)

            walk(pool, body)

        @block.scalar
        def _(act):
            act.wait_ge(prep, PREP)

            def hi_part(it, use, o, **kw):
                bank, n = it.bank(*use)
                act.wait_ge(bank_full, n + 1)
                src = wb[:, bank, :]
                if len(o.shape) == 3:
                    src = src.rearrange("p (c n) -> p c n", c=ND)
                act.activation(o, src, **kw).then_inc(bank_hi, 1)

            def transposed(it, stage, t, o):
                hi_part(it, (stage, "t", t), o[:, 0, :, t * P:(t + 1) * P], func=ACT.Copy)

            def exp(it, stage, u):
                U = it.unit(stage, u)
                act.wait_ge(shifted, U + 1)
                f = F_E0 if stage == "X" else F_E1
                act.activation(pr[u % 4][:, :, 0:GK], pr[u % 4][:, :, 0:GK], ACT.Exp,
                               scale=k["factor"][:, f:f + 1]).then_inc(exp_done, 1)

            def prT_high(it, stage, u):
                U, (t, h) = it.unit(stage, u), unit_place(stage, u)
                act.wait_ge(prT_full, U + 1)
                o = prT[:, 0, 2 * h:2 * h + 2, :, t * P:(t + 1) * P]
                act.activation(o, ptb[0:CH, :, 0:3 * P].rearrange("p g (c n) -> p g c n", c=3), ACT.Copy,
                               scale=PS).then_inc(prT_hi, 1)

            def diagonal(layer, it, b):
                kd, kb, n, w = (k0d, k0b, 4, H0) if layer == 0 else (k1d, k1b, 2, H1)
                act.wait_ge(k0_loaded if layer == 0 else k1_loaded, (b + 1) * 16)
                for j in range(n):
                    last = act.activation(kb[j * w:(j + 1) * w, :, :, j, :], kd[j * w:(j + 1) * w, :, :, :], ACT.Copy)
                if layer == 0:
                    act.activation(mrow[:, :, :], k["maskall"][:, bass.ds(b, 1), :].broadcast_to([1, 4, KEYS]), ACT.Copy).then_inc(k0_ready, 1)
                else:
                    last.then_inc(k1_ready, 1)

            def body(it, loop):
                X, Y, Z, Wb = (it.done[s] for s in "XYZW")
                pres = it.present

                def high(use):
                    stage, what, n = use
                    if what == "t" and stage != "X":
                        transposed(it, stage, n, xT4 if stage == "Z" else xT)
                    elif what == "q":
                        q, bias = (qc, k["bq1"]) if stage == "Y" else (q0T, k["bq0"])
                        hi_part(it, use, q[:, 0, n, :], func=ACT.Identity, bias=bias[:, n:n + 1])
                    elif use[:2] == ("Y", "pv"):
                        hi_part(it, use, qc[:, 0, n, :], func=ACT.Copy)

                def softmax(stage, listed, s):
                    if stage in pres and s >= 2:
                        prT_high(it, stage, s - 2)
                    if stage in pres and s < 8:
                        exp(it, stage, s)
                    for use in it.uses(listed[s]):
                        high(use)

                for s in range(10):
                    softmax("X", A_USES, s)
                    if s == 3 and "Y" in pres:
                        diagonal(1, it, Y)
                for use in it.uses(M_USES):
                    high(use)
                for s in range(10):
                    softmax("Y", B_USES, s)
                    if s == 5 and "W" in pres:
                        diagonal(0, it, Wb)
                for use in it.uses(C_USES):
                    high(use)

            walk(act, body)

        @block.vector
        def _(dve):
            step = Chain(dve, dve_step)
            dve.wait_ge(prep, PREP)

            def ln_stats(j, src, tiles):
                for t in tiles:
                    last = dve.bn_stats(stats[:, j, t, :], src[:, t, :])
                if tiles[-1] == NT - 1 or (j == 1 and tiles[-1] == 1):
                    step(last)
                    ts = slice(0, NT) if j != 1 else slice(tiles[-1] - 1, tiles[-1] + 1)
                    m, v, h = mean[:, j, ts], var[:, j, ts], half[:, j, ts]
                    e, o = stats[:, j, ts, 1], stats[:, j, ts, 4]
                    dve.tensor_tensor(m, e, o, ALU.add)
                    dve.tensor_tensor(h, e, o, ALU.subtract)
                    step(dve.tensor_tensor(v, stats[:, j, ts, 2], stats[:, j, ts, 5], ALU.add))
                    dve.tensor_scalar(m, m, 0.5, None, ALU.mult)
                    dve.tensor_scalar(v, v, 1.0 / D, EPS, ALU.mult, ALU.add)
                    step(dve.scalar_tensor_tensor(out=h, in0=h, scalar=0.25, in1=h, op0=ALU.mult, op1=ALU.mult))
                    dve.tensor_tensor(v, v, h, ALU.add).then_inc(ln_var[j], 1)

            def ln_apply(j, src, tiles, b, signal=True):
                if tiles[0] == 0 or (j == 1 and tiles[0] == 2):
                    dve.wait_ge(ln_rstd[j], parts(j, b, slice(0, tiles[-1] + 1)))
                for t in tiles:
                    ins = dve.tensor_scalar(xn[:, t, :], src[:, t, :], mean[:, j, t:t + 1], rstd[:, j, t:t + 1],
                                            ALU.subtract, ALU.mult)
                    if signal:
                        ins.then_inc(ln_done[j], 1)
                return ins

            def quantise_a(t, b):
                pair = slice(t, t + 2)
                step(ln_apply(1, x1, [t, t + 1], b, signal=False))
                step(dve.tensor_reduce(amax[:, pair], xn[:, pair, :], AX.X, ALU.max, apply_absolute_value=True))

            def quantise_b(t):
                pair = slice(t, t + 2)
                step(dve.tensor_scalar(amax[:, pair], amax[:, pair], 1e-5, None, ALU.max))
                dve.tensor_scalar(cscale[:, pair], amax[:, pair], k["factor"][:, F_WSC:F_WSC + 1], None, ALU.mult)
                step(dve.reciprocal(ascale[:, pair], amax[:, pair]))
                step(dve.tensor_scalar(ascale[:, pair], ascale[:, pair], 127.0, None, ALU.mult))
                for j in (t, t + 1):
                    ins = dve.tensor_scalar(xn[:, j, :], xn[:, j, :], ascale[:, j:j + 1], MAGIC, ALU.mult, ALU.add)
                step(ins)
                dve.tensor_scalar(qi[:, pair, :], xn[:, pair, :], MAGIC, 127.0, ALU.subtract, ALU.min).then_inc(ln_done[1], 2)

            def lo_part(it, use, lo, hi, bias=0.0):
                bank, n = it.bank(*use)
                dve.wait_ge(bank_hi, it.hi(*use) + 1)
                src = wb[:, bank, :]
                if len(lo.shape) == 3:
                    src = src.rearrange("p (c n) -> p c n", c=ND)
                if isinstance(bias, float):
                    ins = dve.tensor_tensor(lo, src, hi, ALU.subtract)
                else:
                    ins = dve.scalar_tensor_tensor(out=lo, in0=src, scalar=bias, in1=hi, op0=ALU.add, op1=ALU.subtract)
                ins.then_inc(bank_free, 1)

            def add_to(it, use, o, factor, a):
                bank, n = it.bank(*use)
                dve.wait_ge(bank_full, n + 1)
                dve.scalar_tensor_tensor(out=o, in0=wb[:, bank, :], scalar=factor, in1=a,
                                         op0=ALU.mult, op1=ALU.add).then_inc(bank_free, 1)

            def transposed(it, stage, t, o):
                c = slice(t * P, (t + 1) * P)
                lo_part(it, (stage, "t", t), o[:, 1, :, c], o[:, 0, :, c])

            def four(ap):
                return ap.rearrange("p g (h n) -> p g h n", h=4)

            def maxima(it, stage, u):
                U = it.unit(stage, u)
                dve.wait_ge(scores_full, U + 1)
                s = four(sc[:, u % 2, :, 0:GK])
                m = mx[:, u % 4, :].rearrange("p (g h) -> p g h", g=2)
                step(dve.tensor_reduce(m, s, AX.X, ALU.max))
                m = mx[:, u % 4, :].rearrange("p (g h u) -> p g h u", g=2, u=1).broadcast_to([P, 2, 4, KEYS])
                dve.tensor_tensor(four(pr[u % 4][:, :, 0:GK]), s, m, ALU.subtract).then_inc(shifted, 1)

            def sums(it, stage, u):
                U = it.unit(stage, u)
                dve.wait_ge(exp_done, U + 1)
                step(dve.tensor_reduce(sm[:, u % 4, :].rearrange("p (g h) -> p g h", g=2), four(pr[u % 4][:, :, 0:GK]), AX.X, ALU.add))
                dve.reciprocal(sm[:, u % 4, :], sm[:, u % 4, :]).then_inc(sums_ready, 1)

            def prT_low(it, stage, u):
                U, (t, h) = it.unit(stage, u), unit_place(stage, u)
                dve.wait_ge(prT_hi, U + 1)
                pair = [prT[:, j, 2 * h:2 * h + 2, :, t * P:(t + 1) * P].rearrange("p g c n -> p (g c) n") for j in range(2)]
                for g in range(2):
                    ins = dve.scalar_tensor_tensor(out=pair[1][:, 3 * g:3 * g + 3], in0=ptb[0:CH, g, 0:3 * P].rearrange("p (c n) -> p c n", c=3),
                                                   scalar=PS, in1=pair[0][:, 3 * g:3 * g + 3], op0=ALU.mult, op1=ALU.subtract)
                ins.then_inc(prT_free, 1)

            f = k["factor"]

            def values0_done(it, t):
                add_to(it, ("X", "pv", t), x1[:, t, :], f[:, F_PV0:F_PV0 + 1], x1[:, t, :])
                dve.wait_ge(bank_free, it.bank("X", "pv", t)[1] + 1)
                ln_stats(1, x1, [t])

            def body(it, loop):
                X, Y, Z, Wb = (it.done[s] for s in "XYZW")
                pres = it.present
                if loop:
                    start = step.count.base + step.count.local
                    step.count.base, step.count.local = start + (it.i - loop[0]) * STEPS_PER_ITERATION, 0

                def low(use):
                    stage, what, n = use
                    if use[:2] == ("X", "t"):
                        bank, before = it.bank(*use)
                        dve.wait_ge(bank_full, before + 1)
                        dve.tensor_copy(qiT[:, :, n * P:(n + 1) * P], wb[:, bank, :].bitcast(BF16)[:, 0:D].rearrange(
                            "p (c n) -> p c n", c=ND)).then_inc(bank_free, 1)
                    elif what == "t":
                        transposed(it, stage, n, xT4 if stage == "Z" else xT)
                    elif what == "q":
                        q, bias = (qc, k["bq1"]) if stage == "Y" else (q0T, k["bq0"])
                        lo_part(it, use, q[:, 1, n, :], q[:, 0, n, :], bias[:, n:n + 1])
                    elif use[:2] == ("X", "pv"):
                        values0_done(it, n)
                    elif use[:2] == ("Y", "pv"):
                        lo_part(it, use, qc[:, 1, n, :], qc[:, 0, n, :])
                    elif what == "out":
                        if n == 0 and not (isinstance(Z, int) and Z == 0):
                            dve.wait_ge(stored, 16 * Z)
                        dve.wait_ge(x2_biased, NT * Z + n + 1)
                        add_to(it, use, x3[:, n, :], f[:, F_OUT:F_OUT + 1], x2b[:, n, :])
                    elif use[:2] == ("X", "f"):
                        dve.wait_ge(x1_biased, NT * X + n + 1)
                        if "Y" in pres:
                            dve.wait_ge(x2_biased, NT * Y + n + 1)
                        add_to(it, use, x2[:, n, :], cscale[:, n:n + 1], x1[:, n, :])
                    else:
                        dve.wait_ge(x3_biased, NT * Z + n + 1)
                        add_to(it, use, x3[:, n, :], k["inv"][:, S_M:S_M + 1], x3[:, n, :])

                def softmax(stage, s):
                    if stage in pres:
                        if 1 <= s < 9:
                            sums(it, stage, s - 1)
                        if s < 8:
                            maxima(it, stage, s)
                        if s >= 2:
                            prT_low(it, stage, s - 2)

                for s in range(10):
                    softmax("X", s)
                    if "Z" in pres and s in (3, 5, 7, 8):
                        t = (s - 2) // 2
                        dve.wait_ge(bank_free, it.bank("Z", "out", t)[1] + 1)
                        ln_stats(3, x3, [t])
                    for use in it.uses(A_USES[s]):
                        low(use)
                    if "X" in pres and s == 8:
                        quantise_a(0, X)
                    if "X" in pres and s == 9:
                        quantise_b(0)
                for n, use in enumerate(M_USES):
                    if use[0] in pres:
                        low(use)
                    if "X" in pres and n == 3:
                        quantise_a(2, X)
                    if "X" in pres and n == 5:
                        quantise_b(2)
                for s in range(10):
                    softmax("Y", s)
                    if "W" in pres and s == 7:
                        if "X" in pres:
                            dve.wait_ge(ln_done[1], NT * (X + 1))
                        ln_apply(0, x1, list(range(NT)), Wb)
                    for use in it.uses(B_USES[s]):
                        low(use)
                    if "Z" in pres and s in (0, 1):
                        if "X" in pres:
                            dve.wait_ge(ln_done[1], NT * (X + 1))
                        ln_apply(3, x3, [2 * s, 2 * s + 1], Z)
                    if "X" in pres and s in (3, 4):
                        dve.wait_ge(bank_free, it.bank("X", "f", 2 * s - 5)[1] + 1)
                        ln_stats(2, x2, [2 * s - 6, 2 * s - 5])
                    if "W" in pres:
                        if s == 5:
                            dve.wait_ge(x_loaded, 16 * (Wb + 1))
                        if s in (5, 6):
                            ln_stats(0, x1, [2 * s - 10, 2 * s - 9])
                for n, use in enumerate(C_USES):
                    if use[0] in pres:
                        low(use)
                    if "X" in pres and n < NT:
                        ln_apply(2, x2, [n], X)
                if loop:
                    assert step.count.local == STEPS_PER_ITERATION, step.count.local
                    step.count.base, step.count.local = start + (loop[1] - loop[0]) * STEPS_PER_ITERATION, 0

            walk(dve, body)

        @block.tensor
        def _(pe):
            pe.wait_ge(prep, PREP)
            ident, identb = k["ident"], k["identb"]

            def take(it, *use):
                bank, n = it.bank(*use)
                if not (isinstance(n, int) and n < 2):
                    pe.wait_ge(bank_free, n - 1)
                return bank

            def transpose_tile(it, stage, t):
                j = "WXYZ".index(stage)
                bank = take(it, stage, "t", t)
                pe.wait_ge(ln_done[j], NT * it.done[stage] + t + 1)
                for c in range(ND):
                    if stage == "X":
                        ins = pe.transpose(wb[:, bank, :].bitcast(BF16)[:, c * P:(c + 1) * P], qi[:, t, c * P:(c + 1) * P], identb[:, :])
                    else:
                        ins = pe.transpose(wb[:, bank, c * P:(c + 1) * P], xn[:, t, c * P:(c + 1) * P], ident[:, :])
                ins.then_inc(bank_full, 1)

            def project(it, stage, m, w, src):
                bank = take(it, stage, "q", m)
                if m == 0:
                    pe.wait_ge(bank_free, it.bank(stage, "t", NT - 1)[1] + 1)
                for c in range(ND):
                    ins = products(pe, wb[:, bank, :], lambda h: w[:, h, c, m * P:(m + 1) * P], lambda h: src[:, h, c, :],
                                   c == 0, c == ND - 1)
                ins.then_inc(bank_full, 1)

            def scores(it, stage, u):
                U, (t, half) = it.unit(stage, u), unit_place(stage, u)
                if not (isinstance(U, int) and U < 2):
                    pe.wait_ge(shifted, U - 1)
                tok = slice(t * P, (t + 1) * P)
                for gg in range(2):
                    g = 2 * half + gg
                    if stage == "X":
                        o = sc[:, u % 2, gg, 0:GK]
                        pe.matmul(o, ones[:, :], mrow[:, :, :].rearrange("o h n -> o (h n)"), start=True, stop=False)
                        ins = products(pe, o, lambda h: q0T[:, h, g, tok],
                                       lambda h: k0b[:, h, g, :, :].rearrange("p j n -> p (j n)"), False, True)
                    else:
                        for e in range(2):
                            pair = 2 * g + e
                            ins = products(pe, sc[:, u % 2, gg, e * 2 * KEYS:(e + 1) * 2 * KEYS], lambda h: qc[:, h, pair, tok],
                                           lambda h: k1b[:, h, pair, :, :].rearrange("p j n -> p (j n)"), e == 0, True, skip=True)
                ins.then_inc(scores_full, 1)

            def probs_transpose(it, stage, u):
                U = it.unit(stage, u)
                pe.wait_ge(probs_ready, U + 1)
                if not (isinstance(U, int) and U < 1):
                    pe.wait_ge(prT_free, U)
                for gg in range(2):
                    for c in range(3):
                        ins = pe.transpose(ptb[0:CH, gg, c * P:(c + 1) * P], pr[u % 4][:, gg, c * CH:(c + 1) * CH], ident[:, :])
                ins.then_inc(prT_full, 1)

            def values0(it, t):
                bank = take(it, "X", "pv", t)
                pe.wait_ge(prT_free, it.unit("X", 2 * t + 1) + 1)
                first = True
                for g in range(G):
                    for c in range(3):
                        o = wb[:, bank, g * P + c * H0:g * P + (c + 2) * H0]
                        ins = products(pe, o, lambda h: prT[:, h, g, c, t * P:(t + 1) * P], lambda h: v0b[:, c, :, h, g, :],
                                       first, g == G - 1 and c == 2, skip=True)
                        first = False
                ins.then_inc(bank_full, 1)

            def values1(it, pair):
                bank = take(it, "Y", "pv", pair)
                if pair % 4 == 0:
                    pe.wait_ge(prT_free, it.unit("Y", pair + 3) + 1)
                g, e = pair // 2, pair % 2
                for n, (c, slot) in enumerate(((0, 0), (1, 2)) if e == 0 else ((1, 4), (2, 6))):
                    ins = products(pe, wb[:, bank, :], lambda h: v1b[:, h, g, slot:slot + 2, :].rearrange("p s d -> p (s d)"),
                                   lambda h: prT[:, h, g, c, :], n == 0, n == 1)
                ins.then_inc(bank_full, 1)

            def output(it, t):
                bank = take(it, "Z", "out", t)
                if t == 0:
                    pe.wait_ge(bank_free, it.bank(*it.order[0])[1])
                for j in range(ND1):
                    ins = products(pe, wb[:, bank, :], lambda h: qc[:, h, j, t * P:(t + 1) * P], lambda h: k["wo"][:, h, j, :],
                                   j == 0, j == ND1 - 1)
                ins.then_inc(bank_full, 1)

            def ffn0(it, t):
                bank = take(it, "X", "f", t)
                pe.wait_ge(bank_free, it.bank("X", "t", t)[1] + 1)
                for c in range(ND):
                    ins = pe.matmul(wb[:, bank, :], qiT[:, c, t * P:(t + 1) * P], k["tern"][:, c, :], start=c == 0, stop=c == ND - 1)
                ins.then_inc(bank_full, 1)

            def ffn1(it, t):
                bank = take(it, "Z", "f", t)
                pe.wait_ge(bank_free, it.bank("Z", "t", t)[1] + 1)
                for c in range(ND):
                    ins = products(pe, wb[:, bank, :], lambda h: xT4[:, h, c, t * P:(t + 1) * P], lambda h: k["m"][:, h, c, :],
                                   c == 0, c == ND - 1)
                ins.then_inc(bank_full, 1)

            def body(it, loop):
                X, Y, Z, Wb = (it.done[s] for s in "XYZW")
                pres = it.present

                def fill(use):
                    stage, what, n = use
                    if what == "t":
                        transpose_tile(it, stage, n)
                    elif what == "q":
                        project(it, stage, n, *((k["wq1"], xT) if stage == "Y" else (k["wq0"], xT)))
                    elif what == "out":
                        output(it, n)
                    elif what == "pv":
                        (values0 if stage == "X" else values1)(it, n)
                    else:
                        (ffn0 if stage == "X" else ffn1)(it, n)

                def softmax(stage, listed, s):
                    if stage in pres:
                        if s + 1 < 8:
                            if stage == "Y" and s + 1 == NT:
                                pe.wait_ge(bank_free, it.bank("Y", "q", ND1 - 1)[1] + 1)
                            scores(it, stage, s + 1)
                        if s >= 2:
                            probs_transpose(it, stage, s - 2)
                    for use in it.uses(listed[s]):
                        fill(use)

                if "X" in pres:
                    pe.wait_ge(k0_ready, X + 1)
                    later = 0 if isinstance(it.i, int) and it.i < 2 else AFTER_W
                    pe.wait_ge(bank_free, it.bank(*it.order[0])[1] - later)
                    scores(it, "X", 0)
                for s in range(10):
                    if s == 4 and "X" in pres:
                        pe.wait_ge(v0_loaded, 16 * len(PIECES) * (X + 1))
                    softmax("X", A_USES, s)
                for use in it.uses(M_USES):
                    fill(use)
                if "Y" in pres:
                    pe.wait_ge(k1_ready, Y + 1)
                    pe.wait_ge(bank_free, it.bank("Y", "q", 3)[1] + 1)
                    scores(it, "Y", 0)
                for s in range(10):
                    if s == 6 and "Y" in pres:
                        pe.wait_ge(v1_loaded, 16 * len(PIECES) * (Y + 1))
                    softmax("Y", B_USES, s)
                for use in it.uses(C_USES):
                    fill(use)

            walk(pe, body)


STEPS_PER_ITERATION = 5 * 3 + 4 * 8 + NT // 2 * 6



def constants():
    n = np.arange(D)
    a = 2.0 * np.pi * ((n[:, None] * n[None, :]) % D) / D
    c, s = np.cos(a), np.sin(a)
    parts = []
    for m in (c, s, -s):
        hi = m.astype(np.float16)
        lo = (m - hi.astype(np.float64)).astype(np.float16)
        for v in (hi, lo):
            parts.append(v.reshape(ND, P, D).transpose(1, 0, 2).reshape(P, ND * D))
    return np.ascontiguousarray(np.concatenate(parts, axis=1)), np.eye(P, dtype=np.float32)


def kernel(**inputs):
    import concourse.bacc as _bacc
    from concourse.bass_utils import run_bass_kernel_spmd as _run

    a = {n: np.asarray(v) for n, v in inputs.items()}

    def blocks(w):
        return w.reshape(-1, P, w.shape[1]).transpose(1, 0, 2)

    def flat(w):
        v = blocks(w)
        return v.reshape(P, -1)

    def by_slot(w, d):
        return w.reshape(w.shape[:-1] + (G, 4, d)).swapaxes(-3, -2).reshape(w.shape)

    dft, eye = constants()
    data = {
        "x": a["x"],
        "ctxT": blocks(a["ctx_1024"].reshape(ROWS, D).T),
        "mask": a["mask_BxS2_ik0"].reshape(1, ROWS),
        "wq0": flat(a["L0_xattn_q_w"].T),
        "bq0": a["L0_xattn_q_b"].reshape(ND, P).T,
        "wk0": blocks(a["L0_xattn_k_w"].T),
        "bk0": a["L0_xattn_k_b"].reshape(ND, P).T,
        "wv0": blocks(by_slot(a["L0_xattn_v_w"].T, H0)),
        "bv0": by_slot(a["L0_xattn_v_b"], H0),
        "packed": a["L0_ffn_packed_weight"].reshape(P, D),
        "wscale": a["L0_ffn_weight_scale"],
        "bf0": a["L0_ffn_bias"],
        "wq1": flat(a["L1_xattn_Wq"].reshape(D, D1)),
        "bq1": a["L1_xattn_bq"].reshape(ND1, P).T,
        "wk1": blocks(a["L1_xattn_Wk"].reshape(D, D1)),
        "bk1": a["L1_xattn_bk"].reshape(ND1, P).T,
        "wv1": blocks(by_slot(a["L1_xattn_Wv"].reshape(D, D1), H1)),
        "bv1": by_slot(a["L1_xattn_bv"].reshape(D1), H1),
        "wo": flat(a["L1_xattn_Wo"].reshape(D1, D)),
        "bo": a["L1_xattn_bo"],
        "wf": np.concatenate([flat(a["L1_ffn_w_freq_real"]), flat(a["L1_ffn_w_freq_imag"])], axis=1),
        "bf1": a["L1_ffn_bias"],
        "dft": dft,
        "eye": eye,
    }
    nc = _bacc.Bacc("TRN2", target_bir_lowering=False, num_devices=1)
    arrays, args = {}, []
    for name, v in data.items():
        v = np.ascontiguousarray(v)
        arrays[f"in_{name}"] = v
        args.append(nc.dram_tensor(f"in_{name}", v.shape, mybir.dt.from_np(v.dtype), kind="ExternalInput").ap())
    out = nc.dram_tensor("out_x", (B, S, D), F32, kind="ExternalOutput").ap()
    program(nc, *args, out)
    r = _run(nc, [arrays], core_ids=[0])
    return r.results[0]["out_x"]
```

```python
import numpy as np
import concourse.bass as bass
from concourse import mybir
from contextlib import ExitStack

F32 = mybir.dt.float32
F16 = mybir.dt.float16
BF16 = mybir.dt.bfloat16
I32 = mybir.dt.int32
ALU = mybir.AluOpType
ACT = mybir.ActivationFunctionType
AX = mybir.AxisListType

P = 128
B, S, D = 8, 512, 512
KEYS = 77
ROWS = B * KEYS
NT = S // P
ND = D // P
H0, H1 = 32, 64
D1 = 16 * H1
ND1 = D1 // P
G = 4
GK = 4 * KEYS
CH = (GK + 2) // 3
GKP = 3 * CH
RC = (ROWS + P - 1) // P
RL = ROWS - (RC - 1) * P
EPS = 1e-5
MAGIC = 12582912.0
PS = 256.0
BIG = -1e30


class Count:

    def __init__(self):
        self.base, self.local = 0, 0

    def next(self):
        self.local += 1
        return self.base + self.local


A_USES = [[],
          [("Y", "t", 0), ("Z", "out", 0)],
          [("Y", "t", 1), ("Y", "t", 2)],
          [("Z", "out", 1)],
          [("Y", "t", 3)],
          [("Z", "out", 2)],
          [("X", "pv", 0)],
          [("X", "pv", 1), ("Z", "out", 3)],
          [("Y", "q", 0)],
          [("Y", "q", 1)],
          [("Y", "q", 2), ("X", "pv", 2)]]
M_USES = [("Y", "q", 3), ("X", "pv", 3), ("X", "t", 0), ("X", "t", 1), ("Y", "q", 4)]
B_USES = [[("X", "t", 2), ("Y", "q", 5)],
          [("Y", "q", 6), ("X", "t", 3)],
          [("X", "f", 0), ("Y", "q", 7), ("X", "f", 1), ("X", "f", 2), ("X", "f", 3)],
          [("Z", "t", 0)],
          [("Z", "f", 0), ("Z", "t", 1)],
          [("Z", "f", 1), ("Z", "t", 2)],
          [("Z", "t", 3), ("Z", "f", 2)],
          [("Y", "pv", 0), ("Z", "f", 3)],
          [("W", "t", 0), ("Y", "pv", 1), ("W", "t", 1), ("Y", "pv", 2)],
          [("W", "t", 2), ("Y", "pv", 3), ("W", "t", 3)],
          [("W", "q", 0)]]
C_USES = [("Y", "pv", 4), ("Y", "pv", 5), ("W", "q", 1), ("W", "q", 2), ("Y", "pv", 6),
          ("W", "q", 3), ("Y", "pv", 7)]
BANK_ORDER = sum(A_USES, []) + M_USES + sum(B_USES, []) + C_USES
AFTER_W = len(BANK_ORDER) - 1 - BANK_ORDER.index(("W", "q", 3))
HI_ORDER = [u for u in BANK_ORDER if u[:2] in (("Y", "t"), ("Y", "q"), ("Z", "t"), ("W", "t"), ("W", "q"), ("Y", "pv"))]
STAGES = "XYZW"
PER = {s: sum(u[0] == s for u in BANK_ORDER) for s in STAGES}
PER_HI = {s: sum(u[0] == s for u in HI_ORDER) for s in STAGES}


class Iteration:

    def __init__(self, i, present):
        self.i, self.present = i, present
        lag = {"W": -1, "X": 0, "Y": 1, "Z": 2}
        self.done = {s: (i - lag[s] if s in present else (0 if isinstance(i, int) and i < lag[s] else B)) for s in STAGES}
        self.order = [u for u in BANK_ORDER if u[0] in present]
        self.hi_order = [u for u in HI_ORDER if u[0] in present]

    def uses(self, listed):
        return [u for u in listed if u[0] in self.present]

    def total(self, per):
        out = 0
        for s in STAGES:
            if per.get(s):
                out = out + self.done[s] * per[s]
        return out

    def bank(self, *use):
        k = self.order.index(use)
        return k % 2, self.total(PER) + k

    def hi(self, *use):
        return self.total(PER_HI) + self.hi_order.index(use)

    def unit(self, stage, u):
        k = u + (8 if stage == "Y" and "X" in self.present else 0)
        return self.total({"X": 8, "Y": 8}) + k


def plan():
    return ([(-1, "W"), (0, "WX"), (1, "WXY")], (2, B - 1, "WXYZ"), [(B - 1, "XYZ"), (B, "YZ"), (B + 1, "Z")])


def walk(eng, body):
    first, (a, b, stages), last = plan()
    for i, p in first:
        body(Iteration(i, p), None)
    with eng.Fori(a, b) as i:
        body(Iteration(i, stages), (a, b))
    for i, p in last:
        body(Iteration(i, p), None)


def products(pe, out, lhs, rhs, start, stop, skip=False):
    kw = dict(skip_group_check=True) if skip else {}
    pe.matmul(out, lhs(0), rhs(0), start=start, stop=False, **kw)
    pe.matmul(out, lhs(0), rhs(1), start=False, stop=False, **kw)
    return pe.matmul(out, lhs(1), rhs(0), start=False, stop=stop, **kw)


def program(nc, x, ctxT, mask, wq0, bq0, wk0, bk0, wv0, bv0, packed, wscale, bf0,
            wq1, bq1, wk1, bk1, wv1, bv1, wo, bo, wf, bf1, dft, eye, out):
    scr_k0 = nc.dram_tensor("scr_k0", (P, B, 2 * ND * KEYS), F16, kind="Internal").ap()
    scr_k1 = nc.dram_tensor("scr_k1", (P, B, 2 * ND1 * KEYS), F16, kind="Internal").ap()
    scr_v0 = nc.dram_tensor("scr_v0", (RC * P, 4, 2 * G * H0), F16, kind="Internal").ap()
    scr_v1 = nc.dram_tensor("scr_v1", (RC * P, 4, 2 * G * H1), F16, kind="Internal").ap()
    keep = ExitStack()
    with keep:
        def sb(stack, name, shape, dt):
            return stack.enter_context(nc.sbuf_tensor(name, shape, dt))

        k = {}
        k["wq0"] = sb(keep, "wq0_hl", [P, 2, ND, D], F16)
        k["wq1"] = sb(keep, "wq1_hl", [P, 2, ND, D1], F16)
        k["wo"] = sb(keep, "wo_hl", [P, 2, ND1, D], F16)
        k["m"] = sb(keep, "m_hl", [P, 2, ND, D], F16)
        k["tern"] = sb(keep, "tern", [P, ND, D], BF16)
        k["ident"] = sb(keep, "ident", [P, P], F32)
        k["identb"] = sb(keep, "identb", [P, P], BF16)
        k["bq0"] = sb(keep, "bq0_s", [P, ND], F32)
        k["bq1"] = sb(keep, "bq1_s", [P, ND1], F32)
        k["bo"] = sb(keep, "bo_b", [P, D], F32)
        k["bf0"] = sb(keep, "bf0_b", [P, D], F32)
        k["bf1"] = sb(keep, "bf1_b", [P, D], F32)
        k["maskall"] = sb(keep, "maskall", [1, B, KEYS], BF16)
        k["x1"] = sb(keep, "x1", [P, NT, D], F32)
        k["scale"] = sb(keep, "scale", [P, 16], F32)
        k["inv"] = sb(keep, "inv", [P, 16], F32)
        k["factor"] = sb(keep, "factor", [P, 8], F32)
        setup(nc, k, ctxT, wk0, bk0, wv0, bv0, wk1, bk1, wv1, bv1, scr_k0, scr_k1, scr_v0, scr_v1,
              mask, wq0, bq0, packed, wscale, bf0, wq1, bq1, wo, bo, wf, bf1, dft, eye, x)
        layers(nc, k, x, scr_k0, scr_k1, scr_v0, scr_v1, out)


S_CTX, S_WK0, S_WV0, S_WK1A, S_WK1B, S_WV1A, S_WV1B, S_K0, S_V0, S_K1, S_V1, S_WF, S_WQ0, S_WQ1, S_WO, S_M = range(16)
F_E0, F_E1, F_PV0, F_OUT, F_WSC, F_A, F_KV = range(7)


class Chain:

    def __init__(self, dve, sem):
        self.dve, self.sem, self.count = dve, sem, Count()

    def __call__(self, ins):
        v = self.count.next()
        ins.then_inc(self.sem, 1)
        self.dve.wait_ge(self.sem, v)


def find_scale(dve, step, k, slot, allmax, allmax_ready, n):
    dve.wait_ge(allmax_ready, n + 1)
    a = allmax[:, slot:slot + 1]
    step(dve.tensor_scalar(a, a, 1e-30, 1e37, ALU.max, ALU.min))
    step(dve.tensor_scalar(a.bitcast(I32), a.bitcast(I32), 0x7F800000, None, ALU.bitwise_and))
    step(dve.reciprocal(k["scale"][:, slot:slot + 1], a))
    step(dve.tensor_scalar(k["scale"][:, slot:slot + 1], k["scale"][:, slot:slot + 1], 32.0, None, ALU.mult))
    step(dve.tensor_scalar(k["inv"][:, slot:slot + 1], a, 1.0 / 32.0, None, ALU.mult))


SPLITS = [("WF", 2), ("WQ0", 1), ("CTX", 1), ("WQ1", 2), ("WK0", 1), ("WO", 2), ("WV0", 1), ("M", 1), ("WK1A", 1), ("WV1A", 1),
          ("K0", 1), ("V0", 1), ("WV1B", 1), ("WK1B", 1), ("V1", 2), ("K1", 2)]
NTH = {name: n for n, (name, _) in enumerate(SPLITS)}


def split_count(name, parts=None):
    n = NTH[name]
    return sum(p for _, p in SPLITS[:n]) + (SPLITS[n][1] if parts is None else parts)


def setup(nc, k, ctxT, wk0, bk0, wv0, bv0, wk1, bk1, wv1, bv1, scr_k0, scr_k1, scr_v0, scr_v1,
          mask, wq0, bq0, packed, wscale, bf0, wq1, bq1, wo, bo, wf, bf1, dft, eye, x):
    here = ExitStack()
    with here:
        def sb(name, shape, dt):
            return here.enter_context(nc.sbuf_tensor(name, shape, dt))

        def sem(name):
            return here.enter_context(nc.semaphore(name))

        stage = sb("a_stage", [P, 2, ND * ROWS], F32)
        ctx_hl = sb("a_ctx_hl", [P, 2, ND, ROWS], F16)
        w_hl = sb("a_w_hl", [P, 2, 2, ND, D], F16)
        dft_kf = sb("a_dft_kf", [P, 3 * 2 * ND * D // 2], F32)
        a_vf = sb("a_a_vf", [P, RC * D1], F32)
        wo_ks = sb("a_wo_ks", [P, ND1 * ROWS], F32)
        wq1_vs = sb("a_wq1_vs", [P, RC * D1], F32)
        mask_mf = sb("a_mask_mf", [P, ND * D], F32)
        dft_hl = dft_kf[:, :].bitcast(F16).rearrange("p (a h c n) -> p a h c n", a=3, h=2, c=ND)
        a_hl = a_vf[:, 0:2 * ND * D].bitcast(F16).rearrange("p (a h c n) -> p a h c n", a=2, h=2, c=ND)
        mf = mask_mf[:, :].rearrange("p (a n) -> p a n", a=ND)
        enc = wo_ks[:, 0:4 * D].bitcast(I32).rearrange("p (s n) -> p s n", s=4)
        pk = wo_ks[:, 4 * D:5 * D].bitcast(I32)
        ternrow = wo_ks[:, 5 * D:7 * D].bitcast(BF16).rearrange("p (s n) -> p s n", s=4)
        mraw = mask_mf[0:1, 0:ROWS].bitcast(I32).rearrange("o (b n) -> o b n", b=B)
        mkf = mask_mf[0:1, ROWS:2 * ROWS].rearrange("o (b n) -> o b n", b=B)
        nval = mask_mf[0:1, 2 * ROWS:2 * ROWS + B]
        kf = dft_kf[:, 0:ND1 * ROWS].rearrange("p (m r) -> p m r", m=ND1)
        vf = a_vf[:, :]
        ks, vs = wo_ks[:, :].bitcast(F16), wq1_vs[:, :].bitcast(F16)
        kb0, kb1 = sb("a_kb0", [P, ND], F32), sb("a_kb1", [P, ND1], F32)
        vb0, vb1 = (k["x1"][:, :, :].rearrange("p t d -> p (t d)")[:, a:b] for a, b in ((0, D), (D, D + D1)))
        absmax, allmax, parts = sb("a_absmax", [P, 16], F32), sb("a_allmax", [P, 16], F32), sb("a_parts", [P, 16, 3], F32)
        kfac = sb("a_kfactor", [P, 4], F32)
        kbank = here.enter_context(nc.psum_tensor("a_kbank", [P, 4, D], F32))
        vbank = here.enter_context(nc.psum_tensor("a_vbank", [P, 4, D], F32))

        loaded = [sem(f"a_loaded{i}") for i in range(2)]
        tern_in, small_in, dft_in, wq1_in, wo_in = sem("a_tern_in"), sem("a_small_in"), sem("a_dft_in"), sem("a_wq1_in"), sem("a_wo_in")
        dve_step, absmax_ready, allmax_ready = sem("a_dve_step"), sem("a_absmax_ready"), sem("a_allmax_ready")
        scale_ready, hi_done, lo_done = sem("a_scale_ready"), sem("a_hi_done"), sem("a_lo_done")
        k_full, k_free, v_full, v_free = sem("a_k_full"), sem("a_k_free"), sem("a_v_full"), sem("a_v_free")
        f_full, f_hi, f_free = sem("a_f_full"), sem("a_f_hi"), sem("a_f_free")
        tern_rows, tern_full, tern_done = sem("a_tern_rows"), sem("a_tern_full"), sem("a_tern_done")
        kout, vout, kfac_ready, part_max, x_in = sem("a_kout"), sem("a_vout"), sem("a_kfac_ready"), sem("a_part_max"), sem("a_x_in")
        K0N, K1N = 2 * ND, 2 * ND1
        F1, F2 = 2 * ND, 3 * ND

        STAGED = [[("WF", wf[:, 0:ND * D], ND * D), ("WQ0", wq0, ND * D), ("WK0", wk0, ND * D), ("WK1A", wk1[:, :, 0:D], ND * D),
                   ("WV1B", wv1[:, :, D:D1], ND * D)],
                  [("WF", wf[:, ND * D:2 * ND * D], ND * D), ("CTX", ctxT, ND * ROWS), ("WV0", wv0, ND * D),
                   ("WV1A", wv1[:, :, 0:D], ND * D), ("WK1B", wk1[:, :, D:D1], ND * D)]]
        W_PLACE = {"WK0": 0, "WV0": 1, "WK1A": 0, "WK1B": 1, "WV1A": 1, "WV1B": 0}
        PLACE_FREE = {"WK0": (f_full, F1), "WV0": (f_full, F1), "WK1A": (k_full, K0N), "WV1A": (v_full, RC),
                      "WV1B": (k_full, K0N + K1N // 2), "WK1B": (v_full, 2 * RC)}
        SLOT = {"WF": S_WF, "WQ0": S_WQ0, "CTX": S_CTX, "WQ1": S_WQ1, "WO": S_WO, "WK0": S_WK0, "WV0": S_WV0, "M": S_M,
                "WK1A": S_WK1A, "WK1B": S_WK1B, "K0": S_K0, "WV1A": S_WV1A, "V0": S_V0, "WV1B": S_WV1B, "K1": S_K1, "V1": S_V1}

        def flat(t):
            return t.rearrange("p a n -> p (a n)")

        def pieces(name):
            if name == "WF":
                return [[(stage[:, i, 0:ND * D], flat(w_hl[:, i, 0, :, :]), flat(w_hl[:, i, 1, :, :]))] for i in range(2)]
            if name == "CTX":
                return [[(stage[:, 1, :], flat(ctx_hl[:, 0, :, :]), flat(ctx_hl[:, 1, :, :]))]]
            if name == "WQ0":
                return [[(stage[:, 0, 0:ND * D], flat(k["wq0"][:, 0, :, :]), flat(k["wq0"][:, 1, :, :]))]]
            if name == "M":
                return [[(flat(mf), flat(k["m"][:, 0, :, :]), flat(k["m"][:, 1, :, :]))]]
            if name in ("WQ1", "WO"):
                w, src = (k["wq1"], wq1_vs) if name == "WQ1" else (k["wo"], wo_ks)
                n = 2 * ND * D
                return [[(src[:, i * n // 2:(i + 1) * n // 2], flat(w[:, 0, :, :])[:, i * n // 2:(i + 1) * n // 2],
                          flat(w[:, 1, :, :])[:, i * n // 2:(i + 1) * n // 2])] for i in range(2)]
            if name in W_PLACE:
                i = W_PLACE[name]
                return [[(stage[:, i, 0:ND * D], flat(w_hl[:, i, 0, :, :]), flat(w_hl[:, i, 1, :, :]))]]
            if name in ("K0", "K1"):
                m, m0 = (ND, ND) if name == "K0" else (ND1, 0)
                o = ks[:, 0:B * 2 * m * KEYS].rearrange("p (b h m k) -> p h m b k", b=B, h=2, m=m)
                i = kf[:, m0:m0 + m, :].rearrange("p m (b k) -> p m b k", b=B)
                return [[(i[:, j], o[:, 0, j], o[:, 1, j]) for j in range(p * ND, (p + 1) * ND)] for p in range(m // ND)]
            n = D if name == "V0" else D1
            o = vs[:, 0:RC * 2 * n].rearrange("p (r j h d) -> p h (r j) d", r=RC, j=4, h=2)
            i = vf[:, 0:RC * n].rearrange("p (rj d) -> p rj d", d=n // 4)
            cuts = [(0, 4 * RC)] if name == "V0" else [(0, 2 * RC), (2 * RC, 4 * RC)]
            return [[(i[:, a:b], o[:, 0, a:b], o[:, 1, a:b])] for a, b in cuts]

        block = here.enter_context(nc.Block())

        @block.sync
        def _(sp):
            def load(i, n):
                name, src, width = STAGED[i][n]
                if n:
                    sp.wait_ge(lo_done, split_count(STAGED[i][n - 1][0]))
                o = stage[:, i, 0:width]
                if len(src.shape) == 3:
                    o = o.rearrange("p (c n) -> p c n", c=ND)
                sp.dma_start(o, src).then_inc(loaded[i], 16)

            load(0, 0)
            load(1, 0)
            sp.dma_start(pk, packed).then_inc(tern_in, 16)
            sp.dma_start(k["ident"][:, :], eye).then_inc(tern_in, 16)
            sp.dma_start(dft_kf[:, :].bitcast(F16), dft).then_inc(dft_in, 16)
            sp.dma_start(k["bq0"][:, :], bq0).then_inc(small_in, 16)
            sp.dma_start(k["bq1"][:, :], bq1).then_inc(small_in, 16)
            sp.dma_start(mraw.rearrange("o b n -> o (b n)"), mask).then_inc(small_in, 16)
            sp.dma_start(k["factor"][:, F_WSC:F_WSC + 1], wscale.partition_broadcast(P)).then_inc(small_in, 16)
            sp.dma_start(kb0[:, :], bk0).then_inc(small_in, 16)
            sp.dma_start(kb1[:, :], bk1).then_inc(small_in, 16)
            sp.dma_start(vb0, bv0.partition_broadcast(P)).then_inc(small_in, 16)
            sp.dma_start(vb1, bv1.partition_broadcast(P)).then_inc(small_in, 16)
            sp.dma_start(k["bo"][:, :], bo.partition_broadcast(P)).then_inc(small_in, 16)
            sp.dma_start(k["bf0"][:, :], bf0.partition_broadcast(P)).then_inc(small_in, 16)
            sp.dma_start(k["bf1"][:, :], bf1.partition_broadcast(P)).then_inc(small_in, 16)
            load(0, 1)
            load(1, 1)
            sp.dma_start(wq1_vs[:, 0:ND * D1], wq1).then_inc(wq1_in, 16)
            load(0, 2)
            sp.wait_ge(tern_full, ND)
            sp.dma_start(wo_ks[:, 0:ND1 * D], wo).then_inc(wo_in, 16)
            load(1, 2)
            load(0, 3)
            load(1, 3)
            load(0, 4)
            load(1, 4)
            sp.wait_ge(lo_done, split_count("K0"))
            sp.dma_start(scr_k0.rearrange("p b n -> p (b n)"), ks[:, 0:B * 2 * ND * KEYS]).then_inc(kout, 16)
            sp.wait_ge(lo_done, split_count("V0"))
            sp.dma_start(scr_v0.rearrange("(r p) j n -> p r (j n)", p=P),
                         vs[:, 0:RC * 2 * D].rearrange("p (r n) -> p r n", r=RC)).then_inc(vout, 16)
            sp.wait_ge(v_free, 3 * RC)
            sp.dma_start(k["x1"][:, :, :], x.rearrange("b (p t) d -> b p t d", t=NT)[0]).then_inc(x_in, 16)
            sp.wait_ge(lo_done, split_count("V1"))
            sp.dma_start(scr_v1.rearrange("(r p) j n -> p r (j n)", p=P),
                         vs.rearrange("p (r n) -> p r n", r=RC)).then_inc(vout, 16)
            sp.wait_ge(lo_done, split_count("K1"))
            sp.dma_start(scr_k1.rearrange("p b n -> p (b n)"), ks).then_inc(kout, 16)
            sp.wait_ge(x_in, 16)
            sp.wait_ge(kout, 32)
            sp.wait_ge(vout, 32)

        @block.gpsimd
        def _(pool):
            for n, (name, _) in enumerate(SPLITS):
                s = slice(SLOT[name], SLOT[name] + 1)
                pool.wait_ge(absmax_ready, n + 1)
                pool.partition_all_reduce(allmax[:, s], absmax[:, s], P, bass.bass_isa.ReduceOp.absmax).then_inc(allmax_ready, 1)

        @block.vector
        def _(dve):
            step = Chain(dve, dve_step)
            arrival = {name: (loaded[i], 16 * (n + 1)) for i in range(2) for n, (name, _, _) in enumerate(STAGED[i])}
            arrival["WQ1"], arrival["WO"] = (wq1_in, 16), (wo_in, 16)
            biased = {"WQ0": k["bq0"], "WQ1": k["bq1"]}

            def maximum(name, views=None):
                slot = SLOT[name]
                am = absmax[:, slot:slot + 1]
                if name in arrival:
                    dve.wait_ge(*arrival[name])
                views = views or [p[0][0] for p in pieces(name)]
                if len(views) == 1 and name not in biased:
                    dve.tensor_reduce(am, views[0], AX.X, ALU.max, apply_absolute_value=True).then_inc(absmax_ready, 1)
                    return
                for j, v in enumerate(views):
                    if name == "WF" and j == 0:
                        dve.wait_ge(loaded[0], 16)
                    if name == "WF" and j == 1:
                        dve.wait_ge(loaded[1], 16)
                    last = dve.tensor_reduce(parts[:, slot, j:j + 1], v, AX.X, ALU.max, apply_absolute_value=True)
                step(last)
                n = len(views)
                if name in biased:
                    b = biased[name]
                    step(dve.tensor_reduce(parts[:, slot, n:n + 1], b[:, :], AX.X, ALU.max, apply_absolute_value=True))
                    step(dve.tensor_scalar(parts[:, slot, n:n + 1], parts[:, slot, n:n + 1], 1.0 / 256.0, None, ALU.mult))
                    n += 1
                dve.tensor_reduce(am, parts[:, slot, 0:n], AX.X, ALU.max).then_inc(absmax_ready, 1)

            def part_maximum(name, j, view):
                slot = SLOT[name]
                dve.tensor_reduce(parts[:, slot, j:j + 1], view, AX.X, ALU.max, apply_absolute_value=True).then_inc(part_max, 1)

            def joined_maximum(name, n, done):
                slot = SLOT[name]
                dve.wait_ge(part_max, done)
                dve.tensor_reduce(absmax[:, slot:slot + 1], parts[:, slot, 0:n], AX.X, ALU.max).then_inc(absmax_ready, 1)

            def scaling(name):
                slot = SLOT[name]
                find_scale(dve, step, k, slot, allmax, allmax_ready, NTH[name])
                if name in biased:
                    b = biased[name]
                    step(dve.tensor_scalar(b[:, :], b[:, :], k["scale"][:, slot:slot + 1], None, ALU.mult))
                dve.tensor_copy(allmax[:, slot:slot + 1], k["scale"][:, slot:slot + 1]).then_inc(scale_ready, 1)

            def low(name, only=None):
                slot = SLOT[name]
                for p, part in enumerate(pieces(name)):
                    if only is not None and p != only:
                        continue
                    dve.wait_ge(hi_done, split_count(name, p + 1))
                    for src, hi, lo in part:
                        ins = dve.scalar_tensor_tensor(out=lo, in0=src, scalar=k["scale"][:, slot:slot + 1], in1=hi,
                                                       op0=ALU.mult, op1=ALU.subtract)
                    ins.then_inc(lo_done, 1)

            def split(name):
                maximum(name)
                scaling(name)
                low(name)

            def ternary():
                dve.wait_ge(tern_in, 32)
                for s in range(4):
                    step(dve.tensor_scalar(enc[:, s, :], pk, 2 * s, 3, ALU.logical_shift_right, ALU.bitwise_and))
                step(dve.tensor_copy(k["identb"][:, :], k["ident"][:, :]))
                dve.tensor_scalar(ternrow, enc, -1.0, None, ALU.add).then_inc(tern_rows, 1)

            def ternary_columns():
                for c in range(ND):
                    dve.wait_ge(tern_full, c + 1)
                    dve.tensor_copy(k["tern"][:, c, :], vbank[:, c, :].bitcast(BF16)[:, 0:D]).then_inc(tern_done, 1)

            def mask_rows():
                step(dve.tensor_scalar(mkf, mraw, 0.0, None, ALU.is_gt))
                step(dve.tensor_reduce(nval, mkf, AX.X, ALU.add))
                step(dve.tensor_scalar(nval, nval, -1.0, float(KEYS), ALU.mult, ALU.add))
                step(dve.reciprocal(nval, nval))
                step(dve.tensor_scalar(nval, nval, 0.0, None, ALU.mult))
                step(dve.tensor_scalar(mkf, mkf, BIG, None, ALU.mult))
                step(dve.tensor_tensor(k["maskall"][:, :, :], mkf,
                                       nval.rearrange("o (b u) -> o b u", u=1).broadcast_to([1, B, KEYS]), ALU.add))

            def fw_low(js):
                for j in js:
                    dve.wait_ge(f_hi, j + 1)
                    dve.scalar_tensor_tensor(out=a_hl[:, j // ND, 1, j % ND, :], in0=kbank[:, j % 4, :], scalar=0.25,
                                             in1=a_hl[:, j // ND, 0, j % ND, :], op0=ALU.mult, op1=ALU.subtract).then_inc(f_free, 1)

            def m_evacuate(js):
                for j in js:
                    dve.wait_ge(f_full, F1 + j + 1)
                    dve.tensor_scalar(mf[:, j, :], kbank[:, j % 4, :], k["factor"][:, F_A:F_A + 1], None, ALU.mult).then_inc(f_free, 1)

            def v_evacuate(slot, bias, n0, col, width, chunks=range(RC)):
                if chunks[0] == 0:
                    step(dve.tensor_tensor(k["factor"][:, F_KV:F_KV + 1], k["inv"][:, S_CTX:S_CTX + 1],
                                           k["inv"][:, slot:slot + 1], ALU.mult))
                for r in chunks:
                    rows = P if r < RC - 1 else RL
                    dve.wait_ge(v_full, n0 + r + 1)
                    dve.scalar_tensor_tensor(out=vf[0:rows, r * width + col:r * width + col + D], in0=vbank[0:rows, (n0 + r) % 4, :],
                                             scalar=k["factor"][0:rows, F_KV:F_KV + 1], in1=bias[0:rows, :],
                                             op0=ALU.mult, op1=ALU.add).then_inc(v_free, 1)

            def factor(slot, a, b, c):
                f = k["factor"][:, slot:slot + 1]
                if b is None:
                    step(dve.tensor_scalar(f, k["inv"][:, a:a + 1], c, None, ALU.mult))
                else:
                    step(dve.tensor_scalar(f, k["inv"][:, a:a + 1], k["inv"][:, b:b + 1], None, ALU.mult))
                    step(dve.tensor_scalar(f, f, c, None, ALU.mult))

            split("WF")
            step(dve.tensor_scalar(k["factor"][:, F_A:F_A + 1], k["inv"][:, S_WF:S_WF + 1], 4.0 / D, None, ALU.mult))
            ternary()
            dve.wait_ge(small_in, 16 * 11)
            mask_rows()
            fw_low([0])
            ternary_columns()
            maximum("WQ0")
            scaling("WQ0")
            maximum("CTX")
            low("WQ0")
            fw_low([1, 2])
            scaling("CTX")
            fw_low([3])
            low("CTX")
            maximum("WQ1")
            fw_low([4])
            scaling("WQ1")
            fw_low([5])
            low("WQ1", 0)
            fw_low([6])
            low("WQ1", 1)
            fw_low([7])
            maximum("WK0")
            scaling("WK0")
            maximum("WO")
            low("WK0")
            scaling("WO")
            maximum("WV0")
            low("WO")
            m_evacuate([0, 1])
            scaling("WV0")
            m_evacuate([2])
            low("WV0")
            m_evacuate([3])
            dve.wait_ge(f_free, F2)
            maximum("M")
            scaling("M")
            maximum("WK1A")
            low("M")
            scaling("WK1A")
            f = k["factor"][:, F_WSC:F_WSC + 1]
            step(dve.tensor_scalar(f, f, 1.0 / 127.0, None, ALU.mult))
            dve.wait_ge(k_full, 1)
            dve.memset(vf[96:P, (RC - 1) * D:RC * D], 0.0)
            step(dve.memset(vf[96:P, (RC - 1) * D1:RC * D1], 0.0))
            low("WK1A")
            v_evacuate(S_WV0, vb0, 0, 0, D, range(3))
            maximum("WV1A")
            v_evacuate(S_WV0, vb0, 0, 0, D, range(3, RC))
            scaling("WV1A")
            dve.wait_ge(k_free, K0N)
            maximum("K0", [kf[:, ND:2 * ND, :].rearrange("p m r -> p (m r)")])
            low("WV1A")
            scaling("K0")
            dve.wait_ge(v_free, RC)
            maximum("V0", [vf[:, 0:RC * D]])
            low("K0")
            scaling("V0")
            maximum("WV1B")
            low("V0")
            dve.wait_ge(lo_done, split_count("V0"))
            v_evacuate(S_WV1A, vb1[:, 0:D], RC, 0, D1, range(2))
            scaling("WV1B")
            v_evacuate(S_WV1A, vb1[:, 0:D], RC, 0, D1, range(2, 4))
            low("WV1B")
            v_evacuate(S_WV1A, vb1[:, 0:D], RC, 0, D1, range(4, RC))
            maximum("WK1B")
            scaling("WK1B")
            dve.wait_ge(k_free, K0N + K1N // 2)
            part_maximum("K1", 0, kf[:, 0:ND, :].rearrange("p m r -> p (m r)"))
            low("WK1B")
            v_evacuate(S_WV1B, vb1[:, D:D1], 2 * RC, D, D1)
            dve.wait_ge(v_free, 3 * RC)
            maximum("V1", [vf])
            scaling("V1")
            low("V1")
            factor(F_PV0, S_V0, None, 1.0 / PS)
            factor(F_OUT, S_V1, S_WO, 1.0 / PS)
            dve.wait_ge(k_free, K0N + K1N - 2)
            part_maximum("K1", 1, kf[:, ND:ND1 - 1, :].rearrange("p m r -> p (m r)"))
            dve.wait_ge(k_free, K0N + K1N)
            part_maximum("K1", 2, kf[:, ND1 - 1, :])
            joined_maximum("K1", 3, 3)
            scaling("K1")
            low("K1")
            factor(F_E0, S_WQ0, S_K0, float(H0) ** -0.5)
            factor(F_E1, S_WQ1, S_K1, float(H1) ** -0.5)

        @block.scalar
        def _(act):
            def high(name, only=None):
                slot = SLOT[name]
                act.wait_ge(scale_ready, NTH[name] + 1)
                if name in PLACE_FREE:
                    act.wait_ge(*PLACE_FREE[name])
                if name == "K1":
                    act.wait_ge(kout, 16)
                if name == "V1":
                    act.wait_ge(vout, 16)
                for p, part in enumerate(pieces(name)):
                    if only is not None and p != only:
                        continue
                    for src, hi, lo in part:
                        ins = act.activation(hi, src, ACT.Copy, scale=k["scale"][:, slot:slot + 1])
                    ins.then_inc(hi_done, 1)

            def fw_high(js):
                for j in js:
                    act.wait_ge(f_full, j + 1)
                    act.activation(a_hl[:, j // ND, 0, j % ND, :], kbank[:, j % 4, :], ACT.Copy, scale=0.25).then_inc(f_hi, 1)

            def k_factor(slot, j):
                act.activation(kfac[:, j:j + 1], k["inv"][:, S_CTX:S_CTX + 1], ACT.Copy,
                               scale=k["inv"][:, slot:slot + 1]).then_inc(kfac_ready, 1)
                act.wait_ge(kfac_ready, j + 1)

            def k_evacuate(n0, m0, bias, j, halves):
                for h in halves:
                    m, half, n = h // 2, h % 2, n0 + h
                    act.wait_ge(k_full, n + 1)
                    act.activation(kf[:, m0 + m, half * ROWS // 2:(half + 1) * ROWS // 2], kbank[:, n % 4, 0:ROWS // 2],
                                   ACT.Identity, bias=bias[:, m:m + 1], scale=kfac[:, j:j + 1]).then_inc(k_free, 1)

            high("WF")
            fw_high([0])
            high("WQ0")
            fw_high([1, 2])
            high("CTX")
            fw_high([3, 4])
            high("WQ1", 0)
            fw_high([5])
            high("WQ1", 1)
            fw_high([6, 7])
            for name in ("WK0", "WO", "WV0"):
                high(name)
            act.wait_ge(small_in, 16 * 11)
            k_factor(S_WK0, 0)
            k_evacuate(0, ND, kb0[:, :], 0, range(0, 4))
            high("M")
            k_evacuate(0, ND, kb0[:, :], 0, range(4, 8))
            high("WK1A")
            k_factor(S_WK1A, 1)
            high("WV1A")
            k_evacuate(K0N, 0, kb1[:, 0:ND], 1, range(0, 4))
            high("K0")
            k_evacuate(K0N, 0, kb1[:, 0:ND], 1, range(4, 8))
            for name in ("V0", "WV1B", "WK1B"):
                high(name)
            k_factor(S_WK1B, 2)
            act.wait_ge(lo_done, split_count("K0"))
            k_evacuate(2 * K0N, ND, kb1[:, ND:ND1], 2, range(0, 4))
            high("V1")
            k_evacuate(2 * K0N, ND, kb1[:, ND:ND1], 2, range(4, 8))
            high("K1")

        @block.tensor
        def _(pe):
            def keys(name, n0):
                pe.wait_ge(lo_done, split_count(name))
                for m in range(ND):
                    for half in range(2):
                        n = n0 + 2 * m + half
                        if n >= 4:
                            pe.wait_ge(k_free, n - 3)
                        else:
                            pe.wait_ge(f_free, 2 * ND + n + 1)
                        for c in range(ND):
                            ins = products(pe, kbank[:, n % 4, 0:ROWS // 2],
                                           lambda h: w_hl[:, W_PLACE[name], h, c, m * P:(m + 1) * P],
                                           lambda h: ctx_hl[:, h, c, half * ROWS // 2:(half + 1) * ROWS // 2], c == 0, c == ND - 1)
                        ins.then_inc(k_full, 1)

            def values(name, n0):
                pe.wait_ge(lo_done, split_count(name))
                for r in range(RC):
                    rows, n = (P if r < RC - 1 else RL), n0 + r
                    if n >= 4:
                        pe.wait_ge(v_free, n - 3)
                    for c in range(ND):
                        ins = products(pe, vbank[0:rows, n % 4, :], lambda h: ctx_hl[:, h, c, r * P:r * P + rows],
                                       lambda h: w_hl[:, W_PLACE[name], h, c, :], c == 0, c == ND - 1)
                    ins.then_inc(v_full, 1)

            def ternary():
                pe.wait_ge(tern_rows, 1)
                for c in range(ND):
                    for s in range(4):
                        ins = pe.transpose(vbank[:, c, :].bitcast(BF16)[:, s * P:(s + 1) * P], ternrow[:, s, c * P:(c + 1) * P], k["identb"][:, :])
                    ins.then_inc(tern_full, 1)

            pe.wait_ge(dft_in, 16)
            COS, SIN, NSIN = range(3)
            for j in range(2 * ND):
                part, o = j // ND, j % ND
                if j >= 4:
                    pe.wait_ge(f_free, j - 3)
                terms = ((0, COS), (1, SIN)) if part == 0 else ((1, COS), (0, NSIN))
                for n, (w, f) in enumerate(terms):
                    if j == 0:
                        pe.wait_ge(lo_done, n + 1)
                    for c in range(ND):
                        ins = products(pe, kbank[:, j % 4, :], lambda h: w_hl[:, w, h, c, o * P:(o + 1) * P],
                                       lambda h: dft_hl[:, f, h, c, :], n == 0 and c == 0, n == 1 and c == ND - 1)
                ins.then_inc(f_full, 1)
                if j == 1:
                    ternary()
            for j in range(ND):
                pe.wait_ge(f_free, 2 * ND)
                for part, f in ((0, COS), (1, NSIN)):
                    for c in range(ND):
                        ins = products(pe, kbank[:, j % 4, :], lambda h: a_hl[:, part, h, c, j * P:(j + 1) * P],
                                       lambda h: dft_hl[:, f, h, c, :], part == 0 and c == 0, part == 1 and c == ND - 1)
                ins.then_inc(f_full, 1)
            keys("WK0", 0)
            pe.wait_ge(tern_done, ND)
            values("WV0", 0)
            keys("WK1A", K0N)
            values("WV1A", RC)
            values("WV1B", 2 * RC)
            keys("WK1B", 2 * K0N)


def layers(nc, k, x, scr_k0, scr_k1, scr_v0, scr_v1, out):
    here = ExitStack()
    with here:
        def sb(name, shape, dt):
            return here.enter_context(nc.sbuf_tensor(name, shape, dt))

        def sem(name):
            return here.enter_context(nc.semaphore(name))

        x1 = k["x1"]
        x2 = sb("x2", [P, NT, D], F32)
        x2b = sb("x2b", [P, NT, D], F32)
        x3 = sb("x3", [P, NT, D], F32)
        xn = sb("xn", [P, NT, D], F32)
        qi = sb("qi", [P, NT, D], BF16)
        xT = sb("xT", [P, 2, ND, S], F16)
        xT4 = sb("xT4", [P, 2, ND, S], F16)
        qiT = sb("qiT", [P, ND, S], BF16)
        q0T = sb("q0T", [P, 2, ND, S], F16)
        qc = sb("qc", [P, 2, ND1, S], F16)
        prT = sb("prT", [CH, 2, G, 3, S], F16)
        pr = [sb(f"pr{i}", [P, 2, GKP], F32) for i in range(4)]
        kd = sb("kd", [P, 2, ND1, KEYS], F16)
        k0d, k1d = kd[:, 0, :, :].rearrange("p (h m) n -> p h m n", h=2), kd[:, :, :, :]
        k0b = sb("k0b", [P, 2, ND, 4, KEYS], F16)
        k1b = sb("k1b", [P, 2, ND1, 2, KEYS], F16)
        v0b = sb("v0b", [CH, 3, 2, 2, G, H0], F16)
        v1b = sb("v1b", [CH, 2, G, 8, H1], F16)
        mrow = sb("mrow", [1, 4, KEYS], BF16)
        ones = sb("ones", [1, P], BF16)
        mx, sm = sb("mx", [P, 4, 8], F32), sb("sm", [P, 4, 8], F32)
        stats = sb("stats", [P, 4, NT, 6], F32)
        mean, half = sb("mean", [P, 4, NT], F32), sb("half", [P, 4, NT], F32)
        var, rstd = sb("var", [P, 4, NT], F32), sb("rstd", [P, 4, NT], F32)
        mhalf = sb("mhalf", [P, NT], F32)
        amax, ascale, cscale = sb("amax", [P, NT], F32), sb("ascale", [P, NT], F32), sb("cscale", [P, NT], F32)
        sc = here.enter_context(nc.psum_tensor("scores", [P, 2, 2, D], F32))
        ptb = here.enter_context(nc.psum_tensor("ptb", [P, 2, D], F32))
        wb = here.enter_context(nc.psum_tensor("wb", [P, 2, D], F32))

        dve_step, prep, prep1 = sem("dve_step"), sem("prep"), sem("prep1")
        x_loaded, k0_loaded, k1_loaded, v0_loaded, v1_loaded, stored = (sem(n) for n in (
            "x_loaded", "k0_loaded", "k1_loaded", "v0_loaded", "v1_loaded", "stored"))
        k0_ready, k1_ready = sem("k0_ready"), sem("k1_ready")
        bank_full, bank_hi, bank_free = sem("bank_full"), sem("bank_hi"), sem("bank_free")
        scores_full, shifted, exp_done, sums_ready, probs_ready = (sem(n) for n in (
            "scores_full", "shifted", "exp_done", "sums_ready", "probs_ready"))
        prT_full, prT_hi, prT_free = sem("prT_full"), sem("prT_hi"), sem("prT_free")
        ln_var = [sem(f"ln_var{i}") for i in range(4)]
        ln_rstd = [sem(f"ln_rstd{i}") for i in range(4)]
        ln_done = [sem(f"ln_done{i}") for i in range(4)]
        x1_biased, x2_biased, x3_biased = sem("x1_biased"), sem("x2_biased"), sem("x3_biased")

        x_v = x.rearrange("b (p t) d -> b p t d", t=NT)
        out_v = out.rearrange("b (p t) d -> b p t d", t=NT)
        PIECES = []
        for hh in range(4):
            r = hh * KEYS
            while r < (hh + 1) * KEYS:
                c = r // CH
                n = min((c + 1) * CH, (hh + 1) * KEYS) - r
                PIECES.append((hh, c, r - c * CH, r - hh * KEYS, n))
                r += n
        V1SLOT = {(0, 0): 0, (1, 0): 1, (1, 1): 3, (2, 1): 4, (2, 2): 6, (3, 2): 7}

        def unit_place(stage, u):
            return (u // 2, u % 2) if stage == "X" else (u % NT, u // NT)

        def parts(j, b, tiles):
            return (2 * b + (2 if tiles.stop == NT else 1)) if j == 1 else b + 1

        PREP = 5
        block = here.enter_context(nc.Block())

        @block.sync
        def _(sp):
            def load_k(layer, b):
                scr_k, kl, width = (scr_k0, k0_loaded, 2 * ND * KEYS) if layer == 0 else (scr_k1, k1_loaded, 2 * ND1 * KEYS)
                sp.dma_start(kd[:, :, :, :].rearrange("p h m n -> p (h m n)")[:, 0:width], scr_k[:, b, :]).then_inc(kl, 16)

            def load_v(layer, b):
                for hh, c, r0, k0, n in PIECES:
                    if layer == 0:
                        src = scr_v0[bass.ds(b * KEYS + k0, n), hh, :]
                        sp.dma_start(v0b[r0:r0 + n, c, hh - c, :, :, :].rearrange("p h g d -> p (h g d)"), src).then_inc(v0_loaded, 16)
                    else:
                        src = scr_v1[bass.ds(b * KEYS + k0, n), hh, :]
                        sp.dma_start(v1b[r0:r0 + n, :, :, V1SLOT[hh, c], :].rearrange("p h g d -> p (h g) d"),
                                     src.rearrange("p (q d) -> p q d", d=H1)).then_inc(v1_loaded, 16)

            load_k(0, 0)
            sp.wait_ge(prep, PREP)

            def body(it, loop):
                i = it.i
                if "Y" in it.present:
                    sp.wait_ge(k0_ready, it.done["X"] + 1 if "X" in it.present else B)
                    load_k(1, it.done["Y"])
                    if not (isinstance(i, int) and i == 1):
                        sp.wait_ge(bank_full, it.bank(*it.order[0])[1])
                    if isinstance(i, int) and i == 1:
                        sp.wait_ge(prep1, 2)
                    load_v(1, it.done["Y"])
                if it.present == "W":
                    load_v(0, 0)
                elif "W" in it.present:
                    if "Y" in it.present:
                        sp.wait_ge(k1_ready, it.done["Y"] + 1)
                    else:
                        sp.wait_ge(k0_ready, it.done["X"] + 1)
                    load_k(0, it.done["W"])
                    sp.wait_ge(bank_full, it.bank("X", "pv", NT - 1)[1] + 1)
                    load_v(0, it.done["W"])
                    sp.wait_ge(bank_free, it.bank("X", "f", NT - 1)[1] + 1)
                    sp.dma_start(x1[:, :, :], x_v[it.done["W"]]).then_inc(x_loaded, 16)
                if "Z" in it.present:
                    sp.wait_ge(bank_free, it.bank("Z", "f", NT - 1)[1] + 1)
                    sp.dma_start(out_v[it.done["Z"]], x3[:, :, :]).then_inc(stored, 16)

            walk(sp, body)
            sp.wait_ge(stored, 16 * B)

        @block.gpsimd
        def _(pool):
            pool.memset(v0b[:, :, :, :, :, :], 0.0).then_inc(prep, 1)
            pool.memset(k0b[:, :, :, :, :], 0.0).then_inc(prep, 1)
            pool.memset(ones[:, :], 1.0).then_inc(prep, 1)
            pool.memset(mhalf[:, :], -0.5).then_inc(prep, 1)
            for n in range(4):
                last = pool.memset(pr[n][:, :, GK:GKP], 0.0)
            last.then_inc(prep, 1)
            pool.wait_ge(prep, PREP)

            def rstd_of(j, b, tiles=slice(0, NT)):
                pool.wait_ge(ln_var[j], parts(j, b, tiles))
                pool.tensor_tensor(rstd[:, j, tiles], var[:, j, tiles], mhalf[:, tiles], ALU.pow).then_inc(ln_rstd[j], 1)

            def normalise(U, n):
                p = pr[n % 4]
                pool.wait_ge(sums_ready, U + 1)
                v = p[:, :, 0:GK].rearrange("p g (h n) -> p g h n", h=4)
                s = sm[:, n % 4, :].rearrange("p (g h u) -> p g h u", g=2, u=1).broadcast_to([P, 2, 4, KEYS])
                pool.tensor_tensor(v, v, s, ALU.mult).then_inc(probs_ready, 1)

            def add_bias(o, a, bias, ready, normed, b, t):
                if normed is not None:
                    pool.wait_ge(normed, NT * b + t + 1)
                pool.tensor_tensor(o[:, t, :], a[:, t, :], bias[:, :], ALU.add).then_inc(ready, 1)

            def body(it, loop):
                X, Y, Z, Wb = (it.done[s] for s in "XYZW")
                pres = it.present
                if "X" in pres:
                    for u in range(8):
                        if u == 7:
                            rstd_of(1, X, slice(0, 2))
                        normalise(it.unit("X", u), u)
                if "Z" in pres:
                    rstd_of(3, Z)
                for t in range(NT):
                    if t == 2 and "X" in pres:
                        for tile in (0, 1):
                            add_bias(x1, x1, k["bf0"], x1_biased, ln_done[1], X, tile)
                        rstd_of(1, X, slice(2, NT))
                    if "Y" in pres:
                        if t == 0 and "Z" in pres:
                            pool.wait_ge(bank_free, it.bank("Z", "out", NT - 1)[1] + 1)
                        add_bias(x2b, x2, k["bo"], x2_biased, None, Y, t)
                for u in range(8):
                    if "X" in pres and u == 4:
                        rstd_of(2, X)
                    if u == 6 and "W" in pres:
                        rstd_of(0, Wb)
                    if "Y" in pres:
                        normalise(it.unit("Y", u), u)
                    if "X" in pres and u == 0:
                        for tile in (2, 3):
                            add_bias(x1, x1, k["bf0"], x1_biased, ln_done[1], X, tile)
                    if "Z" in pres and 1 <= u <= NT:
                        add_bias(x3, x3, k["bf1"], x3_biased, ln_done[3], Z, u - 1)
                if pres == "W":
                    pool.memset(v1b[:, :, :, :, :], 0.0).then_inc(prep1, 1)
                    pool.memset(k1b[:, :, :, :, :], 0.0).then_inc(prep1, 1)

            walk(pool, body)

        @block.scalar
        def _(act):
            act.wait_ge(prep, PREP)

            def hi_part(it, use, o, **kw):
                bank, n = it.bank(*use)
                act.wait_ge(bank_full, n + 1)
                src = wb[:, bank, :]
                if len(o.shape) == 3:
                    src = src.rearrange("p (c n) -> p c n", c=ND)
                act.activation(o, src, **kw).then_inc(bank_hi, 1)

            def transposed(it, stage, t, o):
                hi_part(it, (stage, "t", t), o[:, 0, :, t * P:(t + 1) * P], func=ACT.Copy)

            def exp(it, stage, u):
                U = it.unit(stage, u)
                act.wait_ge(shifted, U + 1)
                f = F_E0 if stage == "X" else F_E1
                act.activation(pr[u % 4][:, :, 0:GK], pr[u % 4][:, :, 0:GK], ACT.Exp,
                               scale=k["factor"][:, f:f + 1]).then_inc(exp_done, 1)

            def prT_high(it, stage, u):
                U, (t, h) = it.unit(stage, u), unit_place(stage, u)
                act.wait_ge(prT_full, U + 1)
                o = prT[:, 0, 2 * h:2 * h + 2, :, t * P:(t + 1) * P]
                act.activation(o, ptb[0:CH, :, 0:3 * P].rearrange("p g (c n) -> p g c n", c=3), ACT.Copy,
                               scale=PS).then_inc(prT_hi, 1)

            def diagonal(layer, it, b):
                kd, kb, n, w = (k0d, k0b, 4, H0) if layer == 0 else (k1d, k1b, 2, H1)
                if layer == 1 and isinstance(b, int) and b == 0:
                    act.wait_ge(prep1, 2)
                act.wait_ge(k0_loaded if layer == 0 else k1_loaded, (b + 1) * 16)
                for j in range(n):
                    last = act.activation(kb[j * w:(j + 1) * w, :, :, j, :], kd[j * w:(j + 1) * w, :, :, :], ACT.Copy)
                if layer == 0:
                    act.activation(mrow[:, :, :], k["maskall"][:, bass.ds(b, 1), :].broadcast_to([1, 4, KEYS]), ACT.Copy).then_inc(k0_ready, 1)
                else:
                    last.then_inc(k1_ready, 1)

            def body(it, loop):
                X, Y, Z, Wb = (it.done[s] for s in "XYZW")
                pres = it.present

                def high(use):
                    stage, what, n = use
                    if what == "t" and stage != "X":
                        transposed(it, stage, n, xT4 if stage == "Z" else xT)
                    elif what == "q":
                        q, bias = (qc, k["bq1"]) if stage == "Y" else (q0T, k["bq0"])
                        hi_part(it, use, q[:, 0, n, :], func=ACT.Identity, bias=bias[:, n:n + 1])
                    elif use[:2] == ("Y", "pv"):
                        hi_part(it, use, qc[:, 0, n, :], func=ACT.Copy)

                def softmax(stage, listed, s):
                    if stage in pres and s >= 3:
                        prT_high(it, stage, s - 3)
                    if stage in pres and s < 8:
                        exp(it, stage, s)
                    for use in it.uses(listed[s]):
                        high(use)

                for s in range(11):
                    softmax("X", A_USES, s)
                    if s == 3 and "Y" in pres:
                        diagonal(1, it, Y)
                for use in it.uses(M_USES):
                    high(use)
                for s in range(11):
                    softmax("Y", B_USES, s)
                    if s == 5 and "W" in pres:
                        diagonal(0, it, Wb)
                for use in it.uses(C_USES):
                    high(use)

            walk(act, body)

        @block.vector
        def _(dve):
            step = Chain(dve, dve_step)
            def ln_stats(j, src, tiles):
                for t in tiles:
                    last = dve.bn_stats(stats[:, j, t, :], src[:, t, :])
                if tiles[-1] == NT - 1 or (j == 1 and tiles[-1] == 1):
                    step(last)
                    ts = slice(0, NT) if j != 1 else slice(tiles[-1] - 1, tiles[-1] + 1)
                    m, v, h = mean[:, j, ts], var[:, j, ts], half[:, j, ts]
                    e, o = stats[:, j, ts, 1], stats[:, j, ts, 4]
                    dve.tensor_tensor(m, e, o, ALU.add)
                    dve.tensor_tensor(h, e, o, ALU.subtract)
                    step(dve.tensor_tensor(v, stats[:, j, ts, 2], stats[:, j, ts, 5], ALU.add))
                    dve.tensor_scalar(m, m, 0.5, None, ALU.mult)
                    dve.tensor_scalar(v, v, 1.0 / D, EPS, ALU.mult, ALU.add)
                    step(dve.scalar_tensor_tensor(out=h, in0=h, scalar=0.25, in1=h, op0=ALU.mult, op1=ALU.mult))
                    dve.tensor_tensor(v, v, h, ALU.add).then_inc(ln_var[j], 1)

            def ln_apply(j, src, tiles, b, signal=True):
                if tiles[0] == 0 or (j == 1 and tiles[0] == 2):
                    dve.wait_ge(ln_rstd[j], parts(j, b, slice(0, tiles[-1] + 1)))
                for t in tiles:
                    ins = dve.tensor_scalar(xn[:, t, :], src[:, t, :], mean[:, j, t:t + 1], rstd[:, j, t:t + 1],
                                            ALU.subtract, ALU.mult)
                    if signal:
                        ins.then_inc(ln_done[j], 1)
                return ins

            def quantise_a(t, b):
                pair = slice(t, t + 2)
                step(ln_apply(1, x1, [t, t + 1], b, signal=False))
                step(dve.tensor_reduce(amax[:, pair], xn[:, pair, :], AX.X, ALU.max, apply_absolute_value=True))

            def quantise_b(t):
                pair = slice(t, t + 2)
                step(dve.tensor_scalar(amax[:, pair], amax[:, pair], 1e-5, None, ALU.max))
                dve.tensor_scalar(cscale[:, pair], amax[:, pair], k["factor"][:, F_WSC:F_WSC + 1], None, ALU.mult)
                step(dve.reciprocal(ascale[:, pair], amax[:, pair]))
                step(dve.tensor_scalar(ascale[:, pair], ascale[:, pair], 127.0, None, ALU.mult))
                for j in (t, t + 1):
                    ins = dve.tensor_scalar(xn[:, j, :], xn[:, j, :], ascale[:, j:j + 1], MAGIC, ALU.mult, ALU.add)
                step(ins)
                dve.tensor_scalar(qi[:, pair, :], xn[:, pair, :], MAGIC, 127.0, ALU.subtract, ALU.min).then_inc(ln_done[1], 2)

            def lo_part(it, use, lo, hi, bias=0.0):
                bank, n = it.bank(*use)
                dve.wait_ge(bank_hi, it.hi(*use) + 1)
                src = wb[:, bank, :]
                if len(lo.shape) == 3:
                    src = src.rearrange("p (c n) -> p c n", c=ND)
                if isinstance(bias, float):
                    ins = dve.tensor_tensor(lo, src, hi, ALU.subtract)
                else:
                    ins = dve.scalar_tensor_tensor(out=lo, in0=src, scalar=bias, in1=hi, op0=ALU.add, op1=ALU.subtract)
                ins.then_inc(bank_free, 1)

            def add_to(it, use, o, factor, a):
                bank, n = it.bank(*use)
                dve.wait_ge(bank_full, n + 1)
                dve.scalar_tensor_tensor(out=o, in0=wb[:, bank, :], scalar=factor, in1=a,
                                         op0=ALU.mult, op1=ALU.add).then_inc(bank_free, 1)

            def transposed(it, stage, t, o):
                c = slice(t * P, (t + 1) * P)
                lo_part(it, (stage, "t", t), o[:, 1, :, c], o[:, 0, :, c])

            def four(ap):
                return ap.rearrange("p g (h n) -> p g h n", h=4)

            def maxima(it, stage, u):
                U = it.unit(stage, u)
                dve.wait_ge(scores_full, U + 1)
                s = four(sc[:, u % 2, :, 0:GK])
                m = mx[:, u % 4, :].rearrange("p (g h) -> p g h", g=2)
                step(dve.tensor_reduce(m, s, AX.X, ALU.max))
                m = mx[:, u % 4, :].rearrange("p (g h u) -> p g h u", g=2, u=1).broadcast_to([P, 2, 4, KEYS])
                dve.tensor_tensor(four(pr[u % 4][:, :, 0:GK]), s, m, ALU.subtract).then_inc(shifted, 1)

            def sums(it, stage, u):
                U = it.unit(stage, u)
                dve.wait_ge(exp_done, U + 1)
                step(dve.tensor_reduce(sm[:, u % 4, :].rearrange("p (g h) -> p g h", g=2), four(pr[u % 4][:, :, 0:GK]), AX.X, ALU.add))
                dve.reciprocal(sm[:, u % 4, :], sm[:, u % 4, :]).then_inc(sums_ready, 1)

            def prT_low(it, stage, u):
                U, (t, h) = it.unit(stage, u), unit_place(stage, u)
                dve.wait_ge(prT_hi, U + 1)
                pair = [prT[:, j, 2 * h:2 * h + 2, :, t * P:(t + 1) * P].rearrange("p g c n -> p (g c) n") for j in range(2)]
                for g in range(2):
                    ins = dve.scalar_tensor_tensor(out=pair[1][:, 3 * g:3 * g + 3], in0=ptb[0:CH, g, 0:3 * P].rearrange("p (c n) -> p c n", c=3),
                                                   scalar=PS, in1=pair[0][:, 3 * g:3 * g + 3], op0=ALU.mult, op1=ALU.subtract)
                ins.then_inc(prT_free, 1)

            f = k["factor"]

            def values0_done(it, t):
                add_to(it, ("X", "pv", t), x1[:, t, :], f[:, F_PV0:F_PV0 + 1], x1[:, t, :])
                dve.wait_ge(bank_free, it.bank("X", "pv", t)[1] + 1)
                ln_stats(1, x1, [t])

            def body(it, loop):
                X, Y, Z, Wb = (it.done[s] for s in "XYZW")
                pres = it.present
                if loop:
                    start = step.count.base + step.count.local
                    step.count.base, step.count.local = start + (it.i - loop[0]) * STEPS_PER_ITERATION, 0

                def low(use):
                    stage, what, n = use
                    if use[:2] == ("X", "t"):
                        bank, before = it.bank(*use)
                        dve.wait_ge(bank_full, before + 1)
                        dve.tensor_copy(qiT[:, :, n * P:(n + 1) * P], wb[:, bank, :].bitcast(BF16)[:, 0:D].rearrange(
                            "p (c n) -> p c n", c=ND)).then_inc(bank_free, 1)
                    elif what == "t":
                        transposed(it, stage, n, xT4 if stage == "Z" else xT)
                    elif what == "q":
                        q, bias = (qc, k["bq1"]) if stage == "Y" else (q0T, k["bq0"])
                        lo_part(it, use, q[:, 1, n, :], q[:, 0, n, :], bias[:, n:n + 1])
                    elif use[:2] == ("X", "pv"):
                        values0_done(it, n)
                    elif use[:2] == ("Y", "pv"):
                        lo_part(it, use, qc[:, 1, n, :], qc[:, 0, n, :])
                    elif what == "out":
                        if n == 0 and not (isinstance(Z, int) and Z == 0):
                            dve.wait_ge(stored, 16 * Z)
                        dve.wait_ge(x2_biased, NT * Z + n + 1)
                        add_to(it, use, x3[:, n, :], f[:, F_OUT:F_OUT + 1], x2b[:, n, :])
                    elif use[:2] == ("X", "f"):
                        dve.wait_ge(x1_biased, NT * X + n + 1)
                        if "Y" in pres:
                            dve.wait_ge(x2_biased, NT * Y + n + 1)
                        add_to(it, use, x2[:, n, :], cscale[:, n:n + 1], x1[:, n, :])
                    else:
                        dve.wait_ge(x3_biased, NT * Z + n + 1)
                        add_to(it, use, x3[:, n, :], k["inv"][:, S_M:S_M + 1], x3[:, n, :])

                def softmax(stage, s):
                    if stage in pres:
                        if s < 8:
                            maxima(it, stage, s)
                        if 1 <= s < 9:
                            sums(it, stage, s - 1)
                        if s >= 3:
                            prT_low(it, stage, s - 3)

                for s in range(11):
                    softmax("X", s)
                    if "Z" in pres and s in (3, 5, 7, 8):
                        t = (s - 2) // 2
                        dve.wait_ge(bank_free, it.bank("Z", "out", t)[1] + 1)
                        ln_stats(3, x3, [t])
                    for use in it.uses(A_USES[s]):
                        low(use)
                    if "X" in pres and s == 9:
                        quantise_a(0, X)
                    if "X" in pres and s == 10:
                        quantise_b(0)
                for n, use in enumerate(M_USES):
                    if use[0] in pres:
                        low(use)
                    if "X" in pres and n == 2:
                        quantise_a(2, X)
                    if "X" in pres and n == 3:
                        quantise_b(2)
                for s in range(11):
                    softmax("Y", s)
                    if "W" in pres and s == 7:
                        if "X" in pres:
                            dve.wait_ge(ln_done[1], NT * (X + 1))
                        ln_apply(0, x1, list(range(NT)), Wb)
                    for use in it.uses(B_USES[s]):
                        low(use)
                    if "Z" in pres and s in (0, 1):
                        if "X" in pres:
                            dve.wait_ge(ln_done[1], NT * (X + 1))
                        ln_apply(3, x3, [2 * s, 2 * s + 1], Z)
                    if "X" in pres and s in (3, 4):
                        dve.wait_ge(bank_free, it.bank("X", "f", 2 * s - 5)[1] + 1)
                        ln_stats(2, x2, [2 * s - 6, 2 * s - 5])
                    if "W" in pres:
                        if s == 4:
                            if not (isinstance(Wb, int) and Wb == 0):
                                dve.wait_ge(x_loaded, 16 * Wb)
                        if s in (4, 5):
                            ln_stats(0, x1, [2 * s - 8, 2 * s - 7])
                for n, use in enumerate(C_USES):
                    if use[0] in pres:
                        low(use)
                    if "X" in pres and n < NT:
                        ln_apply(2, x2, [n], X)
                if loop:
                    assert step.count.local == STEPS_PER_ITERATION, step.count.local
                    step.count.base, step.count.local = start + (loop[1] - loop[0]) * STEPS_PER_ITERATION, 0

            walk(dve, body)

        @block.tensor
        def _(pe):
            pe.wait_ge(prep, PREP)
            ident, identb = k["ident"], k["identb"]

            def take(it, *use):
                bank, n = it.bank(*use)
                if not (isinstance(n, int) and n < 2):
                    pe.wait_ge(bank_free, n - 1)
                return bank

            def transpose_tile(it, stage, t):
                j = "WXYZ".index(stage)
                bank = take(it, stage, "t", t)
                pe.wait_ge(ln_done[j], NT * it.done[stage] + t + 1)
                for c in range(ND):
                    if stage == "X":
                        ins = pe.transpose(wb[:, bank, :].bitcast(BF16)[:, c * P:(c + 1) * P], qi[:, t, c * P:(c + 1) * P], identb[:, :])
                    else:
                        ins = pe.transpose(wb[:, bank, c * P:(c + 1) * P], xn[:, t, c * P:(c + 1) * P], ident[:, :])
                ins.then_inc(bank_full, 1)

            def project(it, stage, m, w, src):
                bank = take(it, stage, "q", m)
                if m == 0:
                    pe.wait_ge(bank_free, it.bank(stage, "t", NT - 1)[1] + 1)
                for c in range(ND):
                    ins = products(pe, wb[:, bank, :], lambda h: w[:, h, c, m * P:(m + 1) * P], lambda h: src[:, h, c, :],
                                   c == 0, c == ND - 1)
                ins.then_inc(bank_full, 1)

            def scores(it, stage, u):
                U, (t, half) = it.unit(stage, u), unit_place(stage, u)
                if not (isinstance(U, int) and U < 2):
                    pe.wait_ge(shifted, U - 1)
                tok = slice(t * P, (t + 1) * P)
                for gg in range(2):
                    g = 2 * half + gg
                    if stage == "X":
                        o = sc[:, u % 2, gg, 0:GK]
                        pe.matmul(o, ones[:, :], mrow[:, :, :].rearrange("o h n -> o (h n)"), start=True, stop=False)
                        ins = products(pe, o, lambda h: q0T[:, h, g, tok],
                                       lambda h: k0b[:, h, g, :, :].rearrange("p j n -> p (j n)"), False, True)
                    else:
                        for e in range(2):
                            pair = 2 * g + e
                            ins = products(pe, sc[:, u % 2, gg, e * 2 * KEYS:(e + 1) * 2 * KEYS], lambda h: qc[:, h, pair, tok],
                                           lambda h: k1b[:, h, pair, :, :].rearrange("p j n -> p (j n)"), e == 0, True, skip=True)
                ins.then_inc(scores_full, 1)

            def probs_transpose(it, stage, u):
                U = it.unit(stage, u)
                pe.wait_ge(probs_ready, U + 1)
                if not (isinstance(U, int) and U < 1):
                    pe.wait_ge(prT_free, U)
                for gg in range(2):
                    for c in range(3):
                        ins = pe.transpose(ptb[0:CH, gg, c * P:(c + 1) * P], pr[u % 4][:, gg, c * CH:(c + 1) * CH], ident[:, :])
                ins.then_inc(prT_full, 1)

            def values0(it, t):
                bank = take(it, "X", "pv", t)
                pe.wait_ge(prT_free, it.unit("X", 2 * t + 1) + 1)
                first = True
                for g in range(G):
                    for c in range(3):
                        o = wb[:, bank, g * P + c * H0:g * P + (c + 2) * H0]
                        ins = products(pe, o, lambda h: prT[:, h, g, c, t * P:(t + 1) * P], lambda h: v0b[:, c, :, h, g, :],
                                       first, g == G - 1 and c == 2, skip=True)
                        first = False
                ins.then_inc(bank_full, 1)

            def values1(it, pair):
                bank = take(it, "Y", "pv", pair)
                if pair % 4 == 0:
                    pe.wait_ge(prT_free, it.unit("Y", pair + 3) + 1)
                g, e = pair // 2, pair % 2
                for n, (c, slot) in enumerate(((0, 0), (1, 2)) if e == 0 else ((1, 4), (2, 6))):
                    ins = products(pe, wb[:, bank, :], lambda h: v1b[:, h, g, slot:slot + 2, :].rearrange("p s d -> p (s d)"),
                                   lambda h: prT[:, h, g, c, :], n == 0, n == 1)
                ins.then_inc(bank_full, 1)

            def output(it, t):
                bank = take(it, "Z", "out", t)
                if t == 0:
                    pe.wait_ge(bank_free, it.bank(*it.order[0])[1])
                for j in range(ND1):
                    ins = products(pe, wb[:, bank, :], lambda h: qc[:, h, j, t * P:(t + 1) * P], lambda h: k["wo"][:, h, j, :],
                                   j == 0, j == ND1 - 1)
                ins.then_inc(bank_full, 1)

            def ffn0(it, t):
                bank = take(it, "X", "f", t)
                pe.wait_ge(bank_free, it.bank("X", "t", t)[1] + 1)
                for c in range(ND):
                    ins = pe.matmul(wb[:, bank, :], qiT[:, c, t * P:(t + 1) * P], k["tern"][:, c, :], start=c == 0, stop=c == ND - 1)
                ins.then_inc(bank_full, 1)

            def ffn1(it, t):
                bank = take(it, "Z", "f", t)
                pe.wait_ge(bank_free, it.bank("Z", "t", t)[1] + 1)
                for c in range(ND):
                    ins = products(pe, wb[:, bank, :], lambda h: xT4[:, h, c, t * P:(t + 1) * P], lambda h: k["m"][:, h, c, :],
                                   c == 0, c == ND - 1)
                ins.then_inc(bank_full, 1)

            def body(it, loop):
                X, Y, Z, Wb = (it.done[s] for s in "XYZW")
                pres = it.present

                def fill(use):
                    stage, what, n = use
                    if what == "t":
                        transpose_tile(it, stage, n)
                    elif what == "q":
                        project(it, stage, n, *((k["wq1"], xT) if stage == "Y" else (k["wq0"], xT)))
                    elif what == "out":
                        output(it, n)
                    elif what == "pv":
                        (values0 if stage == "X" else values1)(it, n)
                    else:
                        (ffn0 if stage == "X" else ffn1)(it, n)

                def softmax(stage, listed, s):
                    if stage in pres:
                        if s + 1 < 8:
                            if stage == "Y" and s + 1 == NT:
                                pe.wait_ge(bank_free, it.bank("Y", "q", ND1 - 1)[1] + 1)
                            scores(it, stage, s + 1)
                        if s >= 3:
                            probs_transpose(it, stage, s - 3)
                    for use in it.uses(listed[s]):
                        fill(use)

                if "X" in pres:
                    pe.wait_ge(k0_ready, X + 1)
                    later = 0 if isinstance(it.i, int) and it.i < 2 else AFTER_W
                    pe.wait_ge(bank_free, it.bank(*it.order[0])[1] - later)
                    scores(it, "X", 0)
                for s in range(11):
                    if s == 4 and "X" in pres:
                        pe.wait_ge(v0_loaded, 16 * len(PIECES) * (X + 1))
                    softmax("X", A_USES, s)
                for use in it.uses(M_USES):
                    fill(use)
                if "Y" in pres:
                    pe.wait_ge(k1_ready, Y + 1)
                    pe.wait_ge(bank_free, it.bank("Y", "q", 3)[1] + 1)
                    scores(it, "Y", 0)
                for s in range(11):
                    if s == 6 and "Y" in pres:
                        pe.wait_ge(v1_loaded, 16 * len(PIECES) * (Y + 1))
                    softmax("Y", B_USES, s)
                for use in it.uses(C_USES):
                    fill(use)

            walk(pe, body)


STEPS_PER_ITERATION = 5 * 3 + 4 * 8 + NT // 2 * 6



def constants():
    n = np.arange(D)
    a = 2.0 * np.pi * ((n[:, None] * n[None, :]) % D) / D
    c, s = np.cos(a), np.sin(a)
    parts = []
    for m in (c, s, -s):
        hi = m.astype(np.float16)
        lo = (m - hi.astype(np.float64)).astype(np.float16)
        for v in (hi, lo):
            parts.append(v.reshape(ND, P, D).transpose(1, 0, 2).reshape(P, ND * D))
    return np.ascontiguousarray(np.concatenate(parts, axis=1)), np.eye(P, dtype=np.float32)


def kernel(**inputs):
    import concourse.bacc as _bacc
    from concourse.bass_utils import run_bass_kernel_spmd as _run

    a = {n: np.asarray(v) for n, v in inputs.items()}

    def blocks(w):
        return w.reshape(-1, P, w.shape[1]).transpose(1, 0, 2)

    def flat(w):
        v = blocks(w)
        return v.reshape(P, -1)

    def by_slot(w, d):
        return w.reshape(w.shape[:-1] + (G, 4, d)).swapaxes(-3, -2).reshape(w.shape)

    dft, eye = constants()
    data = {
        "x": a["x"],
        "ctxT": blocks(a["ctx_1024"].reshape(ROWS, D).T),
        "mask": a["mask_BxS2_ik0"].reshape(1, ROWS),
        "wq0": flat(a["L0_xattn_q_w"].T),
        "bq0": a["L0_xattn_q_b"].reshape(ND, P).T,
        "wk0": blocks(a["L0_xattn_k_w"].T),
        "bk0": a["L0_xattn_k_b"].reshape(ND, P).T,
        "wv0": blocks(by_slot(a["L0_xattn_v_w"].T, H0)),
        "bv0": by_slot(a["L0_xattn_v_b"], H0),
        "packed": a["L0_ffn_packed_weight"].reshape(P, D),
        "wscale": a["L0_ffn_weight_scale"],
        "bf0": a["L0_ffn_bias"],
        "wq1": flat(a["L1_xattn_Wq"].reshape(D, D1)),
        "bq1": a["L1_xattn_bq"].reshape(ND1, P).T,
        "wk1": blocks(a["L1_xattn_Wk"].reshape(D, D1)),
        "bk1": a["L1_xattn_bk"].reshape(ND1, P).T,
        "wv1": blocks(by_slot(a["L1_xattn_Wv"].reshape(D, D1), H1)),
        "bv1": by_slot(a["L1_xattn_bv"].reshape(D1), H1),
        "wo": flat(a["L1_xattn_Wo"].reshape(D1, D)),
        "bo": a["L1_xattn_bo"],
        "wf": np.concatenate([flat(a["L1_ffn_w_freq_real"]), flat(a["L1_ffn_w_freq_imag"])], axis=1),
        "bf1": a["L1_ffn_bias"],
        "dft": dft,
        "eye": eye,
    }
    nc = _bacc.Bacc("TRN2", target_bir_lowering=False, num_devices=1)
    arrays, args = {}, []
    for name, v in data.items():
        v = np.ascontiguousarray(v)
        arrays[f"in_{name}"] = v
        args.append(nc.dram_tensor(f"in_{name}", v.shape, mybir.dt.from_np(v.dtype), kind="ExternalInput").ap())
    out = nc.dram_tensor("out_x", (B, S, D), F32, kind="ExternalOutput").ap()
    program(nc, *args, out)
    r = _run(nc, [arrays], core_ids=[0])
    return r.results[0]["out_x"]
```
